# Optimizing a Trainium2 kernel written in Bass

```python
import numpy as np
import jax
import jax.numpy as jnp

def _softmax(x, axis=-1):
    return jax.nn.softmax(x, axis=axis)

def _gelu(x):
    return jax.nn.gelu(x, approximate=True)

def _silu(x):
    return jax.nn.silu(x)

def _sigmoid(x):
    return jax.nn.sigmoid(x)

def _layernorm(x, axis=-1, eps=1e-05):
    m = jnp.mean(x, axis=axis, keepdims=True)
    v = jnp.var(x, axis=axis, keepdims=True)
    return (x - m) / jnp.sqrt(v + eps)

def _scatter_add(tgt, idx, src, axis=0):
    return tgt.at[idx].add(src)

def _segment_sum(src, seg, n):
    return jax.ops.segment_sum(src, seg, n)
kernel_name = 'mk_gnn_preln_d4_gnn_r8_a3e9ac'

def setup_inputs(seed: int=0):
    np.random.seed(seed)
    _w = jnp.asarray

    def _rec_inputs():
        import jax
        import jax.numpy as jnp
        _gk = jax.random.key(seed)
        x = -0.000202 + 1 * jax.random.normal(jax.random.fold_in(_gk, 1), (12500, 64), jnp.float32)
        _s = jax.random.randint(jax.random.fold_in(_gk, 2), (100000,), 0, 12500, jnp.int32)
        _d = jax.random.randint(jax.random.fold_in(_gk, 3), (100000,), 0, 12500, jnp.int32)
        _loop = jnp.arange(12500, dtype=jnp.int32)
        src = jnp.concatenate([_s, _d, _loop])
        dst = jnp.concatenate([_d, _s, _loop])
        _o = jnp.argsort(dst, stable=True)
        src = src[_o]
        dst = dst[_o]
        edge_type_4 = jax.random.randint(jax.random.fold_in(_gk, 13), (212500,), 0, 4, jnp.int32)
        return (x, src, dst, edge_type_4)
    x, src, dst, edge_type_4 = _rec_inputs()

    def _L0_gnn_setup():
        import jax, jax.numpy as jnp
        import numpy as np
        N = 12500
        E = 200000
        D = 64
        EPS = 1e-12
        key = jax.random.key(seed)
        k1, k2, k3 = jax.random.split(key, 3)
        H = jax.random.normal(k1, (N, D), dtype=jnp.float32)
        row = jnp.sort(jax.random.randint(k2, (E,), 0, N, dtype=jnp.int64))
        col = jax.random.randint(k3, (E,), 0, N, dtype=jnp.int64)
        return {'H': H, 'row': row, 'col': col, 'num_nodes': N}
    _L0_gnn_all = _L0_gnn_setup()
    _L0_gnn_in = {k: v for k, v in _L0_gnn_all.items() if k in ()}
    del _L0_gnn_all

    def _L1_gnn_setup():
        import jax, jax.numpy as jnp
        import numpy as np
        N, E = (6250, 156250)
        IN_DIM, OUT_DIM, HEADS = (64, 64, 4)
        NEG_SLOPE = 0.2
        LN_EPS = 1e-05
        SM_EPS = 1e-16

        def _gat_conv(x, src, dst, W, a_src, a_dst, b, heads, out_c, concat):
            n = x.shape[0]
            xw = (x @ W).reshape(n, heads, out_c)
            asrc = jnp.einsum('nhc,hc->nh', xw, a_src)
            adst = jnp.einsum('nhc,hc->nh', xw, a_dst)
            loop = jnp.arange(n, dtype=src.dtype)
            s = jnp.concatenate([src, loop])
            d = jnp.concatenate([dst, loop])
            e = jax.nn.leaky_relu(asrc[s] + adst[d], NEG_SLOPE)
            m = jax.ops.segment_max(e, d, num_segments=n)
            ex = jnp.exp(e - m[d])
            denom = jax.ops.segment_sum(ex, d, num_segments=n)
            att = ex / (denom[d] + SM_EPS)
            msg = xw[s] * att[:, :, None]
            out = jax.ops.segment_sum(msg, d, num_segments=n)
            out = out.reshape(n, heads * out_c) if concat else out.mean(axis=1)
            return out + b

        def _layer_norm(x, g, b):
            mu = x.mean(-1, keepdims=True)
            var = ((x - mu) ** 2).mean(-1, keepdims=True)
            return (x - mu) * jax.lax.rsqrt(var + LN_EPS) * g + b
        key = jax.random.key(seed)
        ks = jax.random.split(key, 12)
        s = 0.1
        return {'h': jax.random.normal(ks[0], (N, IN_DIM), jnp.float32), 'edge_index': jax.random.randint(ks[1], (2, E), 0, N, jnp.int32), 'W1': jax.random.normal(ks[2], (IN_DIM, HEADS * 16), jnp.float32) * s, 'a1_src': jax.random.normal(ks[3], (HEADS, 16), jnp.float32) * s, 'a1_dst': jax.random.normal(ks[4], (HEADS, 16), jnp.float32) * s, 'b1': jnp.zeros((HEADS * 16,), jnp.float32), 'W2': jax.random.normal(ks[5], (OUT_DIM, OUT_DIM), jnp.float32) * s, 'a2_src': jax.random.normal(ks[6], (1, OUT_DIM), jnp.float32) * s, 'a2_dst': jax.random.normal(ks[7], (1, OUT_DIM), jnp.float32) * s, 'b2': jnp.zeros((OUT_DIM,), jnp.float32), 'ln1_g': jnp.ones((OUT_DIM,), jnp.float32), 'ln1_b': jnp.zeros((OUT_DIM,), jnp.float32), 'ln2_g': jnp.ones((OUT_DIM,), jnp.float32), 'ln2_b': jnp.zeros((OUT_DIM,), jnp.float32)}
    _L1_gnn_all = _L1_gnn_setup()
    _L1_gnn_in = {k: v for k, v in _L1_gnn_all.items() if k in ('W1', 'a1_src', 'a1_dst', 'b1', 'W2', 'a2_src', 'a2_dst', 'b2', 'ln1_g', 'ln1_b', 'ln2_g', 'ln2_b')}
    del _L1_gnn_all

    def _L2_gnn_setup():
        import jax, jax.numpy as jnp
        import numpy as np
        N_NODES = 6250
        N_EDGES = 100000
        D_IN = 64
        D_OUT = 64
        key = jax.random.key(seed)
        k1, k2, k3, k4 = jax.random.split(key, 4)
        x = jax.random.normal(k1, (N_NODES, D_IN), dtype=jnp.float32)
        edge_index = jax.random.randint(k2, (2, N_EDGES), 0, N_NODES, dtype=jnp.int64)
        W = jax.random.normal(k3, (D_IN, D_OUT), dtype=jnp.float32) * (1.0 / np.sqrt(D_IN))
        b = jax.random.normal(k4, (D_OUT,), dtype=jnp.float32) * 0.01
        return {'x': x, 'edge_index': edge_index, 'W': W, 'b': b}
    _L2_gnn_all = _L2_gnn_setup()
    _L2_gnn_in = {k: v for k, v in _L2_gnn_all.items() if k in ('W', 'b')}
    del _L2_gnn_all

    def _L3_gnn_setup():
        import jax, jax.numpy as jnp
        import numpy as np
        N = 6250
        E = 100000
        D = 64
        A = 64
        R = 4
        OUT = 64
        key = jax.random.key(seed)
        ks = jax.random.split(key, 10)
        h = jax.random.normal(ks[0], (N, D), jnp.float32)
        r = jax.random.normal(ks[1], (R, 2 * D, D), jnp.float32) * 0.1
        a = jax.random.normal(ks[2], (R, A), jnp.float32)
        Wa_w = jax.random.normal(ks[3], (A, 2 * D), jnp.float32) * (1.0 / np.sqrt(2 * D))
        Wa_b = jnp.zeros((A,), jnp.float32)
        lin_w = jax.random.normal(ks[4], (OUT, 2 * D), jnp.float32) * (1.0 / np.sqrt(2 * D))
        lin_b = jnp.zeros((OUT,), jnp.float32)
        src = jax.random.randint(ks[5], (E,), 0, N)
        dst = jax.random.randint(ks[6], (E,), 0, N)
        etype = jax.random.randint(ks[7], (E,), 0, R)
        return dict(h=h, r=r, a=a, Wa_w=Wa_w, Wa_b=Wa_b, lin_w=lin_w, lin_b=lin_b, src=src, dst=dst, etype=etype)
    _L3_gnn_all = _L3_gnn_setup()
    _L3_gnn_in = {k: v for k, v in _L3_gnn_all.items() if k in ('r', 'a', 'Wa_w', 'Wa_b', 'lin_w', 'lin_b')}
    del _L3_gnn_all
    return {'x': x, 'src': src, 'dst': dst, 'edge_type_4': edge_type_4, 'L1_gnn_W1': _L1_gnn_in['W1'], 'L1_gnn_a1_src': _L1_gnn_in['a1_src'], 'L1_gnn_a1_dst': _L1_gnn_in['a1_dst'], 'L1_gnn_b1': _L1_gnn_in['b1'], 'L1_gnn_W2': _L1_gnn_in['W2'], 'L1_gnn_a2_src': _L1_gnn_in['a2_src'], 'L1_gnn_a2_dst': _L1_gnn_in['a2_dst'], 'L1_gnn_b2': _L1_gnn_in['b2'], 'L1_gnn_ln1_g': _L1_gnn_in['ln1_g'], 'L1_gnn_ln1_b': _L1_gnn_in['ln1_b'], 'L1_gnn_ln2_g': _L1_gnn_in['ln2_g'], 'L1_gnn_ln2_b': _L1_gnn_in['ln2_b'], 'L2_gnn_W': _L2_gnn_in['W'], 'L2_gnn_b': _L2_gnn_in['b'], 'L3_gnn_r': _L3_gnn_in['r'], 'L3_gnn_a': _L3_gnn_in['a'], 'L3_gnn_Wa_w': _L3_gnn_in['Wa_w'], 'L3_gnn_Wa_b': _L3_gnn_in['Wa_b'], 'L3_gnn_lin_w': _L3_gnn_in['lin_w'], 'L3_gnn_lin_b': _L3_gnn_in['lin_b']}

def reference(x, src, dst, edge_type_4, L1_gnn_W1, L1_gnn_a1_src, L1_gnn_a1_dst, L1_gnn_b1, L1_gnn_W2, L1_gnn_a2_src, L1_gnn_a2_dst, L1_gnn_b2, L1_gnn_ln1_g, L1_gnn_ln1_b, L1_gnn_ln2_g, L1_gnn_ln2_b, L2_gnn_W, L2_gnn_b, L3_gnn_r, L3_gnn_a, L3_gnn_Wa_w, L3_gnn_Wa_b, L3_gnn_lin_w, L3_gnn_lin_b):
    import jax
    import jax.numpy as jnp

    def _L0_gnn_ref(H, row, col, num_nodes):
        import jax, jax.numpy as jnp
        import numpy as np
        N = 12500
        E = 200000
        D = 64
        EPS = 1e-12
        norm = jnp.sqrt(jnp.sum(H * H, axis=1, keepdims=True))
        Hn = H / jnp.maximum(norm, EPS)
        scores = jnp.sum(Hn[row] * Hn[col], axis=1)
        m = jax.ops.segment_max(scores, row, num_segments=num_nodes)
        e = jnp.exp(scores - m[row])
        s = jax.ops.segment_sum(e, row, num_segments=num_nodes)
        attn = e / s[row]
        out = jax.ops.segment_sum(attn[:, None] * H[col], row, num_segments=num_nodes)
        return out

    def _L1_gnn_ref(h, edge_index, W1, a1_src, a1_dst, b1, W2, a2_src, a2_dst, b2, ln1_g, ln1_b, ln2_g, ln2_b):
        import jax, jax.numpy as jnp
        import numpy as np
        N, E = (6250, 156250)
        IN_DIM, OUT_DIM, HEADS = (64, 64, 4)
        NEG_SLOPE = 0.2
        LN_EPS = 1e-05
        SM_EPS = 1e-16

        def _gat_conv(x, src, dst, W, a_src, a_dst, b, heads, out_c, concat):
            n = x.shape[0]
            xw = (x @ W).reshape(n, heads, out_c)
            asrc = jnp.einsum('nhc,hc->nh', xw, a_src)
            adst = jnp.einsum('nhc,hc->nh', xw, a_dst)
            loop = jnp.arange(n, dtype=src.dtype)
            s = jnp.concatenate([src, loop])
            d = jnp.concatenate([dst, loop])
            e = jax.nn.leaky_relu(asrc[s] + adst[d], NEG_SLOPE)
            m = jax.ops.segment_max(e, d, num_segments=n)
            ex = jnp.exp(e - m[d])
            denom = jax.ops.segment_sum(ex, d, num_segments=n)
            att = ex / (denom[d] + SM_EPS)
            msg = xw[s] * att[:, :, None]
            out = jax.ops.segment_sum(msg, d, num_segments=n)
            out = out.reshape(n, heads * out_c) if concat else out.mean(axis=1)
            return out + b

        def _layer_norm(x, g, b):
            mu = x.mean(-1, keepdims=True)
            var = ((x - mu) ** 2).mean(-1, keepdims=True)
            return (x - mu) * jax.lax.rsqrt(var + LN_EPS) * g + b
        src, dst = (edge_index[0], edge_index[1])
        x = _gat_conv(h, src, dst, W1, a1_src, a1_dst, b1, HEADS, 16, True)
        x = jax.nn.elu(_layer_norm(x, ln1_g, ln1_b))
        z = _gat_conv(x, src, dst, W2, a2_src, a2_dst, b2, 1, OUT_DIM, False)
        z = jax.nn.elu(_layer_norm(z, ln2_g, ln2_b))
        return z

    def _L2_gnn_ref(x, edge_index, W, b):
        import jax, jax.numpy as jnp
        import numpy as np
        N_NODES = 6250
        N_EDGES = 100000
        D_IN = 64
        D_OUT = 64
        N = x.shape[0]
        loop = jnp.arange(N, dtype=edge_index.dtype)
        src = jnp.concatenate([edge_index[0], loop])
        dst = jnp.concatenate([edge_index[1], loop])
        xw = x @ W
        ones = jnp.ones(src.shape[0], dtype=x.dtype)
        deg = jax.ops.segment_sum(ones, dst, num_segments=N)
        dis = jnp.where(deg > 0, jax.lax.rsqrt(jnp.maximum(deg, 1.0)), 0.0)
        norm = dis[src] * dis[dst]
        msgs = norm[:, None] * xw[src]
        out = jax.ops.segment_sum(msgs, dst, num_segments=N) + b
        return jax.nn.relu(out)

    def _L3_gnn_ref(h, r, a, Wa_w, Wa_b, lin_w, lin_b, src, dst, etype):
        import jax, jax.numpy as jnp
        import numpy as np
        N = 6250
        E = 100000
        D = 64
        A = 64
        R = 4
        OUT = 64
        num_nodes = h.shape[0]
        hs = h[src]
        hd = h[dst]
        cat = jnp.concatenate([hd, hs], axis=-1)
        gate_logit = jnp.zeros((cat.shape[0], r.shape[-1]), cat.dtype)
        for i in range(r.shape[0]):
            gate_logit = gate_logit + jnp.where((etype == i)[:, None], cat @ r[i], 0.0)
        gate = jax.nn.sigmoid(gate_logit)
        att_feat = jax.nn.leaky_relu(cat @ Wa_w.T + Wa_b)
        a_sc = jnp.sum(att_feat * a[0], axis=-1)
        seg_max = jax.ops.segment_max(a_sc, dst, num_segments=num_nodes)
        ex = jnp.exp(a_sc - seg_max[dst])
        seg_sum = jax.ops.segment_sum(ex, dst, num_segments=num_nodes)
        att_n = ex / seg_sum[dst]
        scale = att_n[:, None] * gate
        msg = hs * scale
        h_N = jax.ops.segment_sum(msg, dst, num_segments=num_nodes)
        out = jnp.concatenate([h, h_N], axis=-1) @ lin_w.T + lin_b
        return jax.nn.leaky_relu(out)
    edge_index = jnp.stack([src, dst])
    h = jnp.maximum(_layernorm(x, axis=-1), 0.0)
    x = x + _L0_gnn_ref(h, src, dst, 12500)
    h = jnp.maximum(_layernorm(x, axis=-1), 0.0)
    x = x + _L1_gnn_ref(h, edge_index, L1_gnn_W1, L1_gnn_a1_src, L1_gnn_a1_dst, L1_gnn_b1, L1_gnn_W2, L1_gnn_a2_src, L1_gnn_a2_dst, L1_gnn_b2, L1_gnn_ln1_g, L1_gnn_ln1_b, L1_gnn_ln2_g, L1_gnn_ln2_b)
    h = jnp.maximum(_layernorm(x, axis=-1), 0.0)
    x = x + _L2_gnn_ref(h, edge_index, L2_gnn_W, L2_gnn_b)
    h = jnp.maximum(_layernorm(x, axis=-1), 0.0)
    x = x + _L3_gnn_ref(h, L3_gnn_r, L3_gnn_a, L3_gnn_Wa_w, L3_gnn_Wa_b, L3_gnn_lin_w, L3_gnn_lin_b, src, dst, edge_type_4)
    return x

_drawn_inputs = setup_inputs


def setup_inputs(seed=0):
    import zlib

    import numpy as np

    out = dict(_drawn_inputs(seed))
    spreads = {'L1_gnn_b1': (0.0, 0.1),
     'L1_gnn_b2': (0.0, 0.1),
     'L1_gnn_ln1_g': (1.0, 0.2),
     'L1_gnn_ln1_b': (0.0, 0.1),
     'L1_gnn_ln2_g': (1.0, 0.2),
     'L1_gnn_ln2_b': (0.0, 0.1),
     'L3_gnn_Wa_b': (0.0, 2.0),
     'L3_gnn_lin_b': (0.0, 0.1)}
    factors = {'L1_gnn_a1_dst': 26.728, 'L1_gnn_a2_src': 5.546, 'L1_gnn_a2_dst': 8.0, 'L2_gnn_b': 8.0}
    for name, (base, spread) in spreads.items():
        noise = np.random.default_rng([zlib.crc32(name.encode()), seed]).standard_normal(out[name].shape)
        drawn = base * np.exp(spread * noise) if base else spread * noise
        out[name] = jnp.asarray(drawn.astype(out[name].dtype))
    for name, factor in factors.items():
        out[name] = (out[name] * factor).astype(out[name].dtype)
    return out
```

```python
from contextlib import ExitStack

import concourse.bass as bass
from concourse import mybir

F32, BF16, I32 = mybir.dt.float32, mybir.dt.bfloat16, mybir.dt.int32
ALU = mybir.AluOpType
ACT = mybir.ActivationFunctionType
AX = mybir.AxisListType.X
DVE = [mybir.EngineType.DVE]

N, E, D, TYPES = 12500, 212500, 64, 4
P = 128
BLOCKS = -(-N // P)
NPAD = BLOCKS * P
ROWS = NPAD + P
SLOTS = 4
RING = 4
STAGES = 2
PER_STAGE = RING // STAGES
WIDE = 32
WCH = WIDE // SLOTS
CHUNKS = E // SLOTS + BLOCKS + 16
CROW = 2 * SLOTS + 1
EP, EC = 125, 1700
NP_, NC = 125, 100
BINS = 64
H1, C1 = 4, 16
SLOPE, LN_EPS, SM_EPS = 0.2, 1e-5, 1e-16
MINUS = -1e30
GROUP = 14
TURNS = BLOCKS // GROUP
AW = D + 1
RROW = AW + 2 * D
OROW = AW + TYPES * D


class Mem:

    def __init__(self, nc, ctx):
        self.nc, self.ctx = nc, ctx
        self.stage = nc.next_id()
        self.sems = []
        ctx.callback(self.close)

    def close(self):
        if self.sems:
            self.nc.clear_and_free_semaphores(self.sems)
            self.nc.all_engine_barrier()

    def name(self, name):
        return f"{name}_{self.stage}"

    def sb(self, name, shape, dt=F32):
        return self.ctx.enter_context(self.nc.sbuf_tensor(self.name(name), shape, dt))

    def ps(self, name, shape, dt=F32):
        return self.ctx.enter_context(self.nc.psum_tensor(self.name(name), shape, dt))

    def sem(self, name):
        self.sems.append(self.nc.alloc_semaphore(self.name(name)))
        return self.sems[-1]


class Chain:

    def __init__(self, eng, sem):
        self.eng, self.sem, self.n = eng, sem, 0

    def add(self, ins):
        ins.then_inc(self.sem, 1)
        self.n += 1
        return self.n

    def wait(self, n=None):
        self.eng.wait_ge(self.sem, self.n if n is None else n)

    def link(self, ins):
        self.add(ins)
        self.wait()


def chunk_at(nc, c):
    return nc.s_assert_within(c, 0, CHUNKS - 1, skip_runtime_bounds_check_because="CHUNKS holds "
                              "the chunks of any degrees: their blocks' largest add up to at most E")




def at(ap, axis=0):
    return bass.IndirectOffsetOnAxis(ap=ap, axis=axis)


def bc(ap, shape):
    return ap.to_broadcast(shape)


def constants(nc, k):
    with ExitStack() as ctx:
        made = Mem(nc, ctx).sem("const_made")
        block = ctx.enter_context(nc.Block())

        @block.gpsimd
        def _(pool):
            ch = Chain(pool, made)
            ch.add(pool.memset(k.ident[:, :], 0.0))
            ch.add(pool.memset(k.ones[:, :], 1.0))
            ch.add(pool.memset(k.before[:, :], 1.0))
            ch.add(pool.memset(k.zeros[:, :], 0.0))
            ch.add(pool.iota(k.iota_i[:, :], [[1, P]], base=0, channel_multiplier=0))
            ch.add(pool.iota(k.node_i[:, :], [[P, BLOCKS]], base=0, channel_multiplier=1))
            ch.link(pool.iota(k.dummy_i[:, :], [[0, 1]], base=NPAD, channel_multiplier=1))
            ch.add(pool.affine_select(out=k.ident[:, :], in_=k.ident[:, :], compare_op=ALU.not_equal,
                                      fill=1.0, base=0, pattern=[[-1, P]], channel_multiplier=1))
            ch.link(pool.affine_select(out=k.before[:, :], in_=k.before[:, :], compare_op=ALU.is_gt,
                                       fill=0.0, base=0, pattern=[[1, P]], channel_multiplier=-1))

        @block.vector
        def _(dve):
            dve.wait_ge(made, 9)
            nc.vector.tensor_copy(k.iota[:, :], k.iota_i[:, :]).then_inc(k.const_ready, 1)
            nc.vector.tensor_copy(k.dummy[:, :], k.dummy_i[:, :]).then_inc(k.const_ready, 1)
            nc.vector.tensor_scalar(k.dummy4[:, :], k.dummy_i[:, :], 4.0, None, ALU.mult)\
                .then_inc(k.const_ready, 1)
            dve.wait_ge(k.const_ready, 3)


def count_and_open(nc, k, a):
    T = 17
    with ExitStack() as ctx:
        m = Mem(nc, ctx)
        src = m.sb("src_sb", [EP, EC], I32)
        dst = m.sb("dst_sb", [EP, EC], I32)
        typ = m.sb("typ_sb", [EP, EC], I32)
        lo_i = m.sb("lo_i", [EP, EC], I32)
        hi_i = m.sb("hi_i", [EP, EC], I32)
        lo = m.sb("lo", [EP, EC], BF16)
        hi = m.sb("hi", [EP, EC], BF16)
        iota_b = m.sb("iota_b", [P, P], BF16)
        hot = m.sb("hot", [EP, 2, T, P + BLOCKS], BF16)
        zero_b = m.sb("zero_b", [P, P + BLOCKS], BF16)
        xd = m.sb("xd", [NP_, NC, D])
        hh = m.sb("hh", [NP_, NC, 2 * D])
        sq = m.sb("sq", [NP_, NC, D])
        st = m.sb("st", [NP_, 4, NC])
        counts = m.ps("counts", [P, BLOCKS])
        dst_in, code_in, x_in = m.sem("dst_in"), m.sem("code_in"), m.sem("x_in")
        codes_out, runs_out, h_out = m.sem("codes_out"), m.sem("runs_out"), m.sem("h_out")
        step, codes_made = m.sem("dve_step"), m.sem("codes_made")
        hot_ready = [m.sem("hot_ready0"), m.sem("hot_ready1")]
        hot_used = [m.sem("hot_used0"), m.sem("hot_used1")]
        turn_step = m.sem("turn_step")
        counted = m.sem("counted")
        var_ready, std_ready = m.sem("var_ready"), m.sem("std_ready")
        h_made = m.sem("h_made")
        block = ctx.enter_context(nc.Block())

        @block.sync
        def _(sp):
            sp.dma_start(dst[:, :], a["dst"].rearrange("(p c) -> p c", p=EP)).then_inc(dst_in, 16)
            sp.dma_start(src[:, :], a["src"].rearrange("(p c) -> p c", p=EP)).then_inc(code_in, 16)
            sp.dma_start(typ[:, :], a["edge_type_4"].rearrange("(p c) -> p c", p=EP)).then_inc(code_in, 16)
            sp.dma_start(xd[:, :, :], a["x"].rearrange("(p c) d -> p c d", p=NP_)).then_inc(x_in, 16)
            sp.wait_ge(codes_made, 1)
            sp.dma_start(k.codes[0:E].rearrange("(p c) -> p c", p=EP), src[:, :]).then_inc(codes_out, 16)
            sp.dma_start(k.codes[E:E + WIDE].rearrange("(a c) -> a c", a=1),
                         k.zeros[0:1, 0:WIDE].bitcast(I32)).then_inc(codes_out, 16)
            sp.wait_ge(codes_out, 32)
            overlapped = bass.AP(k.codes.tensor, 0, [[1, E], [1, WIDE]])
            sp.dma_start(k.runs[:, :], overlapped).then_inc(runs_out, 16)
            sp.dma_start(k.hn_tab[N:N + P, :], k.zeros[:, 0:D]).then_inc(h_out, 16)
            sp.dma_start(k.hn_tab[N + P:ROWS, :], k.zeros[0:ROWS - N - P, 0:D]).then_inc(h_out, 16)
            sp.dma_start(k.hh_tab[N:NPAD, :], k.zeros[0:NPAD - N, 0:2 * D]).then_inc(h_out, 16)
            sp.dma_start(k.x1_tab[N:NPAD, :], k.zeros[0:NPAD - N, 0:D]).then_inc(h_out, 16)
            for s in range(SLOTS):
                sp.dma_start(k.sums[s].rearrange("(p c) d -> p c d", p=P),
                             bc(k.zeros[:, 0:D + 1].unsqueeze(1), [P, ROWS // P, D + 1])).then_inc(h_out, 16)
            sp.wait_ge(h_made, 1)
            sp.dma_start(k.hn_tab[0:N, :].rearrange("(p c) d -> p c d", p=NP_), sq[:, :, :]).then_inc(h_out, 16)
            sp.dma_start(k.hh_tab[0:N, :].rearrange("(p c) d -> p c d", p=NP_), hh[:, :, :]).then_inc(h_out, 16)
            sp.wait_ge(runs_out, 16)
            sp.wait_ge(h_out, 16 * (6 + SLOTS))

        @block.vector
        def _(dve):
            ch = Chain(dve, step)
            ch.add(nc.vector.tensor_copy(iota_b[:, :], k.iota[:, :]))
            ch.add(nc.vector.memset(zero_b[:, :], 0.0))
            dve.wait_ge(dst_in, 16)
            ch.add(nc.vector.tensor_single_scalar(lo_i[:, :], dst[:, :], P - 1, ALU.bitwise_and))
            ch.link(nc.vector.tensor_single_scalar(hi_i[:, :], dst[:, :], 7, ALU.logical_shift_right))
            ch.add(nc.vector.tensor_copy(lo[:, :], lo_i[:, :]))
            ch.add(nc.vector.tensor_copy(hi[:, :], hi_i[:, :]))
            dve.wait_ge(code_in, 32)
            nc.vector.scalar_tensor_tensor(out=src[:, :], in0=src[:, :], scalar=float(TYPES), in1=typ[:, :],
                                           op0=ALU.mult, op1=ALU.add).then_inc(codes_made, 1)
            ch.wait()
            dve.sem_inc(hot_used[0], 1)
            dve.sem_inc(hot_used[1], 1)
            with dve.Fori(0, EC // (2 * T)) as i:
                for h in range(2):
                    cols = bass.ds(i * (2 * T) + h * T, T)
                    dve.wait_ge(hot_used[h], i + 1)
                    nc.vector.tensor_tensor(hot[:, h, :, 0:P], bc(lo[:, cols].unsqueeze(2), [EP, T, P]),
                                            bc(iota_b[0:EP, :].unsqueeze(1), [EP, T, P]), ALU.is_equal)\
                        .then_inc(hot_ready[h], 1)
                    nc.vector.tensor_tensor(hot[:, h, :, P:P + BLOCKS],
                                            bc(hi[:, cols].unsqueeze(2), [EP, T, BLOCKS]),
                                            bc(iota_b[0:EP, 0:BLOCKS].unsqueeze(1), [EP, T, BLOCKS]),
                                            ALU.is_equal).then_inc(hot_ready[h], 1)
            dve.wait_ge(counted, 1)
            ch.link(nc.vector.tensor_copy(k.deg[:, :], counts[:, :]))
            dve.wait_ge(x_in, 16)
            h = hh[:, :, 0:D]
            relu_norm(nc, dve, ch, xd[:, :, :], h, sq[:, :, :], st, [NP_, NC, D], var_ready, std_ready, 1)
            ch.link(nc.vector.tensor_tensor(sq[:, :, :], h, h, ALU.mult))
            ch.link(nc.vector.tensor_reduce(st[:, 0, :], sq[:, :, :], AX, ALU.add))
            nc.vector.tensor_copy(st[:, 1, :], st[:, 0, :]).then_inc(var_ready, 1)
            dve.wait_ge(std_ready, 2)
            ch.link(nc.vector.tensor_scalar(st[:, 0, :], st[:, 2, :], 1e-12, None, ALU.max))
            ch.link(nc.vector.reciprocal(st[:, 3, :], st[:, 0, :]))
            ch.link(nc.vector.tensor_tensor(hh[:, :, D:2 * D], h, bc(st[:, 3, :].unsqueeze(2), [NP_, NC, D]),
                                            ALU.mult))
            nc.vector.tensor_copy(sq[:, :, :], hh[:, :, D:2 * D]).then_inc(h_made, 1)
            dve.wait_ge(h_made, 1)

        @block.scalar
        def _(act):
            for n in range(2):
                act.wait_ge(var_ready, n + 1)
                nc.scalar.activation(st[:, 2, :], st[:, 1, :], ACT.Sqrt).then_inc(std_ready, 1)

        @block.tensor
        def _(pe):
            pe.wait_ge(step, 2)
            nc.tensor.matmul(counts[:, :], zero_b[0:EP, 0:P], zero_b[0:EP, P:P + BLOCKS], start=True, stop=False,
                             skip_group_check=True)
            with pe.Fori(0, EC // (2 * T)) as i:
                for h in range(2):
                    pe.wait_ge(hot_ready[h], i * 2 + 2)
                    for t in range(T):
                        last = nc.tensor.matmul(counts[:, :], hot[:, h, t, 0:P], hot[:, h, t, P:P + BLOCKS],
                                                start=False, stop=False, skip_group_check=True)
                    last.then_inc(hot_used[h], 1)
            nc.tensor.matmul(counts[:, :], zero_b[0:EP, 0:P], zero_b[0:EP, P:P + BLOCKS], start=False, stop=True,
                             skip_group_check=True).then_inc(counted, 1)


def relu_norm(nc, dve, ch, x, h, sq, st, shape, var_ready, std_ready, n):
    wide = lambda j: bc(st[:, j, :].unsqueeze(2), shape)
    ch.link(nc.vector.tensor_reduce(st[:, 0, :], x, AX, ALU.add))
    ch.link(nc.vector.tensor_scalar(st[:, 3, :], st[:, 0, :], 1.0 / D, None, ALU.mult))
    ch.link(nc.vector.tensor_tensor(h, x, wide(3), ALU.subtract))
    ch.link(nc.vector.tensor_tensor(sq, h, h, ALU.mult))
    ch.link(nc.vector.tensor_reduce(st[:, 0, :], sq, AX, ALU.add))
    nc.vector.tensor_scalar(st[:, 1, :], st[:, 0, :], 1.0 / D, LN_EPS, ALU.mult, ALU.add).then_inc(var_ready, 1)
    dve.wait_ge(std_ready, n)
    ch.link(nc.vector.reciprocal(st[:, 3, :], st[:, 2, :]))
    ch.link(nc.vector.tensor_scalar(sq, h, 0.0, None, ALU.max))
    ch.link(nc.vector.tensor_tensor(h, sq, wide(3), ALU.mult))


def rank_nodes(nc, k):
    with ExitStack() as ctx:
        m = Mem(nc, ctx)
        tot = m.sb("tot", [P, BLOCKS])
        incl = m.sb("incl", [P, BLOCKS])
        binned = m.sb("binned", [P, BLOCKS])
        same = m.sb("same", [P, BINS, BLOCKS])
        upto = m.sb("upto", [P, BINS, BLOCKS])
        cnt = m.sb("cnt", [P, BINS])
        cum = m.sb("cum", [P, BINS])
        btot = m.sb("btot", [P, BINS])
        off = m.sb("off", [P, BINS])
        rank = m.sb("rank", [P, BLOCKS])
        rank_i = m.sb("rank_i", [P, BLOCKS], I32)
        info = m.sb("info", [P, BLOCKS, 4], I32)
        p_tot = m.ps("p_tot", [P, BLOCKS])
        p_pre = m.ps("p_pre", [P, BLOCKS])
        p_btot = m.ps("p_btot", [P, BINS])
        p_bpre = m.ps("p_bpre", [P, BINS])
        step, summed, cnt_ready, bsummed = m.sem("step"), m.sem("summed"), m.sem("cnt_ready"), m.sem("bsummed")
        ranked, scattered = m.sem("ranked"), m.sem("scattered")
        block = ctx.enter_context(nc.Block())

        @block.tensor
        def _(pe):
            nc.tensor.matmul(p_tot[:, :], k.ones[:, :], k.deg[:, :], start=True, stop=True)
            nc.tensor.matmul(p_pre[:, :], k.before[:, :], k.deg[:, :], start=True, stop=True).then_inc(summed, 1)
            pe.wait_ge(cnt_ready, 1)
            nc.tensor.matmul(p_btot[:, :], k.ones[:, :], cnt[:, :], start=True, stop=True)
            nc.tensor.matmul(p_bpre[:, :], k.before[:, :], cnt[:, :], start=True, stop=True).then_inc(bsummed, 1)

        @block.vector
        def _(dve):
            ch = Chain(dve, step)
            ch.link(nc.vector.tensor_scalar(binned[:, :], k.deg[:, :], float(BINS - 1), None, ALU.min))
            ch.link(nc.vector.tensor_tensor(same[:, :, :], bc(binned[:, :].unsqueeze(1), [P, BINS, BLOCKS]),
                                            bc(k.iota[:, 0:BINS].unsqueeze(2), [P, BINS, BLOCKS]), ALU.is_equal))
            ch.link(nc.vector.tensor_reduce(cnt[:, :], same[:, :, :], AX, ALU.add))
            dve.sem_inc(cnt_ready, 1)
            flat = same[:, :, :].rearrange("p v j -> p (v j)")
            ch.add(nc.vector.tensor_tensor_scan(upto[:, :, :].rearrange("p v j -> p (v j)"), flat, flat, 0.0,
                                                ALU.add, ALU.max))
            ch.link(nc.vector.tensor_tensor_scan(cum[:, :], cnt[:, :], cnt[:, :], 0.0, ALU.add, ALU.max))
            ch.link(nc.vector.tensor_tensor(off[:, :], cnt[:, :], cum[:, :], ALU.subtract))
            dve.wait_ge(bsummed, 1)
            ch.link(nc.vector.tensor_copy(btot[:, :], p_btot[:, :]))
            ch.link(nc.vector.tensor_tensor_scan(cum[:, :], btot[:, :], btot[:, :], 0.0, ALU.add, ALU.max))
            ch.link(nc.vector.tensor_tensor(cum[:, :], cum[:, :], btot[:, :], ALU.subtract))
            ch.link(nc.vector.tensor_tensor(off[:, :], off[:, :], cum[:, :], ALU.add))
            ch.link(nc.vector.tensor_tensor(off[:, :], off[:, :], p_bpre[:, :], ALU.add))
            ch.link(nc.vector.tensor_tensor(upto[:, :, :], upto[:, :, :],
                                            bc(off[:, :].unsqueeze(2), [P, BINS, BLOCKS]), ALU.add))
            ch.link(nc.vector.tensor_tensor(upto[:, :, :], upto[:, :, :], same[:, :, :], ALU.mult))
            ch.link(nc.vector.tensor_reduce(rank[:, :], upto[:, :, :].rearrange("p v j -> p j v"), AX, ALU.add))
            ch.link(nc.vector.tensor_scalar(rank_i[:, :], rank[:, :], -1.0, None, ALU.add))
            dve.wait_ge(summed, 1)
            ch.link(nc.vector.tensor_copy(tot[:, :], p_tot[:, :]))
            ch.link(nc.vector.tensor_tensor_scan(incl[:, :], tot[:, :], tot[:, :], 0.0, ALU.add, ALU.max))
            ch.link(nc.vector.tensor_tensor(incl[:, :], incl[:, :], tot[:, :], ALU.subtract))
            ch.add(nc.vector.tensor_tensor(info[:, :, 1], incl[:, :], p_pre[:, :], ALU.add))
            ch.add(nc.vector.tensor_copy(info[:, :, 0], k.node_i[:, :]))
            ch.add(nc.vector.tensor_copy(info[:, :, 2], k.deg[:, :]))
            ch.link(nc.vector.memset(info[:, :, 3], 0))
            dve.sem_inc(ranked, 1)

        @block.gpsimd
        def _(pool):
            pool.wait_ge(ranked, 1)
            for j in range(BLOCKS):
                pool.indirect_dma_start(k.info_tab[:, :], at(rank_i[:, j:j + 1]), info[:, j, :], None)\
                    .then_inc(scattered, 16)
            pool.wait_ge(scattered, 16 * BLOCKS)


def build_chunks(nc, k):
    with ExitStack() as ctx:
        m = Mem(nc, ctx)
        info = m.sb("info_r", [P, BLOCKS, 4], I32)
        first = m.sb("first", [P, BLOCKS])
        first_i = m.sb("first_i", [P, BLOCKS], I32)
        wide = m.sb("wide", [P, BLOCKS, WIDE], I32)
        valid = m.sb("valid", [P, BLOCKS, WIDE])
        code = m.sb("code", [P, BLOCKS, WIDE])
        code_i = m.sb("code_i", [P, BLOCKS, WIDE], I32)
        rows = m.sb("rows", [P, BLOCKS, WCH, CROW], I32)
        tail = m.sb("tail", [P, 1, CROW], I32)
        dmax = m.sb("dmax", [BLOCKS, 4])
        nch_i = m.sb("nch_i", [BLOCKS, 1], I32)
        row = m.sb("row", [1, 4, BLOCKS])
        one = m.sb("one", [1, BLOCKS])
        ctl = m.sb("ctl", [1, 8])
        x_first = m.sb("x_first", [P, 1])
        x_first_i = m.sb("x_first_i", [P, 1], I32)
        x_wide = m.sb("x_wide", [P, WIDE], I32)
        x_valid = m.sb("x_valid", [P, SLOTS])
        x_code = m.sb("x_code", [P, SLOTS])
        x_code_i = m.sb("x_code_i", [P, SLOTS], I32)
        x_pos = m.sb("x_pos", [P, 1])
        x_row = m.sb("x_row", [P, 1, CROW], I32)
        p_deg = m.ps("p_deg", [BLOCKS, P])
        p_start = m.ps("p_start", [BLOCKS, 1])
        p_row = m.ps("p_row", [1, 4, BLOCKS])
        info_in, step, deg_ready, degT = m.sem("info_in"), m.sem("step"), m.sem("deg_ready"), m.sem("degT")
        nch_ready, start_ready, cols_ready, rows_ready = (m.sem("nch_ready"), m.sem("start_ready"),
                                                          m.sem("cols_ready"), m.sem("rows_ready"))
        first_ready, wide_in, blocks_ready = m.sem("first_ready"), m.sem("wide_in"), m.sem("blocks_ready")
        chunk_rows, written = m.sem("chunk_rows"), m.sem("written")
        x_asked, x_in, x_made, x_out, x_turn = (m.sem("x_asked"), m.sem("x_in"), m.sem("x_made"), m.sem("x_out"),
                                                m.sem("x_turn"))
        tail_out, in_row, x_step, tick = m.sem("tail_out"), m.sem("in_row"), m.sem("x_step"), m.sem("tick")
        block = ctx.enter_context(nc.Block())

        @block.gpsimd
        def _(pool):
            pool.iota(rows[:, :, :, CROW - 1], [[1, BLOCKS], [0, WCH]], base=0, channel_multiplier=0)\
                .then_inc(blocks_ready, 1)
            pool.wait_ge(first_ready, 1)
            for b in range(BLOCKS):
                pool.indirect_dma_start(wide[:, b, :], None, k.runs[:, :], at(first_i[:, b:b + 1])).then_inc(wide_in, 16)
            pool.wait_ge(rows_ready, 1)
            n_x = pool.value_load(k.ctl_i[0:1, 3:4], min_val=1, max_val=CHUNKS)
            with pool.Fori(0, n_x) as t:
                pool.wait_ge(x_asked, t + 1)
                pool.sem_inc(x_turn, 1)
                pool.indirect_dma_start(x_wide[:, :], None, k.runs[:, :], at(x_first_i[:, :])).then_inc(x_in, 16)

        @block.tensor
        def _(pe):
            pe.wait_ge(deg_ready, 1)
            nc.tensor.transpose(p_deg[:, :], k.deg_r[:, :], k.ident[:, :]).then_inc(degT, 1)
            pe.wait_ge(nch_ready, 1)
            nc.tensor.matmul(p_start[:, :], k.before[0:BLOCKS, 0:BLOCKS], dmax[:, 1:2], start=True, stop=True)\
                .then_inc(start_ready, 1)
            pe.wait_ge(cols_ready, 1)
            for j in range(2):
                last = nc.tensor.matmul(p_row[:, j, :], dmax[:, 1 + j:2 + j], k.ident[0:BLOCKS, 0:BLOCKS],
                                        start=True, stop=True)
            last.then_inc(in_row, 1)

        @block.vector
        def _(dve):
            ch = Chain(dve, step)
            dve.wait_ge(info_in, 16)
            ch.add(nc.vector.tensor_copy(k.node_r[:, :], info[:, :, 0]))
            ch.add(nc.vector.tensor_copy(first[:, :], info[:, :, 1]))
            ch.add(nc.vector.memset(tail[:, :, :], 0))
            ch.link(nc.vector.tensor_copy(k.deg_r[:, :], info[:, :, 2]))
            dve.sem_inc(deg_ready, 1)
            nc.vector.tensor_scalar(first_i[:, :], first[:, :], float(E - 1), None, ALU.min).then_inc(first_ready, 1)
            dve.wait_ge(degT, 1)
            ch.link(nc.vector.tensor_reduce(dmax[:, 0:1], p_deg[:, :], AX, ALU.max))
            ch.link(nc.vector.tensor_scalar(nch_i[:, :], dmax[:, 0:1], float(SLOTS - 1), None, ALU.add))
            ch.link(nc.vector.tensor_single_scalar(nch_i[:, :], nch_i[:, :], 2, ALU.logical_shift_right))
            ch.link(nc.vector.tensor_scalar(dmax[:, 1:2], nch_i[:, :], 1.0, None, ALU.max))
            dve.sem_inc(nch_ready, 1)
            dve.wait_ge(start_ready, 1)
            ch.link(nc.vector.tensor_copy(dmax[:, 2:3], p_start[:, :]))
            dve.sem_inc(cols_ready, 1)
            dve.wait_ge(in_row, 1)
            ch.link(nc.vector.tensor_copy(row[:, 0:2, :], p_row[:, 0:2, :]))
            ch.add(nc.vector.tensor_scalar(row[:, 2, :], row[:, 0, :], float(WCH), None, ALU.min))
            ch.link(nc.vector.tensor_scalar(one[:, :], row[:, 0, :], float(WCH), None, ALU.is_le))
            ch.link(nc.vector.tensor_reduce(ctl[:, 2:3], one[:, :], AX, ALU.add))
            ch.link(nc.vector.tensor_scalar(ctl[:, 2:3], ctl[:, 2:3], float(BLOCKS - 1), None, ALU.min))
            ch.link(nc.vector.tensor_scalar(one[:, :], row[:, 0, :], float(-WCH), 0.0, ALU.add, ALU.max))
            ch.link(nc.vector.tensor_scalar(one[:, BLOCKS - 1:BLOCKS], one[:, BLOCKS - 1:BLOCKS], 1.0, None, ALU.max))
            ch.link(nc.vector.tensor_tensor_scan(row[:, 3, :], one[:, :], one[:, :], 0.0, ALU.add, ALU.max))
            ch.add(nc.vector.tensor_copy(ctl[:, 3:4], row[:, 3, BLOCKS - 1:BLOCKS]))
            ch.link(nc.vector.tensor_reduce(ctl[:, 4:5], row[:, 2, :], AX, ALU.add))
            ch.add(nc.vector.tensor_tensor(row[:, 3, :], row[:, 3, :], one[:, :], ALU.subtract))
            ch.add(nc.vector.memset(ctl[:, 5:8], 0.0))
            ch.link(nc.vector.tensor_tensor(ctl[:, 1:2], row[:, 0, BLOCKS - 1:BLOCKS], row[:, 1, BLOCKS - 1:BLOCKS],
                                            ALU.add))
            ch.link(nc.vector.tensor_scalar(ctl[:, 0:1], ctl[:, 1:2], float(RING - 1), None, ALU.add))
            ch.link(nc.vector.tensor_copy(k.ctl_i[:, :], ctl[:, :]))
            ch.add(nc.vector.tensor_single_scalar(k.ctl_i[:, 0:1], k.ctl_i[:, 0:1], 2, ALU.logical_shift_right))
            ch.link(nc.vector.tensor_copy(k.row_i[:, :, :], row[:, :, :]))
            dve.sem_inc(rows_ready, 1)
            ch.add(nc.vector.tensor_tensor(valid[:, :, :], bc(k.iota[:, 0:WIDE].unsqueeze(1), [P, BLOCKS, WIDE]),
                                           bc(k.deg_r[:, :].unsqueeze(2), [P, BLOCKS, WIDE]), ALU.is_lt))
            dve.wait_ge(wide_in, 16 * BLOCKS)
            ch.link(nc.vector.tensor_copy(code[:, :, :], wide[:, :, :]))
            v2 = lambda z: z[:, :, :].rearrange("p b w -> p (b w)")
            ch.link(nc.vector.scalar_tensor_tensor(out=v2(code), in0=v2(code), scalar=k.dummy4[:, :], in1=v2(valid),
                                                   op0=ALU.subtract, op1=ALU.mult))
            ch.link(nc.vector.tensor_scalar(v2(code_i), v2(code), k.dummy4[:, :], None, ALU.add))
            ch.add(nc.vector.tensor_copy(rows[:, :, :, SLOTS:2 * SLOTS],
                                         code_i[:, :, :].rearrange("p b (c s) -> p b c s", s=SLOTS)))
            ch.link(nc.vector.tensor_single_scalar(v2(wide), v2(code_i), 2, ALU.logical_shift_right))
            ch.add(nc.vector.tensor_copy(rows[:, :, :, 0:SLOTS],
                                         wide[:, :, :].rearrange("p b (c s) -> p b c s", s=SLOTS)))
            ch.add(nc.vector.tensor_copy(tail[:, 0, 0:SLOTS], bc(k.dummy[:, :], [P, SLOTS])))
            ch.add(nc.vector.tensor_copy(tail[:, 0, SLOTS:2 * SLOTS], bc(k.dummy4[:, :], [P, SLOTS])))
            ch.link(nc.vector.memset(tail[:, 0, CROW - 1:CROW], BLOCKS - 1))
            dve.sem_inc(chunk_rows, 1)
            dve.wait_ge(blocks_ready, 1)
            b0 = dve.value_load(k.ctl_i[0:1, 2:3], min_val=0, max_val=BLOCKS - 1)
            with dve.Fori(b0, BLOCKS) as b:
                n_c = dve.value_load(k.row_i[0:1, 0, bass.ds(b, 1)], min_val=1, max_val=CHUNKS)
                t0 = dve.value_load(k.row_i[0:1, 3, bass.ds(b, 1)], min_val=0, max_val=CHUNKS)
                dve.sem_clear(x_step)
                xs = Chain(dve, x_step)
                xs.link(nc.vector.memset(x_pos[:, :], float(WIDE)))
                with dve.Fori(WCH, n_c) as c:
                    dve.sem_clear(x_step)
                    xs = Chain(dve, x_step)
                    xs.link(nc.vector.tensor_tensor(x_first[:, :], first[:, bass.ds(b, 1)], x_pos[:, :], ALU.add))
                    nc.vector.tensor_scalar(x_first_i[:, :], x_first[:, :], float(E - 1), None, ALU.min)\
                        .then_inc(x_asked, 1)
                    xs.link(nc.vector.tensor_scalar(x_valid[:, :], k.iota[:, 0:SLOTS], x_pos[:, :], None, ALU.add))
                    xs.link(nc.vector.tensor_tensor(x_valid[:, :], x_valid[:, :],
                                                    bc(k.deg_r[:, bass.ds(b, 1)], [P, SLOTS]), ALU.is_lt))
                    xs.link(nc.vector.tensor_scalar(x_pos[:, :], x_pos[:, :], float(SLOTS), None, ALU.add))
                    dve.wait_ge(x_in, (t0 + (c - WCH)) * 16 + 16)
                    xs.link(nc.vector.tensor_copy(x_code[:, :], x_wide[:, 0:SLOTS]))
                    xs.link(nc.vector.scalar_tensor_tensor(out=x_code[:, :], in0=x_code[:, :], scalar=k.dummy4[:, :],
                                                           in1=x_valid[:, :], op0=ALU.subtract, op1=ALU.mult))
                    xs.link(nc.vector.tensor_scalar(x_code_i[:, :], x_code[:, :], k.dummy4[:, :], None, ALU.add))
                    xs.add(nc.vector.tensor_copy(x_row[:, 0, SLOTS:2 * SLOTS], x_code_i[:, :]))
                    xs.add(nc.vector.tensor_single_scalar(x_row[:, 0, 0:SLOTS], x_code_i[:, :], 2,
                                                          ALU.logical_shift_right))
                    xs.link(nc.vector.tensor_copy(x_row[:, 0, CROW - 1:CROW], rows[:, bass.ds(b, 1), 0, CROW - 1]))
                    dve.sem_inc(x_made, 1)
                    dve.wait_ge(x_out, (t0 + (c - WCH)) * 16 + 16)
                    dve.sem_inc(tick, 1)

        @block.sync
        def _(sp):
            sp.dma_start(info[:, :, :], k.info_tab[:, :].rearrange("(b p) c -> p b c", p=P)).then_inc(info_in, 16)
            sp.wait_ge(rows_ready, 1)
            n_w = sp.value_load(k.ctl_i[0:1, 4:5], min_val=1, max_val=BLOCKS * WCH)
            total = sp.value_load(k.ctl_i[0:1, 1:2], min_val=1, max_val=CHUNKS - 16)
            b0 = sp.value_load(k.ctl_i[0:1, 2:3], min_val=0, max_val=BLOCKS - 1)
            sp.wait_ge(chunk_rows, 1)
            sp.wait_ge(blocks_ready, 1)
            with sp.Fori(0, BLOCKS) as b:
                n_b = sp.value_load(k.row_i[0:1, 2, bass.ds(b, 1)], min_val=1, max_val=WCH)
                c_b = sp.value_load(k.row_i[0:1, 1, bass.ds(b, 1)], min_val=0, max_val=CHUNKS - 16)
                with sp.Fori(0, n_b) as c:
                    sp.dma_start(k.chunk_tab[bass.ds(chunk_at(nc, c_b + c), 1)].rearrange("a p c -> p a c"),
                                 rows[:, bass.ds(b, 1), bass.ds(c, 1), :].rearrange("p a b c -> p (a b) c"))\
                        .then_inc(written, 16)
            with sp.Fori(b0, BLOCKS) as b:
                n_c = sp.value_load(k.row_i[0:1, 0, bass.ds(b, 1)], min_val=1, max_val=CHUNKS)
                c_b = sp.value_load(k.row_i[0:1, 1, bass.ds(b, 1)], min_val=0, max_val=CHUNKS - 16)
                t0 = sp.value_load(k.row_i[0:1, 3, bass.ds(b, 1)], min_val=0, max_val=CHUNKS)
                with sp.Fori(WCH, n_c) as c:
                    sp.wait_ge(x_made, t0 + (c - WCH) + 1)
                    sp.sem_inc(tick, 1)
                    sp.dma_start(k.chunk_tab[bass.ds(chunk_at(nc, c_b + c), 1)].rearrange("a p c -> p a c"), x_row[:, :, :])\
                        .then_inc(x_out, 16)
                    sp.wait_ge(x_out, (t0 + (c - WCH)) * 16 + 16)
                    sp.sem_inc(tick, 1)
            for j in range(8):
                sp.dma_start(k.chunk_tab[bass.ds(chunk_at(nc, total + j), 1)].rearrange("a p c -> p a c"), tail[:, :, :])\
                    .then_inc(tail_out, 16)
            sp.wait_ge(written, n_w * 16)
            sp.sem_inc(tick, 1)
            sp.wait_ge(tail_out, 16 * 8)


def fetch_rows(nc, k, table, width, parts):
    with ExitStack() as ctx:
        m = Mem(nc, ctx)
        held = [m.sb(f"held{j}", [P, width]) for j in range(GROUP)]
        landed = [m.sem(f"landed{j}") for j in range(GROUP)]
        copied = [m.sem(f"copied{j}") for j in range(GROUP)]
        index = m.sb("index", [P, GROUP], I32)
        block = ctx.enter_context(nc.Block())

        @block.gpsimd
        def _(pool):
            for b in range(BLOCKS):
                j = b % GROUP
                if b >= GROUP:
                    pool.wait_ge(copied[j], (b // GROUP) * len(parts))
                pool.indirect_dma_start(held[j][:, :], None, table, at(k.node_r[:, b:b + 1])).then_inc(landed[j], 16)

        @block.vector
        def _(dve):
            with dve.Fori(0, TURNS) as t:
                for j in range(GROUP):
                    dve.wait_ge(landed[j], t * 16 + 16)
                    for buf, c0, n in parts:
                        nc.vector.tensor_copy(buf[:, bass.ds(t * GROUP + j, 1), 0:n],
                                              held[j][:, c0:c0 + n].unsqueeze(1)).then_inc(copied[j], 1)
            for j in range(GROUP):
                dve.wait_ge(copied[j], TURNS * len(parts))


def cosine_edges(nc, k, own_hn, own_v):
    W = D + 2
    with ExitStack() as ctx:
        m = Mem(nc, ctx)
        lists = [m.sb(f"list{s}", [P, PER_STAGE, SLOTS], I32) for s in range(STAGES)]
        meta = m.sb("meta", [1, RING], I32)
        got = m.sb("got", [P, RING, SLOTS, D])
        prod = m.sb("prod", [P, SLOTS, D])
        score = m.sb("score", [P, 2, SLOTS])
        ex = m.sb("ex", [P, 2, SLOTS])
        idx = m.sb("idx", [P, RING, SLOTS])
        vals = m.sb("vals", [P, 2, SLOTS, W])
        eq = m.sb("eq", [P, 2, SLOTS, P])
        firsts = m.sb("firsts", [P, SLOTS])
        moved = m.sb("moved", [P, SLOTS])
        to = m.sb("to", [P, RING, SLOTS], I32)
        out = m.sb("out_rows", [P, RING, SLOTS, W])
        weight = m.sb("weight", [P, 2])
        wexp = m.sb("wexp", [P, P])
        p_idx = [m.ps(f"p_idx{j}", [P, SLOTS, P]) for j in range(2)]
        p_sum = [m.ps(f"p_sum{j}", [P, SLOTS, 128]) for j in range(2)]
        list_in = [m.sem(f"list_in{s}") for s in range(STAGES)]
        list_used = [m.sem(f"list_used{s}") for s in range(STAGES)]
        meta_in, meta_used = m.sem("meta_in"), m.sem("meta_used")
        landed = [m.sem(f"landed{q}") for q in range(RING)]
        got_free = [m.sem(f"got_free{q}") for q in range(RING)]
        step, turn_step, pool_turn = m.sem("step"), m.sem("turn_step"), m.sem("pool_turn")
        idx_ready, spread, eq_ready = m.sem("idx_ready"), m.sem("spread"), m.sem("eq_ready")
        score_ready, ex_ready, vals_ready = m.sem("score_ready"), m.sem("ex_ready"), m.sem("vals_ready")
        summed, sum_copied, tick = m.sem("summed"), m.sem("sum_copied"), m.sem("tick")
        scattered = m.sem("scattered")
        rows_ready, to_ready = m.sem("rows_ready"), m.sem("to_ready")
        added = [m.sem(f"added{s}") for s in range(SLOTS)]
        block = ctx.enter_context(nc.Block())

        @block.sync
        def _(sp):
            n = sp.value_load(k.ctl_i[0:1, 0:1], min_val=1, max_val=CHUNKS // RING - 2)
            for s in range(STAGES):
                sp.dma_start(lists[s][:, :, :], k.chunk_tab[s * PER_STAGE:(s + 1) * PER_STAGE, :, 0:SLOTS]
                             .rearrange("a p c -> p a c")).then_inc(list_in[s], 16)
            sp.dma_start(meta[:, :], k.chunk_tab[0:RING, 0, CROW - 1:CROW].rearrange("a c -> c a"),
                         allow_slow_non_contiguous=True)\
                .then_inc(meta_in, 16)
            with sp.Fori(0, n) as i:
                for s in range(STAGES):
                    sp.wait_ge(list_used[s], (i + 1) * 2 * PER_STAGE)
                    sp.sem_inc(tick, 1)
                    sp.dma_start(lists[s][:, :, :], k.chunk_tab[bass.ds(i * RING + RING + s * PER_STAGE, PER_STAGE),
                                                                :, 0:SLOTS].rearrange("a p c -> p a c"))\
                        .then_inc(list_in[s], 16)
                    if s == 0:
                        sp.wait_ge(meta_used, i + 1)
                        sp.sem_inc(tick, 1)
                        sp.dma_start(meta[:, :], k.chunk_tab[bass.ds(i * RING + RING, RING), 0, CROW - 1:CROW]
                                     .rearrange("a c -> c a"), allow_slow_non_contiguous=True).then_inc(meta_in, 16)
            sp.wait_ge(list_in[0], n * 16 + 16)
            sp.wait_ge(list_in[1], n * 16 + 16)
            sp.wait_ge(meta_in, n * 16 + 16)
            sp.sem_inc(tick, 1)

        @block.gpsimd
        def _(pool):
            n = pool.value_load(k.ctl_i[0:1, 0:1], min_val=1, max_val=CHUNKS // RING - 2)

            def gather(q):
                s, c = divmod(q, PER_STAGE)
                for j in range(SLOTS):
                    pool.indirect_dma_start(got[:, q, j, :], None, k.hn_tab[:, :], at(lists[s][:, c, j:j + 1]))\
                        .then_inc(landed[q], 16)

            def scatter(q):
                for j in range(SLOTS):
                    pool.indirect_dma_start(k.sums[j][:, :], at(to[:, q, j:j + 1]), out[:, q, j, 0:D + 1], None,
                                            compute_op=ALU.add).then_inc(added[j], 16)

            pool.sem_inc(scattered, RING - 1)
            for j in range(SLOTS):
                pool.indirect_dma_start(k.sums[j][:, :], at(k.dummy_i[:, :]), k.zeros[:, 0:D + 1], None,
                                        compute_op=ALU.add).then_inc(added[j], 16)
            pool.wait_ge(list_in[0], 16)
            gather(0)
            gather(1)
            with pool.Fori(0, n) as i:
                def gather_turn(q, ahead):
                    if q % PER_STAGE == 0:
                        pool.wait_ge(list_in[q // PER_STAGE], (i + ahead + 1) * 16)
                    pool.wait_ge(got_free[q], i + ahead + 1)
                    pool.sem_inc(pool_turn, 1)
                    gather(q)

                def scatter_turn(q):
                    pool.wait_ge(to_ready, i * RING + q + 1)
                    pool.wait_ge(rows_ready, i * RING + q + 1)
                    for j in range(SLOTS):
                        pool.wait_ge(added[j], (i * RING + q + 1) * 16)
                    pool.sem_inc(scattered, 1)
                    scatter(q)

                gather_turn(2, 0)
                scatter_turn(0)
                gather_turn(3, 0)
                scatter_turn(1)
                gather_turn(0, 1)
                scatter_turn(2)
                gather_turn(1, 1)
                scatter_turn(3)
            for j in range(SLOTS):
                pool.wait_ge(added[j], n * (16 * RING) + 16)
            for q in range(2):
                pool.wait_ge(landed[q], n * 64 + 64)

        @block.vector
        def _(dve):
            n = dve.value_load(k.ctl_i[0:1, 0:1], min_val=1, max_val=CHUNKS // RING - 2)
            ch = Chain(dve, step)
            ch.link(nc.vector.memset(wexp[:, :], 0.5))
            ch.link(nc.vector.tensor_tensor_scan(wexp[:, :], wexp[:, :], wexp[:, :], 2.0 ** 61, ALU.mult, ALU.bypass))
            ch.link(nc.vector.tensor_tensor(eq[:, 0, 0, :], wexp[:, :], k.ident[:, :], ALU.mult))
            ch.link(nc.vector.tensor_reduce(weight[:, 0:1], eq[:, 0, 0, :], AX, ALU.add))
            ch.link(nc.vector.tensor_scalar(weight[:, 1:2], weight[:, 0:1], 2.0, None, ALU.mult))
            for z in range(2):
                ch.add(nc.vector.tensor_copy(vals[:, z, :, D + 1:D + 2], bc(weight[:, 0:1].unsqueeze(1), [P, SLOTS, 1])))
            ch.wait()
            for q in range(RING):
                dve.sem_inc(got_free[q], 1)
            with dve.Fori(0, n) as i:
                dve.sem_clear(turn_step)
                ts = Chain(dve, turn_step)
                dve.wait_ge(meta_in, i * 16 + 16)
                dve.sem_inc(tick, 1)
                _, b = nc.values_load_multi_w_load_instructions(meta[0:1, 0:RING], engines=DVE, min_val=0,
                                                                max_val=BLOCKS - 1)
                dve.sem_inc(meta_used, 1)

                def indices(s):
                    dve.wait_ge(list_in[s], i * 16 + 16)
                    nc.vector.tensor_copy(idx[:, s * PER_STAGE:(s + 1) * PER_STAGE, :], lists[s][:, :, :])\
                        .then_inc(idx_ready, 1)
                    dve.wait_ge(idx_ready, i * 2 + s + 1)
                    dve.sem_inc(list_used[s], PER_STAGE)

                def first_half(q):
                    dve.wait_ge(landed[q], i * 64 + 64)
                    dve.sem_inc(list_used[q // PER_STAGE], 1)
                    ts.add(nc.vector.tensor_tensor(prod[:, :, :], got[:, q, :, :],
                                                   bc(own_hn[:, bass.ds(b[q], 1), :], [P, SLOTS, D]), ALU.mult))
                    ts.wait()
                    dve.sem_inc(got_free[q], 1)
                    nc.vector.tensor_reduce(score[:, q % 2, :], prod[:, :, :], AX, ALU.add).then_inc(score_ready, 1)
                    dve.wait_ge(score_ready, i * RING + q + 1)
                    dve.wait_ge(spread, i * RING + q + 1)
                    nc.vector.tensor_tensor(eq[:, q % 2, :, :], p_idx[q % 2][:, :, :],
                                            bc(idx[:, q, :].unsqueeze(2), [P, SLOTS, P]), ALU.is_equal)\
                        .then_inc(eq_ready, 1)

                def second_half(q):
                    dve.wait_ge(ex_ready, i * RING + q + 1)
                    nc.vector.tensor_tensor(vals[:, q % 2, :, 0:D + 1],
                                            bc(own_v[:, bass.ds(b[q], 1), :], [P, SLOTS, D + 1]),
                                            bc(ex[:, q % 2, :].unsqueeze(2), [P, SLOTS, D + 1]), ALU.mult)\
                        .then_inc(vals_ready, 1)

                def third_half(q):
                    dve.wait_ge(rows_ready, i * RING + q + 1)
                    ts.link(nc.vector.tensor_scalar(firsts[:, :], out[:, q, :, D + 1], weight[:, 1:2], None,
                                                    ALU.is_le))
                    ts.link(nc.vector.scalar_tensor_tensor(out=moved[:, :], in0=idx[:, q, :], scalar=k.dummy[:, :],
                                                           in1=firsts[:, :], op0=ALU.subtract, op1=ALU.mult))
                    dve.wait_ge(scattered, i * RING + q + 1)
                    nc.vector.tensor_scalar(to[:, q, :], moved[:, :], k.dummy[:, :], None, ALU.add)\
                        .then_inc(to_ready, 1)
                    dve.wait_ge(to_ready, i * RING + q + 1)

                indices(0)
                first_half(0)
                first_half(1)
                second_half(0)
                indices(1)
                third_half(0)
                second_half(1)
                first_half(2)
                third_half(1)
                second_half(2)
                first_half(3)
                third_half(2)
                second_half(3)
                third_half(3)

        @block.scalar
        def _(act):
            n = act.value_load(k.ctl_i[0:1, 0:1], min_val=1, max_val=CHUNKS // RING - 2)
            act.sem_inc(sum_copied, 2)
            with act.Fori(0, n) as i:
                def exps(q):
                    act.wait_ge(score_ready, i * RING + q + 1)
                    nc.scalar.activation(ex[:, q % 2, :], score[:, q % 2, :], ACT.Exp).then_inc(ex_ready, 1)

                def rows(q):
                    act.wait_ge(summed, i * RING + q + 1)
                    act.wait_ge(scattered, i * RING + q + 1)
                    nc.scalar.activation(out[:, q, :, :], p_sum[q % 2][:, :, 0:W], ACT.Copy).then_inc(rows_ready, 1)
                    act.wait_ge(rows_ready, i * RING + q + 1)
                    act.sem_inc(sum_copied, 1)

                exps(0)
                exps(1)
                rows(0)
                exps(2)
                rows(1)
                exps(3)
                rows(2)
                rows(3)

        @block.tensor
        def _(pe):
            n = pe.value_load(k.ctl_i[0:1, 0:1], min_val=1, max_val=CHUNKS // RING - 2)
            with pe.Fori(0, n) as i:
                def spread_idx(q):
                    pe.wait_ge(idx_ready, i * 2 + q // PER_STAGE + 1)
                    if q >= 2:
                        pe.wait_ge(eq_ready, i * RING + q - 1)
                    for j in range(SLOTS):
                        last = nc.tensor.matmul(p_idx[q % 2][:, j, :], bc(idx[:, q, j:j + 1], [P, P]), k.ident[:, :],
                                                start=True, stop=True)
                    last.then_inc(spread, 1)

                def sum_equal(q):
                    pe.wait_ge(eq_ready, i * RING + q + 1)
                    pe.wait_ge(vals_ready, i * RING + q + 1)
                    pe.wait_ge(sum_copied, i * RING + q + 1)
                    for j in range(SLOTS):
                        last = nc.tensor.matmul(p_sum[q % 2][:, j, 0:W], eq[:, q % 2, j, :], vals[:, q % 2, j, :],
                                                start=True, stop=True)
                    last.then_inc(summed, 1)

                spread_idx(0)
                spread_idx(1)
                sum_equal(0)
                spread_idx(2)
                sum_equal(1)
                spread_idx(3)
                sum_equal(2)
                sum_equal(3)



def cosine_close(nc, k, a):
    with ExitStack() as ctx:
        m = Mem(nc, ctx)
        x = m.sb("x_close", [NP_, NC, D])
        part = [m.sb(f"part{j}", [NP_, NC, D + 1]) for j in range(SLOTS)]
        den = m.sb("den", [NP_, NC])
        inv = m.sb("inv", [NP_, NC])
        x_in, stored, step, done = m.sem("x_in"), m.sem("stored"), m.sem("step"), m.sem("done")
        part_in = [m.sem(f"part_in{j}") for j in range(SLOTS)]
        block = ctx.enter_context(nc.Block())

        @block.sync
        def _(sp):
            for j in range(SLOTS):
                sp.dma_start(part[j][:, :, :], k.sums[j][0:N, :].rearrange("(p c) d -> p c d", p=NP_))\
                    .then_inc(part_in[j], 16)
            sp.dma_start(x[:, :, :], a["x"].rearrange("(p c) d -> p c d", p=NP_)).then_inc(x_in, 16)
            sp.wait_ge(done, 1)
            sp.dma_start(k.x1_tab[0:N, :].rearrange("(p c) d -> p c d", p=NP_), x[:, :, :]).then_inc(stored, 16)
            sp.wait_ge(stored, 16)

        @block.vector
        def _(dve):
            ch = Chain(dve, step)
            dve.wait_ge(part_in[0], 16)
            for j in range(1, SLOTS):
                dve.wait_ge(part_in[j], 16)
                ch.link(nc.vector.tensor_tensor(part[0][:, :, :], part[0][:, :, :], part[j][:, :, :], ALU.add))
            ch.link(nc.vector.tensor_scalar(den[:, :], part[0][:, :, D], 1e-30, None, ALU.max))
            ch.link(nc.vector.reciprocal(inv[:, :], den[:, :]))
            ch.link(nc.vector.tensor_tensor(part[1][:, :, 0:D], part[0][:, :, 0:D],
                                            bc(inv[:, :].unsqueeze(2), [NP_, NC, D]), ALU.mult))
            dve.wait_ge(x_in, 16)
            nc.vector.tensor_tensor(x[:, :, :], x[:, :, :], part[1][:, :, 0:D], ALU.add).then_inc(done, 1)


def load_weights(nc, k, a):
    HW = H1 * (C1 + 1)
    with ExitStack() as ctx:
        m = Mem(nc, ctx)
        plain1, plain2 = m.sb("plain1", [P, D]), m.sb("plain2", [P, D])
        att = {n: m.sb("att_" + n, [P, D]) for n in ("a1_src", "a1_dst", "a2_src", "a2_dst")}
        prod = m.sb("prod", [P, D])
        wide = {n: m.sb("wide_" + n, [D, 2, 2, D]) for n in ("Wa_w", "lin_w")}
        p_w = [m.ps(f"p_w{j}", [P, D]) for j in range(4)]
        loaded, step, turned = m.sem("loaded"), m.sem("step"), m.sem("turned")
        block = ctx.enter_context(nc.Block())
        both = ((0, D), (D, P))

        @block.sync
        def _(sp):
            n = 0

            def load(dst, src):
                nonlocal n
                sp.dma_start(dst, src).then_inc(loaded, 16)
                n += 1

            for lo, hi in both:
                load(plain1[lo:hi, :], a["L1_gnn_W1"])
                load(plain2[lo:hi, :], a["L1_gnn_W2"])
                load(k.w_gcn[lo:hi, :], a["L2_gnn_W"])
                for t in range(TYPES):
                    load(k.w_src[lo:hi, 1 + t, :], a["L3_gnn_r"][t, D:2 * D, :])
                    load(k.w_own[lo:hi, 1 + t, :], a["L3_gnn_r"][t, 0:D, :])
            for name, tile in att.items():
                load(tile[:, :], a["L1_gnn_" + name].rearrange("h c -> (h c)").partition_broadcast(P))
            for name, tile in k.vec.items():
                load(tile[:, :], a[name].partition_broadcast(P))
            load(k.att_a[:, :], a["L3_gnn_a"][0, :].partition_broadcast(P))
            for name, tile in wide.items():
                for c in range(2):
                    load(tile[:, :, c, :], a["L3_gnn_" + name].rearrange("o (h i) -> o h i", h=2))
            k.weights_loaded = n * 16
            sp.wait_ge(loaded, k.weights_loaded)
            sp.sem_inc(turned, 1)

        @block.tensor
        def _(pe):
            pe.wait_ge(turned, 1)
            for j, name in enumerate(("Wa_w", "lin_w")):
                for h in range(2):
                    last = nc.tensor.transpose(p_w[2 * j + h][:, :], wide[name][:, h, :, :].rearrange("o c i -> o (c i)"),
                                               k.ident[0:D, 0:D])
            last.then_inc(turned, 1)

        @block.vector
        def _(dve):
            ch = Chain(dve, step)
            ch.link(nc.vector.memset(k.w_gat1[:, :], 0.0))
            ch.link(nc.vector.memset(k.w_gat2[:, :], 0.0))
            dve.wait_ge(turned, 1)
            for plain, w, heads, c, names in ((plain1, k.w_gat1, H1, C1, ("a1_src", "a1_dst")),
                                              (plain2, k.w_gat2, 1, D, ("a2_src", "a2_dst"))):
                ch.link(nc.vector.tensor_copy(w[:, 0:heads * (c + 1)].rearrange("p (h c) -> p h c", h=heads)[:, :, 0:c],
                                              plain[:, :].rearrange("p (h c) -> p h c", h=heads)))
                for n, name in enumerate(names):
                    at0 = heads * (c + 1) + n * heads
                    ch.link(nc.vector.tensor_tensor(prod[:, :], plain[:, :], att[name][:, :], ALU.mult))
                    ch.link(nc.vector.tensor_reduce(w[:, at0:at0 + heads],
                                                    prod[:, :].rearrange("p (h c) -> p h c", h=heads), AX, ALU.add))
            dve.wait_ge(turned, 2)
            for j, dst in enumerate((k.w_own[:, 0, :], k.w_src[:, 0, :], k.w_lin[:, 0, :], k.w_lin[:, 1, :])):
                ch.link(nc.vector.tensor_copy(dst, p_w[j][:, :]))
            ch.link(nc.vector.memset(k.att_a1[:, :], 1.0))
            ch.link(nc.vector.tensor_copy(k.att_a1[:, 0:D], k.att_a[:, :]))


def open_layer(nc, k, x, h):
    with ExitStack() as ctx:
        m = Mem(nc, ctx)
        sq, st = m.sb("sq", [P, BLOCKS, D]), m.sb("st", [P, 4, BLOCKS])
        step, var_ready, std_ready = m.sem("step"), m.sem("var_ready"), m.sem("std_ready")
        block = ctx.enter_context(nc.Block())

        @block.vector
        def _(dve):
            relu_norm(nc, dve, Chain(dve, step), x[:, :, :], h[:, :, :], sq[:, :, :], st, [P, BLOCKS, D],
                      var_ready, std_ready, 1)

        @block.scalar
        def _(act):
            act.wait_ge(var_ready, 1)
            nc.scalar.activation(st[:, 2, :], st[:, 1, :], ACT.Sqrt).then_inc(std_ready, 1)


def project(nc, k, h, weights, width, rows):
    with ExitStack() as ctx:
        m = Mem(nc, ctx)
        p_t = [m.ps(f"p_t{j}", [P, P]) for j in range(2)]
        p_o = [m.ps(f"p_o{j}", [P, 2, 512]) for j in range(2)]
        staged = m.sb("staged", [P, 2, 2, D])
        hT = m.sb("hT", [P, 2, P])
        tr, copied, made, stored = m.sem("transposed"), m.sem("copied"), m.sem("made"), m.sem("stored")
        stage_ready, stage_free, tick = m.sem("stage_ready"), m.sem("stage_free"), m.sem("tick")
        block = ctx.enter_context(nc.Block())
        PAIRS = BLOCKS // 2
        TP = 7

        @block.gpsimd
        def _(pool):
            with pool.Fori(0, PAIRS // TP) as t:
                for j in range(TP):
                    n = t * TP + j
                    pool.wait_ge(stage_free, n + (1 if j else 2))
                    pool.sem_inc(tick, 1)
                    nc.gpsimd.tensor_copy(staged[:, j % 2, :, :], h[:, bass.ds(n * 2, 2), :]).then_inc(stage_ready, 1)

        @block.tensor
        def _(pe):
            pe.sem_inc(stage_free, 2)
            with pe.Fori(0, PAIRS // TP) as t:
                for j in range(TP):
                    n, z = t * TP + j, j % 2
                    pe.wait_ge(stored, n + (1 if j else 2))
                    pe.wait_ge(stage_ready, n + 1)
                    nc.tensor.transpose(p_t[z][:, :], staged[:, z, :, :].rearrange("p b d -> p (b d)"),
                                        k.ident[:, :]).then_inc(tr, 1)
                    pe.wait_ge(copied, n + 1)
                    pe.sem_inc(stage_free, 1)
                    for y in range(2):
                        last = nc.tensor.matmul(p_o[z][:, y, 0:width], hT[y * D:(y + 1) * D, z, :],
                                                weights[y * D:(y + 1) * D, 0:width], start=True, stop=True)
                    last.then_inc(made, 1)

        @block.scalar
        def _(act):
            with act.Fori(0, PAIRS // TP) as t:
                for j in range(TP):
                    act.wait_ge(tr, t * TP + j + 1)
                    nc.scalar.activation(hT[:, j % 2, :], p_t[j % 2][:, :], ACT.Copy).then_inc(copied, 1)

        @block.vector
        def _(dve):
            dve.sem_inc(stored, 2)
            with dve.Fori(0, PAIRS // TP) as t:
                for j in range(TP):
                    n = t * TP + j
                    dve.wait_ge(made, n + 1)
                    nc.vector.tensor_copy(rows[:, bass.ds(n * 2, 2), 0:width], p_o[j % 2][:, :, 0:width])\
                        .then_inc(stored, 1)
            dve.wait_ge(stored, PAIRS + 2)


def spread_rows(nc, k, rows, width, table, dummy_col):
    with ExitStack() as ctx:
        m = Mem(nc, ctx)
        dummy = m.sb("dummy", [P, width])
        set_, out = m.sem("dummy_set"), m.sem("rows_out")
        spread = m.sem("spread")
        block = ctx.enter_context(nc.Block())

        @block.vector
        def _(dve):
            nc.vector.memset(dummy[:, :], 0.0).then_inc(set_, 1)
            dve.wait_ge(set_, 1)
            if dummy_col is not None:
                nc.vector.memset(dummy[:, dummy_col:width], MINUS).then_inc(set_, 1)
                dve.wait_ge(set_, 2)
            dve.sem_inc(set_, 1)

        @block.sync
        def _(sp):
            sp.wait_ge(set_, 2 if dummy_col is None else 3)
            sp.dma_start(table[NPAD:ROWS, :], dummy[:, :]).then_inc(out, 16)
            sp.wait_ge(out, 16)

        @block.gpsimd
        def _(pool):
            for b in range(BLOCKS):
                pool.indirect_dma_start(table, at(k.node_r[:, b:b + 1]), rows[:, b, 0:width], None)\
                    .then_inc(spread, 16)
            pool.wait_ge(spread, 16 * BLOCKS)


def ring_buffers(m, width):
    r = type("Ring", (), {})()
    r.lists = [m.sb(f"list{s}", [P, PER_STAGE, SLOTS], I32) for s in range(STAGES)]
    r.meta = m.sb("meta", [1, RING], I32)
    r.got = m.sb("got", [P, RING, SLOTS, width])
    r.list_in = [m.sem(f"list_in{s}") for s in range(STAGES)]
    r.list_used = [m.sem(f"list_used{s}") for s in range(STAGES)]
    r.meta_in, r.meta_used = m.sem("meta_in"), m.sem("meta_used")
    r.landed = [m.sem(f"landed{q}") for q in range(RING)]
    r.got_free = [m.sem(f"got_free{q}") for q in range(RING)]
    r.tick, r.turn_step = m.sem("tick"), m.sem("turn_step")
    return r


def turns(eng, k):
    return eng.value_load(k.ctl_i[0:1, 0:1], min_val=1, max_val=CHUNKS // RING - 2)


def load_lists(nc, sp, k, r, i, first, own=None):
    for s in range(STAGES):
        sp.wait_ge(r.list_used[s], (i + 1) * PER_STAGE)
        sp.sem_inc(r.tick, 1)
        sp.dma_start(r.lists[s][:, :, :], k.chunk_tab[bass.ds(i * RING + s * PER_STAGE, PER_STAGE), :,
                                                      first:first + SLOTS].rearrange("a p c -> p a c"))\
            .then_inc(r.list_in[s], 16)
    sp.wait_ge(r.meta_used, i + 1)
    sp.sem_inc(r.tick, 1)
    sp.dma_start(r.meta[:, :], k.chunk_tab[bass.ds(i * RING, RING), 0, CROW - 1:CROW].rearrange("a c -> c a"),
                 allow_slow_non_contiguous=True).then_inc(r.meta_in, 16)


def gather_all(nc, pool, k, r, table):
    n = turns(pool, k)
    with pool.Fori(0, n) as i:
        for q in range(RING):
            s, c = divmod(q, PER_STAGE)
            if c == 0:
                pool.wait_ge(r.list_in[s], i * 16 + 16)
            pool.wait_ge(r.got_free[q], i + 1)
            pool.sem_inc(r.tick, 1)
            for j in range(SLOTS):
                pool.indirect_dma_start(r.got[:, q, j, :], None, table, at(r.lists[s][:, c, j:j + 1]))\
                    .then_inc(r.landed[q], 16)


def ring_credits(dve, r, readers=1):
    for q in range(RING):
        dve.sem_inc(r.got_free[q], 1)
    for s in range(STAGES):
        dve.sem_inc(r.list_used[s], PER_STAGE)
    dve.sem_inc(r.meta_used, readers)


def turn_blocks(nc, eng, engines, r, i):
    eng.wait_ge(r.meta_in, i * 16 + 16)
    eng.sem_inc(r.tick, 1)
    _, b = nc.values_load_multi_w_load_instructions(r.meta[0:1, 0:RING], engines=engines, min_val=0,
                                                    max_val=BLOCKS - 1)
    eng.sem_inc(r.meta_used, 1)
    return b


def gat_edges(nc, k, heads, c, state, top, own_dst, table):
    HW = heads * (c + 1)
    W = HW + heads
    with ExitStack() as ctx:
        m = Mem(nc, ctx)
        r = ring_buffers(m, W)
        e = m.sb("e", [P, 2, SLOTS + 1, heads])
        p = m.sb("p", [P, 2, SLOTS + 1, heads])
        prod = m.sb("prod", [P, SLOTS, HW])
        part = m.sb("part", [P, HW])
        old = m.sb("old", [P, HW])
        e_ready, p_ready = m.sem("e_ready"), m.sem("p_ready")
        block = ctx.enter_context(nc.Block())

        @block.sync
        def _(sp):
            n = turns(sp, k)
            with sp.Fori(0, n) as i:
                load_lists(nc, sp, k, r, i, 0)

        @block.gpsimd
        def _(pool):
            gather_all(nc, pool, k, r, table)

        @block.vector
        def _(dve):
            n = turns(dve, k)
            ring_credits(dve, r)
            with dve.Fori(0, n) as i:
                dve.sem_clear(r.turn_step)
                ts = Chain(dve, r.turn_step)
                b = turn_blocks(nc, dve, DVE, r, i)

                def scores(q):
                    z = q % 2
                    dve.wait_ge(r.landed[q], i * 64 + 64)
                    dve.sem_inc(r.list_used[q // PER_STAGE], 1)
                    blk = bass.ds(b[q], 1)
                    ts.add(nc.vector.tensor_copy(e[:, z, SLOTS, :], top[:, blk, :].rearrange("p b h -> p (b h)")))
                    ts.link(nc.vector.tensor_tensor(e[:, z, 0:SLOTS, :], r.got[:, q, :, HW:W],
                                                    bc(own_dst[:, blk, :], [P, SLOTS, heads]), ALU.add))
                    ts.link(nc.vector.scalar_tensor_tensor(out=e[:, z, 0:SLOTS, :], in0=e[:, z, 0:SLOTS, :],
                                                           scalar=SLOPE, in1=e[:, z, 0:SLOTS, :],
                                                           op0=ALU.mult, op1=ALU.max))
                    ts.link(nc.vector.tensor_reduce(top[:, blk, :].rearrange("p b h -> p (b h)"),
                                                    e[:, z, :, :].rearrange("p s h -> p h s"), AX, ALU.max))
                    n_e = nc.vector.tensor_tensor(e[:, z, :, :], e[:, z, :, :],
                                                  bc(top[:, blk, :], [P, SLOTS + 1, heads]), ALU.subtract)
                    n_e.then_inc(e_ready, 1)

                def sums(q):
                    z = q % 2
                    blk = bass.ds(b[q], 1)
                    dve.wait_ge(p_ready, i * RING + q + 1)
                    hc = "p s (h c) -> p s h c"
                    ts.add(nc.vector.tensor_tensor(prod[:, :, :].rearrange(hc, h=heads),
                                                   r.got[:, q, :, 0:HW].rearrange(hc, h=heads),
                                                   bc(p[:, z, 0:SLOTS, :].unsqueeze(3), [P, SLOTS, heads, c + 1]),
                                                   ALU.mult))
                    ts.link(nc.vector.tensor_tensor(old[:, :].rearrange("p (h c) -> p h c", h=heads),
                                                    state[:, blk, 0:HW].rearrange("p b (h c) -> p (b h) c", h=heads),
                                                    bc(p[:, z, SLOTS, :].unsqueeze(2), [P, heads, c + 1]), ALU.mult))
                    dve.sem_inc(r.got_free[q], 1)
                    ts.link(nc.vector.tensor_reduce(part[:, :], prod[:, :, :].rearrange("p s f -> p f s"), AX, ALU.add))
                    ts.link(nc.vector.tensor_tensor(state[:, blk, 0:HW].rearrange("p b f -> p (b f)"), part[:, :],
                                                    old[:, :], ALU.add))

                scores(0)
                for q in range(1, RING):
                    scores(q)
                    sums(q - 1)
                sums(RING - 1)
                dve.wait_ge(e_ready, i * RING + RING)

        @block.scalar
        def _(act):
            n = turns(act, k)
            with act.Fori(0, n) as i:
                for q in range(RING):
                    act.wait_ge(e_ready, i * RING + q + 1)
                    nc.scalar.activation(p[:, q % 2, :, :], e[:, q % 2, :, :], ACT.Exp).then_inc(p_ready, 1)


def gcn_edges(nc, k, state, table):
    with ExitStack() as ctx:
        m = Mem(nc, ctx)
        r = ring_buffers(m, D)
        part = m.sb("part", [P, D])
        block = ctx.enter_context(nc.Block())

        @block.sync
        def _(sp):
            n = turns(sp, k)
            with sp.Fori(0, n) as i:
                load_lists(nc, sp, k, r, i, 0)

        @block.gpsimd
        def _(pool):
            gather_all(nc, pool, k, r, table)

        @block.vector
        def _(dve):
            n = turns(dve, k)
            ring_credits(dve, r)
            with dve.Fori(0, n) as i:
                dve.sem_clear(r.turn_step)
                ts = Chain(dve, r.turn_step)
                b = turn_blocks(nc, dve, DVE, r, i)
                for q in range(RING):
                    own = state[:, bass.ds(b[q], 1), :].rearrange("p b d -> p (b d)")
                    dve.wait_ge(r.landed[q], i * 64 + 64)
                    dve.sem_inc(r.list_used[q // PER_STAGE], 1)
                    ts.link(nc.vector.tensor_reduce(part[:, :], r.got[:, q, :, :].rearrange("p s f -> p f s"), AX,
                                                    ALU.add))
                    dve.sem_inc(r.got_free[q], 1)
                    ts.link(nc.vector.tensor_tensor(own, own, part[:, :], ALU.add))


def gat_open(nc, k, heads, c, state, own_dst, top):
    HW = heads * (c + 1)
    with ExitStack() as ctx:
        m = Mem(nc, ctx)
        step = m.sem("step")
        block = ctx.enter_context(nc.Block())

        @block.vector
        def _(dve):
            ch = Chain(dve, step)
            ones = state[:, :, 0:HW].rearrange("p b (h c) -> p b h c", h=heads)[:, :, :, c:c + 1]
            ch.add(nc.vector.memset(ones, 1.0))
            ch.add(nc.vector.tensor_copy(own_dst[:, :, :], state[:, :, HW + heads:HW + 2 * heads]))
            ch.link(nc.vector.tensor_tensor(top[:, :, :], state[:, :, HW:HW + heads],
                                            state[:, :, HW + heads:HW + 2 * heads], ALU.add))
            ch.link(nc.vector.scalar_tensor_tensor(out=top[:, :, :], in0=top[:, :, :], scalar=SLOPE,
                                                   in1=top[:, :, :], op0=ALU.mult, op1=ALU.max))


def gat_close(nc, k, heads, c, state, bias, gain, shift, y, x_add):
    HW = heads * (c + 1)
    with ExitStack() as ctx:
        m = Mem(nc, ctx)
        sq, ex = m.sb("sq", [P, BLOCKS, D]), m.sb("ex", [P, BLOCKS, D])
        st = m.sb("st", [P, 4, BLOCKS])
        den = m.sb("den", [P, 2, BLOCKS, heads])
        step, var_ready, std_ready = m.sem("step"), m.sem("var_ready"), m.sem("std_ready")
        low_ready, ex_ready = m.sem("low_ready"), m.sem("ex_ready")
        block = ctx.enter_context(nc.Block())
        full = [P, BLOCKS, D]

        @block.vector
        def _(dve):
            ch = Chain(dve, step)
            tt, ts = nc.vector.tensor_tensor, nc.vector.tensor_scalar
            cols = state[:, :, 0:HW].rearrange("p b (h c) -> p b h c", h=heads)
            wide = lambda j: bc(st[:, j, :].unsqueeze(2), full)
            vec = lambda t: bc(t[:, :].unsqueeze(1), full)
            Y, SQ = y[:, :, :], sq[:, :, :]
            ch.link(ts(den[:, 0, :, :], cols[:, :, :, c], SM_EPS, None, ALU.add))
            ch.link(nc.vector.reciprocal(den[:, 1, :, :], den[:, 0, :, :]))
            ch.link(tt(y[:, :, :].rearrange("p b (h c) -> p b h c", h=heads), cols[:, :, :, 0:c],
                       bc(den[:, 1, :, :].unsqueeze(3), [P, BLOCKS, heads, c]), ALU.mult))
            ch.link(tt(Y, Y, vec(bias), ALU.add))
            ch.link(nc.vector.tensor_reduce(st[:, 0, :], Y, AX, ALU.add))
            ch.link(ts(st[:, 3, :], st[:, 0, :], 1.0 / D, None, ALU.mult))
            ch.link(tt(Y, Y, wide(3), ALU.subtract))
            ch.link(tt(SQ, Y, Y, ALU.mult))
            ch.link(nc.vector.tensor_reduce(st[:, 0, :], SQ, AX, ALU.add))
            ts(st[:, 1, :], st[:, 0, :], 1.0 / D, LN_EPS, ALU.mult, ALU.add).then_inc(var_ready, 1)
            dve.wait_ge(std_ready, 1)
            ch.link(nc.vector.reciprocal(st[:, 3, :], st[:, 2, :]))
            ch.link(tt(Y, Y, wide(3), ALU.mult))
            ch.link(tt(Y, Y, vec(gain), ALU.mult))
            ch.link(tt(Y, Y, vec(shift), ALU.add))
            ts(SQ, Y, 0.0, None, ALU.min).then_inc(low_ready, 1)
            ch.link(ts(Y, Y, 0.0, -1.0, ALU.max, ALU.add))
            dve.wait_ge(ex_ready, 1)
            ch.link(tt(Y, Y, ex[:, :, :], ALU.add))
            if x_add is not None:
                ch.link(tt(x_add[:, :, :], x_add[:, :, :], Y, ALU.add))

        @block.scalar
        def _(act):
            act.wait_ge(var_ready, 1)
            nc.scalar.activation(st[:, 2, :], st[:, 1, :], ACT.Sqrt).then_inc(std_ready, 1)
            act.wait_ge(low_ready, 1)
            nc.scalar.activation(ex[:, :, :], sq[:, :, :], ACT.Exp).then_inc(ex_ready, 1)


def gcn_scale(nc, k, state, dis):
    with ExitStack() as ctx:
        m = Mem(nc, ctx)
        root = m.sb("root", [P, 2, BLOCKS])
        step, deg_ready, root_ready = m.sem("step"), m.sem("deg_ready"), m.sem("root_ready")
        block = ctx.enter_context(nc.Block())

        @block.vector
        def _(dve):
            ch = Chain(dve, step)
            nc.vector.tensor_scalar(root[:, 0, :], k.deg_r[:, :], 1.0, None, ALU.add).then_inc(deg_ready, 1)
            dve.wait_ge(root_ready, 1)
            ch.link(nc.vector.reciprocal(dis[:, :], root[:, 1, :]))
            ch.link(nc.vector.tensor_tensor(state[:, :, :], state[:, :, :],
                                            bc(dis[:, :].unsqueeze(2), [P, BLOCKS, D]), ALU.mult))

        @block.scalar
        def _(act):
            act.wait_ge(deg_ready, 1)
            nc.scalar.activation(root[:, 1, :], root[:, 0, :], ACT.Sqrt).then_inc(root_ready, 1)


def gcn_close(nc, k, state, dis, bias, x):
    with ExitStack() as ctx:
        m = Mem(nc, ctx)
        step = m.sem("step")
        block = ctx.enter_context(nc.Block())

        @block.vector
        def _(dve):
            ch = Chain(dve, step)
            S, full = state[:, :, :], [P, BLOCKS, D]
            ch.link(nc.vector.tensor_tensor(S, S, bc(dis[:, :].unsqueeze(2), full), ALU.mult))
            ch.link(nc.vector.tensor_tensor(S, S, bc(bias[:, :].unsqueeze(1), full), ALU.add))
            ch.link(nc.vector.scalar_tensor_tensor(out=x[:, :, :].rearrange("p b d -> p (b d)"),
                                                   in0=state[:, :, :].rearrange("p b d -> p (b d)"), scalar=0.0,
                                                   in1=x[:, :, :].rearrange("p b d -> p (b d)"),
                                                   op0=ALU.max, op1=ALU.add))


def rel_tables(nc, k, h):
    with ExitStack() as ctx:
        m = Mem(nc, ctx)
        p_t = [m.ps(f"p_t{j}", [P, P]) for j in range(2)]
        p_s = [m.ps(f"p_s{j}", [P, (1 + TYPES) * D]) for j in range(2)]
        p_w = [m.ps(f"p_w{j}", [P, (1 + TYPES) * D]) for j in range(2)]
        staged = m.sb("staged", [P, 2, 2, D])
        stage_ready = m.sem("stage_ready")
        hT = m.sb("hT", [P, 2, P])
        rows = [m.sb(f"rows{j}", [P, TYPES, RROW]) for j in range(GROUP)]
        own = [m.sb(f"own{j}", [P, OROW]) for j in range(GROUP)]
        dummy = m.sb("dummy", [P, TYPES, RROW])
        tr, copied, made_s, made_w = m.sem("tr"), m.sem("copied"), m.sem("made_s"), m.sem("made_w")
        src_done, own_done = m.sem("src_done"), m.sem("own_done")
        half_done = m.sem("half_done")
        spread = [m.sem(f"spread{j}") for j in range(GROUP)]
        own_out = [m.sem(f"own_out{j}") for j in range(GROUP)]
        set_, dummy_out, tick = m.sem("set"), m.sem("dummy_out"), m.sem("tick")
        rows_free, own_free = m.sem("rows_free"), m.sem("own_free")
        block = ctx.enter_context(nc.Block())

        @block.tensor
        def _(pe):
            pe.wait_ge(copied, 1)
            with pe.Fori(0, TURNS) as t:
                for j in range(GROUP):
                    n, z = t * GROUP + j, j % 2
                    if z == 0:
                        pe.wait_ge(stage_ready, t * (GROUP // 2) + j // 2 + 1)
                        nc.tensor.transpose(p_t[(j // 2) % 2][:, :], staged[:, (j // 2) % 2, :, :]
                                            .rearrange("p b d -> p (b d)"), k.ident[:, :]).then_inc(tr, 1)
                        pe.wait_ge(copied, t * (GROUP // 2) + j // 2 + 2)
                    lhsT = hT[z * D:(z + 1) * D, (j // 2) % 2, :]
                    pe.wait_ge(src_done, n + 1)
                    nc.tensor.matmul(p_s[z][:, :], lhsT, k.w_src[z * D:(z + 1) * D, :, :].rearrange("p t d -> p (t d)"),
                                     start=True, stop=True).then_inc(made_s, 1)
                    pe.wait_ge(own_done, n + 1)
                    nc.tensor.matmul(p_w[z][:, :], lhsT, k.w_own[z * D:(z + 1) * D, :, :].rearrange("p t d -> p (t d)"),
                                     start=True, stop=True).then_inc(made_w, 1)

        @block.scalar
        def _(act):
            act.sem_inc(copied, 1)
            act.sem_inc(src_done, 2)
            act.wait_ge(set_, GROUP + GROUP)
            with act.Fori(0, TURNS) as t:
                for j in range(GROUP):
                    n, z = t * GROUP + j, j % 2
                    if z == 0:
                        act.wait_ge(tr, t * (GROUP // 2) + j // 2 + 1)
                        nc.scalar.activation(hT[:, (j // 2) % 2, :], p_t[(j // 2) % 2][:, :], ACT.Copy)\
                            .then_inc(copied, 1)
                    act.wait_ge(made_s, n + 1)
                    act.wait_ge(rows_free, n + 1)
                    nc.scalar.activation(rows[j][:, :, 0:D], bc(p_s[z][:, 0:D].unsqueeze(1), [P, TYPES, D]), ACT.Copy)
                    nc.scalar.activation(rows[j][:, :, AW:AW + D],
                                         p_s[z][:, D:].rearrange("p (t d) -> p t d", t=TYPES), ACT.Copy)\
                        .then_inc(src_done, 1)

        @block.vector
        def _(dve):
            for j in range(GROUP):
                nc.vector.memset(rows[j][:, :, D:AW], 0.0).then_inc(set_, 1)
                nc.vector.memset(own[j][:, D:AW], 0.0).then_inc(set_, 1)
            nc.vector.memset(dummy[:, :, :], 0.0).then_inc(set_, 1)
            dve.wait_ge(set_, 2 * GROUP + 1)
            nc.vector.memset(dummy[:, :, D:AW], MINUS * 100).then_inc(set_, 1)
            dve.wait_ge(set_, 2 * GROUP + 2)
            dve.sem_inc(own_done, 2)
            with dve.Fori(0, TURNS) as t:
                for j in range(GROUP):
                    n, z = t * GROUP + j, j % 2
                    dve.wait_ge(rows_free, n + 1)
                    nc.vector.tensor_scalar(rows[j][:, :, AW + D:RROW], bc(h[:, bass.ds(n, 1), :], [P, TYPES, D]), 0.5,
                                            None, ALU.mult).then_inc(half_done, 1)
                    dve.wait_ge(own_free, n + 1)
                    dve.wait_ge(made_w, n + 1)
                    nc.vector.tensor_tensor(own[j][:, 0:D], p_w[z][:, 0:D], k.vec["L3_gnn_Wa_b"][:, :], ALU.add)
                    nc.vector.tensor_copy(own[j][:, AW:OROW], p_w[z][:, D:]).then_inc(own_done, 1)

        @block.gpsimd
        def _(pool):
            pool.sem_inc(rows_free, GROUP)

            def stage(pair):
                z = pair % (GROUP // 2) % 2
                if pair >= 2:
                    pool.wait_ge(tr, pair - (pair % (GROUP // 2) > 0))
                nc.gpsimd.tensor_copy(staged[:, z, :, :], h[:, 2 * pair:2 * pair + 2, :]).then_inc(stage_ready, 1)

            stage(0)
            for b in range(BLOCKS):
                if b % 2 == 0 and b + 2 < BLOCKS:
                    stage(b // 2 + 1)
                pool.wait_ge(src_done, b + 3)
                pool.wait_ge(half_done, b + 1)
                pool.indirect_dma_start(k.rel_tab[0:NPAD, :], at(k.node_r[:, b:b + 1]),
                                        rows[b % GROUP][:, :, :].rearrange("p t c -> p (t c)"), None)\
                    .then_inc(spread[b % GROUP], 16)
                if b >= 4:
                    c = b - 4
                    pool.wait_ge(spread[c % GROUP], 16 * (c // GROUP + 1))
                    pool.sem_inc(rows_free, 1)
            for j in range(GROUP):
                pool.wait_ge(spread[j], 16 * TURNS)

        @block.sync
        def _(sp):
            sp.wait_ge(set_, 2 * GROUP + 2)
            sp.dma_start(k.rel_tab[NPAD:ROWS, :], dummy[:, :, :].rearrange("p t c -> p (t c)")).then_inc(dummy_out, 16)
            sp.sem_inc(own_free, GROUP)
            with sp.Fori(0, TURNS) as t:
                for j in range(GROUP):
                    sp.wait_ge(own_done, t * GROUP + j + 3)
                    sp.sem_inc(tick, 1)
                    sp.dma_start(k.own_tab[bass.ds(t * GROUP + j, 1)].rearrange("a p c -> p (a c)"), own[j][:, :])\
                        .then_inc(own_out[j], 16)
                    if j % 2:
                        for c in (j - 1, j):
                            sp.wait_ge(own_out[c], t * 16 + 16)
                            sp.sem_inc(own_free, 1)
            sp.wait_ge(dummy_out, 16)


def rel_edges(nc, k, state, top):
    with ExitStack() as ctx:
        m = Mem(nc, ctx)
        r = ring_buffers(m, RROW)
        own = m.sb("own", [P, RING, OROW])
        typ_i, typ = m.sb("typ_i", [P, RING, SLOTS], I32), m.sb("typ", [P, RING, SLOTS])
        is_t = m.sb("is_t", [P, TYPES, RING, SLOTS])
        feat = m.sb("feat", [P, SLOTS, AW])
        e = m.sb("e", [P, 2, SLOTS + 1])
        p = m.sb("p", [P, 2, SLOTS + 1])
        gate = m.sb("gate", [P, 2, SLOTS, D])
        th = m.sb("th", [P, 2, SLOTS, D])
        msg = m.sb("msg", [P, SLOTS, D])
        part, old = m.sb("part", [P, AW]), m.sb("old", [P, AW])
        own_in = [m.sem(f"own_in{q}") for q in range(RING)]
        own_free = [m.sem(f"own_free{q}") for q in range(RING)]
        e_ready, p_ready, g_ready, t_ready = m.sem("e_ready"), m.sem("p_ready"), m.sem("g_ready"), m.sem("t_ready")
        block = ctx.enter_context(nc.Block())

        @block.sync
        def _(sp):
            n = turns(sp, k)
            with sp.Fori(0, n) as i:
                for s in range(STAGES):
                    sp.wait_ge(r.list_used[s], (i + 1) * PER_STAGE)
                    sp.sem_inc(r.tick, 1)
                    sp.dma_start(r.lists[s][:, :, :], k.chunk_tab[bass.ds(i * RING + s * PER_STAGE, PER_STAGE), :,
                                                                  SLOTS:2 * SLOTS].rearrange("a p c -> p a c"))\
                        .then_inc(r.list_in[s], 16)
                sp.wait_ge(r.meta_used, i * 2 + 2)
                sp.sem_inc(r.tick, 1)
                sp.dma_start(r.meta[:, :], k.chunk_tab[bass.ds(i * RING, RING), 0, CROW - 1:CROW]
                             .rearrange("a c -> c a"), allow_slow_non_contiguous=True).then_inc(r.meta_in, 16)
                b = turn_blocks(nc, sp, [mybir.EngineType.SP], r, i)
                for q in range(RING):
                    sp.wait_ge(own_free[q], i + 1)
                    sp.sem_inc(r.tick, 1)
                    sp.dma_start(own[:, q, :], k.own_tab[bass.ds(b[q], 1)].rearrange("a p c -> p (a c)"))\
                        .then_inc(own_in[q], 16)

        @block.gpsimd
        def _(pool):
            gather_all(nc, pool, k, r, k.rel_tab.rearrange("n (t c) -> (n t) c", t=TYPES))

        @block.vector
        def _(dve):
            n = turns(dve, k)
            ring_credits(dve, r, readers=2)
            for q in range(RING):
                dve.sem_inc(own_free[q], 1)
            with dve.Fori(0, n) as i:
                dve.sem_clear(r.turn_step)
                ts = Chain(dve, r.turn_step)
                b = turn_blocks(nc, dve, DVE, r, i)

                def types(s):
                    c0, c1 = s * PER_STAGE, (s + 1) * PER_STAGE
                    dve.wait_ge(r.list_in[s], i * 16 + 16)
                    ts.link(nc.vector.tensor_single_scalar(typ_i[:, c0:c1, :], r.lists[s][:, :, :], TYPES - 1,
                                                           ALU.bitwise_and))
                    ts.link(nc.vector.tensor_copy(typ[:, c0:c1, :], typ_i[:, c0:c1, :]))
                    for t in range(TYPES):
                        ts.add(nc.vector.tensor_scalar(is_t[:, t, c0:c1, :], typ[:, c0:c1, :], float(t), None,
                                                       ALU.is_equal))
                    ts.wait()

                def scores(q):
                    z, blk = q % 2, bass.ds(b[q], 1)
                    F = feat[:, :, :]
                    dve.wait_ge(r.landed[q], i * 64 + 64)
                    dve.sem_inc(r.list_used[q // PER_STAGE], 1)
                    dve.wait_ge(own_in[q], i * 16 + 16)
                    ts.add(nc.vector.tensor_copy(e[:, z, SLOTS:SLOTS + 1], top[:, blk]))
                    ts.link(nc.vector.tensor_tensor(F, r.got[:, q, :, 0:AW],
                                                    bc(own[:, q, 0:AW].unsqueeze(1), [P, SLOTS, AW]), ALU.add))
                    ts.link(nc.vector.scalar_tensor_tensor(out=F, in0=F, scalar=0.01, in1=F, op0=ALU.mult,
                                                           op1=ALU.max))
                    ts.link(nc.vector.tensor_tensor(F, F, bc(k.att_a1[:, :].unsqueeze(1), [P, SLOTS, AW]), ALU.mult))
                    ts.link(nc.vector.tensor_reduce(e[:, z, 0:SLOTS], F, AX, ALU.add))
                    ts.link(nc.vector.tensor_reduce(top[:, blk], e[:, z, :], AX, ALU.max))
                    nc.vector.tensor_tensor(e[:, z, :], e[:, z, :], bc(top[:, blk], [P, SLOTS + 1]), ALU.subtract)\
                        .then_inc(e_ready, 1)

                def gates(q):
                    z = q % 2
                    for t in range(TYPES):
                        for s in range(SLOTS):
                            before = r.got[:, q, s, AW:AW + D] if t == 0 else gate[:, z, s, :]
                            ins = nc.vector.scalar_tensor_tensor(
                                out=gate[:, z, s, :], in0=own[:, q, AW + t * D:AW + (t + 1) * D],
                                scalar=is_t[:, t, q, s:s + 1], in1=before, op0=ALU.mult, op1=ALU.add)
                            if t < TYPES - 1:
                                ts.add(ins)
                        if t < TYPES - 1:
                            ts.wait()
                    ins.then_inc(g_ready, 1)

                def sums(q):
                    z, blk = q % 2, bass.ds(b[q], 1)
                    dve.wait_ge(t_ready, i * RING + q + 1)
                    dve.sem_inc(own_free[q], 1)
                    ts.link(nc.vector.scalar_tensor_tensor(out=msg[:, :, :], in0=th[:, z, :, :], scalar=1.0,
                                                           in1=r.got[:, q, :, AW + D:RROW], op0=ALU.add, op1=ALU.mult))
                    dve.sem_inc(r.got_free[q], 1)
                    dve.wait_ge(p_ready, i * RING + q + 1)
                    ts.add(nc.vector.tensor_scalar(old[:, :], state[:, blk, :].rearrange("p b f -> p (b f)"),
                                                   p[:, z, SLOTS:SLOTS + 1], None, ALU.mult))
                    ts.add(nc.vector.tensor_reduce(part[:, D:AW], p[:, z, 0:SLOTS], AX, ALU.add))
                    ts.link(nc.vector.tensor_tensor(msg[:, :, :], msg[:, :, :],
                                                    bc(p[:, z, 0:SLOTS].unsqueeze(2), [P, SLOTS, D]), ALU.mult))
                    ts.link(nc.vector.tensor_reduce(part[:, 0:D], msg[:, :, :].rearrange("p s f -> p f s"), AX,
                                                    ALU.add))
                    ts.link(nc.vector.tensor_tensor(state[:, blk, :].rearrange("p b f -> p (b f)"), part[:, :],
                                                    old[:, :], ALU.add))

                for q in range(RING):
                    if q % PER_STAGE == 0:
                        types(q // PER_STAGE)
                    scores(q)
                    gates(q)
                    if q:
                        sums(q - 1)
                sums(RING - 1)

        @block.scalar
        def _(act):
            n = turns(act, k)
            with act.Fori(0, n) as i:
                for q in range(RING):
                    act.wait_ge(e_ready, i * RING + q + 1)
                    nc.scalar.activation(p[:, q % 2, :], e[:, q % 2, :], ACT.Exp).then_inc(p_ready, 1)
                    act.wait_ge(g_ready, i * RING + q + 1)
                    nc.scalar.activation(th[:, q % 2, :, :], gate[:, q % 2, :, :], ACT.Tanh, scale=0.5)\
                        .then_inc(t_ready, 1)


def rel_close(nc, k, h, state, x, out):
    with ExitStack() as ctx:
        m = Mem(nc, ctx)
        den, inv = m.sb("den", [P, BLOCKS]), m.sb("inv", [P, BLOCKS])
        hn = m.sb("hn", [P, BLOCKS, D])
        p_t = [m.ps(f"p_t{j}", [P, 2, P]) for j in range(2)]
        p_o = [m.ps(f"p_o{j}", [P, 2, 512]) for j in range(2)]
        staged = m.sb("staged", [P, 2, 2, 2, D])
        stage_ready = m.sem("stage_ready")
        hT = m.sb("hT", [P, 2, 2, P])
        lin = m.sb("lin", [P, 2, 2, D])
        step, hn_ready = m.sem("step"), m.sem("hn_ready")
        tr, copied, made, read, stored, spread = (m.sem("tr"), m.sem("copied"), m.sem("made"), m.sem("read"),
                                                  m.sem("stored"), m.sem("spread"))
        turn_step = m.sem("turn_step")
        block = ctx.enter_context(nc.Block())
        PAIRS, TP = BLOCKS // 2, 7

        @block.vector
        def _(dve):
            ch = Chain(dve, step)
            ch.link(nc.vector.tensor_scalar(den[:, :], state[:, :, D], 1e-30, None, ALU.max))
            ch.link(nc.vector.reciprocal(inv[:, :], den[:, :]))
            nc.vector.tensor_tensor(hn[:, :, :], state[:, :, 0:D], bc(inv[:, :].unsqueeze(2), [P, BLOCKS, D]),
                                    ALU.mult).then_inc(hn_ready, 1)
            dve.sem_inc(read, 2)
            with dve.Fori(0, PAIRS // TP) as t:
                dve.sem_clear(turn_step)
                ts = Chain(dve, turn_step)
                for j in range(TP):
                    n, z = t * TP + j, j % 2
                    L = lin[:, z, :, :].rearrange("p b d -> p (b d)")
                    xb = x[:, bass.ds(n * 2, 2), :].rearrange("p b d -> p (b d)")
                    dve.wait_ge(made, n + 1)
                    ts.link(nc.vector.tensor_tensor(lin[:, z, :, :], p_o[z][:, :, 0:D],
                                                    bc(k.vec["L3_gnn_lin_b"][:, :].unsqueeze(1), [P, 2, D]), ALU.add))
                    dve.sem_inc(read, 1)
                    ts.link(nc.vector.scalar_tensor_tensor(out=L, in0=L, scalar=0.01, in1=L, op0=ALU.mult,
                                                           op1=ALU.max))
                    nc.vector.tensor_tensor(xb, xb, L, ALU.add).then_inc(stored, 1)
                    dve.wait_ge(stored, n + 1)

        @block.tensor
        def _(pe):
            pe.wait_ge(hn_ready, 1)
            with pe.Fori(0, PAIRS // TP) as t:
                for j in range(TP):
                    n, z = t * TP + j, j % 2
                    pe.wait_ge(read, n + (1 if j else 2))
                    pe.wait_ge(stage_ready, n * 2 + 2)
                    for w in range(2):
                        last = nc.tensor.transpose(p_t[z][:, w, :], staged[:, z, w, :, :]
                                                   .rearrange("p b d -> p (b d)"), k.ident[:, :])
                    last.then_inc(tr, 1)
                    pe.wait_ge(copied, n + 1)
                    for y in range(2):
                        for w in range(2):
                            last = nc.tensor.matmul(p_o[z][:, y, 0:D], hT[y * D:(y + 1) * D, z, w, :],
                                                    k.w_lin[y * D:(y + 1) * D, w, :], start=(w == 0), stop=(w == 1))
                    last.then_inc(made, 1)

        @block.scalar
        def _(act):
            with act.Fori(0, PAIRS // TP) as t:
                for j in range(TP):
                    act.wait_ge(tr, t * TP + j + 1)
                    nc.scalar.activation(hT[:, j % 2, :, :], p_t[j % 2][:, :, :], ACT.Copy).then_inc(copied, 1)

        @block.gpsimd
        def _(pool):
            def stage(pair):
                z = pair % (GROUP // 2) % 2
                if pair >= 2:
                    pool.wait_ge(tr, pair - (pair % (GROUP // 2) > 0))
                for w, buf in enumerate((h, hn)):
                    nc.gpsimd.tensor_copy(staged[:, z, w, :, :], buf[:, 2 * pair:2 * pair + 2, :])\
                        .then_inc(stage_ready, 1)

            pool.wait_ge(hn_ready, 1)
            stage(0)
            for b in range(BLOCKS):
                if b % 2 == 0 and b + 2 < BLOCKS:
                    stage(b // 2 + 1)
                pool.wait_ge(stored, b // 2 + 1)
                pool.indirect_dma_start(out, at(k.node_r[:, b:b + 1]), x[:, b, :], None, bounds_check=N - 1,
                                        oob_is_err=False).then_inc(spread, 16)
            pool.wait_ge(spread, 16 * BLOCKS)


def gnn_program(nc, a, out):
    ctx = ExitStack()
    with ctx:
        k = type("Kept", (), {})()
        m = Mem(nc, ctx)
        k.ident, k.ones, k.before = m.sb("ident", [P, P]), m.sb("ones", [P, P]), m.sb("before", [P, P])
        k.zeros = m.sb("zeros", [P, 2 * D])
        k.iota_i, k.iota = m.sb("iota_i", [P, P], I32), m.sb("iota", [P, P])
        k.node_i = m.sb("node_i", [P, BLOCKS], I32)
        k.dummy_i, k.dummy, k.dummy4 = m.sb("dummy_i", [P, 1], I32), m.sb("dummy_row", [P, 1]), m.sb("dummy4", [P, 1])
        k.deg, k.deg_r = m.sb("deg", [P, BLOCKS]), m.sb("deg_r", [P, BLOCKS])
        k.node_r = m.sb("node_r", [P, BLOCKS], I32)
        k.ctl_i, k.row_i = m.sb("ctl_i", [1, 8], I32), m.sb("row_i", [1, 4, BLOCKS], I32)
        k.const_ready = m.sem("const_ready")

        def dram(name, shape, dt=F32):
            return nc.dram_tensor(name, shape, dt, kind="Internal").ap()

        k.codes = dram("codes", [E + WIDE], I32)
        k.runs = dram("runs", [E, WIDE], I32)
        k.info_tab = dram("info_tab", [NPAD, 4], I32)
        k.chunk_tab = dram("chunk_tab", [CHUNKS, P, CROW], I32)
        k.hn_tab, k.hh_tab = dram("hn_tab", [ROWS, D]), dram("hh_tab", [NPAD, 2 * D])
        k.sums = [dram(f"sums{j}", [ROWS, D + 1]) for j in range(SLOTS)]
        k.x1_tab = dram("x1_tab", [NPAD, D])
        k.gat1_tab = dram("gat1_tab", [ROWS, H1 * (C1 + 2)])
        k.gat2_tab = dram("gat2_tab", [ROWS, D + 2])
        k.gcn_tab = dram("gcn_tab", [ROWS, D])
        k.rel_tab = dram("rel_tab", [ROWS, TYPES * RROW])
        k.own_tab = dram("own_tab", [BLOCKS, P, OROW])
        k.w_gat1, k.w_gat2 = m.sb("w_gat1", [P, H1 * (C1 + 3)]), m.sb("w_gat2", [P, D + 3])
        k.w_gcn = m.sb("w_gcn", [P, D])
        k.w_src, k.w_own = m.sb("w_src", [P, 1 + TYPES, D]), m.sb("w_own", [P, 1 + TYPES, D])
        k.w_lin = m.sb("w_lin", [P, 2, D])
        k.att_a, k.att_a1 = m.sb("att_a", [P, D]), m.sb("att_a1", [P, AW])
        k.vec = {n: m.sb("v_" + n, [P, D]) for n in _VECS}
        constants(nc, k)
        count_and_open(nc, k, a)
        rank_nodes(nc, k)
        build_chunks(nc, k)
        layers(nc, k, a, out)


def clear(nc, pairs):
    with ExitStack() as ctx:
        cleared = Mem(nc, ctx).sem("cleared")
        block = ctx.enter_context(nc.Block())

        @block.vector
        def _(dve):
            for buf, value in pairs:
                nc.vector.memset(buf, value).then_inc(cleared, 1)
            dve.wait_ge(cleared, len(pairs))


def layers(nc, k, a, out):
    load_weights(nc, k, a)
    with ExitStack() as ctx:
        m = Mem(nc, ctx)
        own_hn, own_v = m.sb("own_hn", [P, BLOCKS, D]), m.sb("own_v", [P, BLOCKS, D + 1])
        fetch_rows(nc, k, k.hh_tab, 2 * D, [(own_v, 0, D), (own_hn, D, D)])
        clear(nc, [(own_v[:, :, D:D + 1], 1.0)])
        cosine_edges(nc, k, own_hn, own_v)
    cosine_close(nc, k, a)
    with ExitStack() as ctx:
        m = Mem(nc, ctx)
        x, h = m.sb("x", [P, BLOCKS, D]), m.sb("h", [P, BLOCKS, D])
        fetch_rows(nc, k, k.x1_tab, D, [(x, 0, D)])
        open_layer(nc, k, x, h)
        for step, heads, c, w, tab, res in ((1, H1, C1, k.w_gat1, k.gat1_tab, None), (2, 1, D, k.w_gat2, k.gat2_tab, x)):
            HW = heads * (c + 1)
            with ExitStack() as ctx2:
                m2 = Mem(nc, ctx2)
                state = m2.sb(f"state{step}", [P, BLOCKS, HW + 2 * heads])
                own_dst, top = m2.sb(f"own_dst{step}", [P, BLOCKS, heads]), m2.sb(f"top{step}", [P, BLOCKS, heads])
                project(nc, k, h, w, HW + 2 * heads, state)
                gat_open(nc, k, heads, c, state, own_dst, top)
                spread_rows(nc, k, state, HW + heads, tab, HW)
                gat_edges(nc, k, heads, c, state, top, own_dst, tab)
                v = lambda n: k.vec["L1_gnn_" + n]
                gat_close(nc, k, heads, c, state, v(f"b{step}"), v(f"ln{step}_g"), v(f"ln{step}_b"), h, res)
        open_layer(nc, k, x, h)
        with ExitStack() as ctx2:
            m2 = Mem(nc, ctx2)
            state, dis = m2.sb("gcn_state", [P, BLOCKS, D]), m2.sb("dis", [P, BLOCKS])
            project(nc, k, h, k.w_gcn, D, state)
            gcn_scale(nc, k, state, dis)
            spread_rows(nc, k, state, D, k.gcn_tab, None)
            gcn_edges(nc, k, state, k.gcn_tab)
            gcn_close(nc, k, state, dis, k.vec["L2_gnn_b"], x)
        open_layer(nc, k, x, h)
        rel_tables(nc, k, h)
        with ExitStack() as ctx2:
            m2 = Mem(nc, ctx2)
            state, top = m2.sb("rel_state", [P, BLOCKS, AW]), m2.sb("rel_top", [P, BLOCKS])
            clear(nc, [(state[:, :, :], 0.0), (top[:, :], MINUS)])
            rel_edges(nc, k, state, top)
            rel_close(nc, k, h, state, x, out)


_VECS = ["L1_gnn_b1", "L1_gnn_b2", "L1_gnn_ln1_g", "L1_gnn_ln1_b", "L1_gnn_ln2_g", "L1_gnn_ln2_b", "L2_gnn_b",
         "L3_gnn_Wa_b", "L3_gnn_lin_b"]
_INS = ["x", "src", "dst", "edge_type_4", "L1_gnn_W1", "L1_gnn_a1_src", "L1_gnn_a1_dst", "L1_gnn_W2",
        "L1_gnn_a2_src", "L1_gnn_a2_dst", "L2_gnn_W", "L3_gnn_r", "L3_gnn_a", "L3_gnn_Wa_w", "L3_gnn_lin_w"] + _VECS


def kernel(**inputs):
    import numpy as _np
    import concourse.bacc as _bacc
    from concourse import mybir as _mybir
    from concourse.bass_utils import run_bass_kernel_spmd as _run

    nc = _bacc.Bacc("TRN2", target_bir_lowering=False, num_devices=1)
    arrays, args = {}, {}
    for name in _INS:
        arr = _np.ascontiguousarray(inputs[name])
        arrays[f"in_{name}_dram"] = arr
        args[name] = nc.dram_tensor(f"in_{name}_dram", arr.shape, _mybir.dt.from_np(arr.dtype),
                                    kind="ExternalInput").ap()
    out = nc.dram_tensor("out_dram", (N, D), F32, kind="ExternalOutput").ap()
    gnn_program(nc, args, out)
    r = _run(nc, [arrays], core_ids=[0])
    return r.results[0]["out_dram"]
```

```python
from contextlib import ExitStack

import concourse.bass as bass
from concourse import mybir

F32, BF16, I32 = mybir.dt.float32, mybir.dt.bfloat16, mybir.dt.int32
ALU = mybir.AluOpType
ACT = mybir.ActivationFunctionType
AX = mybir.AxisListType.X
DVE = [mybir.EngineType.DVE]

N, E, D, TYPES = 12500, 212500, 64, 4
P = 128
BLOCKS = -(-N // P)
NPAD = BLOCKS * P
ROWS = NPAD + P
SLOTS = 4
RING = 4
STAGES = 2
PER_STAGE = RING // STAGES
WIDE = 32
WCH = WIDE // SLOTS
CHUNKS = E // SLOTS + BLOCKS + 16
CROW = 2 * SLOTS + 1
EP, EC = 125, 1700
NP_, NC = 125, 100
BINS = 64
H1, C1 = 4, 16
SLOPE, REL_SLOPE, LN_EPS, SM_EPS = 0.2, 0.01, 1e-5, 1e-16
MINUS = -1e30
GROUP = 14
TURNS = BLOCKS // GROUP
AW = D + 1
RROW = AW + 2 * D
OROW = AW + TYPES * D


class Mem:

    def __init__(self, nc, ctx):
        self.nc, self.ctx = nc, ctx
        self.stage = nc.next_id()
        self.sems = []
        ctx.callback(self.close)

    def close(self):
        if self.sems:
            self.nc.clear_and_free_semaphores(self.sems)
            self.nc.all_engine_barrier()

    def name(self, name):
        return f"{name}_{self.stage}"

    def sb(self, name, shape, dt=F32):
        return self.ctx.enter_context(self.nc.sbuf_tensor(self.name(name), shape, dt))

    def ps(self, name, shape, dt=F32):
        return self.ctx.enter_context(self.nc.psum_tensor(self.name(name), shape, dt))

    def sem(self, name):
        self.sems.append(self.nc.alloc_semaphore(self.name(name)))
        return self.sems[-1]


class Chain:

    def __init__(self, eng, sem):
        self.eng, self.sem, self.n = eng, sem, 0

    def add(self, ins):
        ins.then_inc(self.sem, 1)
        self.n += 1
        return self.n

    def wait(self, n=None):
        self.eng.wait_ge(self.sem, self.n if n is None else n)

    def link(self, ins):
        self.add(ins)
        self.wait()


def chunk_at(nc, c):
    return nc.s_assert_within(c, 0, CHUNKS - 1, skip_runtime_bounds_check_because="CHUNKS holds "
                              "the chunks of any degrees: their blocks' largest add up to at most E")




def at(ap, axis=0):
    return bass.IndirectOffsetOnAxis(ap=ap, axis=axis)


def bc(ap, shape):
    return ap.to_broadcast(shape)


def constants(nc, k):
    with ExitStack() as ctx:
        made = Mem(nc, ctx).sem("const_made")
        block = ctx.enter_context(nc.Block())

        @block.gpsimd
        def _(pool):
            ch = Chain(pool, made)
            ch.add(pool.memset(k.ident[:, :], 0.0))
            ch.add(pool.memset(k.ones[:, :], 1.0))
            ch.add(pool.memset(k.before[:, :], 1.0))
            ch.add(pool.memset(k.zeros[:, :], 0.0))
            ch.add(pool.iota(k.iota_i[:, :], [[1, P]], base=0, channel_multiplier=0))
            ch.add(pool.iota(k.node_i[:, :], [[P, BLOCKS]], base=0, channel_multiplier=1))
            ch.link(pool.iota(k.dummy_i[:, :], [[0, 1]], base=NPAD, channel_multiplier=1))
            ch.add(pool.affine_select(out=k.ident[:, :], in_=k.ident[:, :], compare_op=ALU.not_equal,
                                      fill=1.0, base=0, pattern=[[-1, P]], channel_multiplier=1))
            ch.link(pool.affine_select(out=k.before[:, :], in_=k.before[:, :], compare_op=ALU.is_gt,
                                       fill=0.0, base=0, pattern=[[1, P]], channel_multiplier=-1))

        @block.vector
        def _(dve):
            dve.wait_ge(made, 9)
            nc.vector.tensor_copy(k.iota[:, :], k.iota_i[:, :]).then_inc(k.const_ready, 1)
            nc.vector.tensor_copy(k.dummy[:, :], k.dummy_i[:, :]).then_inc(k.const_ready, 1)
            nc.vector.tensor_scalar(k.dummy4[:, :], k.dummy_i[:, :], 4.0, None, ALU.mult)\
                .then_inc(k.const_ready, 1)
            dve.wait_ge(k.const_ready, 3)


def count_and_open(nc, k, a):
    T = 17
    with ExitStack() as ctx:
        m = Mem(nc, ctx)
        src = m.sb("src_sb", [EP, EC], I32)
        dst = m.sb("dst_sb", [EP, EC], I32)
        typ = m.sb("typ_sb", [EP, EC], I32)
        lo_i = m.sb("lo_i", [EP, EC], I32)
        hi_i = m.sb("hi_i", [EP, EC], I32)
        lo = m.sb("lo", [EP, EC], BF16)
        hi = m.sb("hi", [EP, EC], BF16)
        iota_b = m.sb("iota_b", [P, P], BF16)
        hot = m.sb("hot", [EP, 2, T, P + BLOCKS], BF16)
        zero_b = m.sb("zero_b", [P, P + BLOCKS], BF16)
        xd = m.sb("xd", [NP_, NC, D])
        hh = m.sb("hh", [NP_, NC, 2 * D])
        sq = m.sb("sq", [NP_, NC, D])
        st = m.sb("st", [NP_, 4, NC])
        counts = m.ps("counts", [P, BLOCKS])
        dst_in, code_in, x_in = m.sem("dst_in"), m.sem("code_in"), m.sem("x_in")
        codes_out, runs_out, h_out = m.sem("codes_out"), m.sem("runs_out"), m.sem("h_out")
        step, codes_made = m.sem("dve_step"), m.sem("codes_made")
        hot_ready = [m.sem("hot_ready0"), m.sem("hot_ready1")]
        hot_used = [m.sem("hot_used0"), m.sem("hot_used1")]
        turn_step = m.sem("turn_step")
        counted = m.sem("counted")
        var_ready, std_ready = m.sem("var_ready"), m.sem("std_ready")
        h_made = m.sem("h_made")
        block = ctx.enter_context(nc.Block())

        @block.sync
        def _(sp):
            sp.dma_start(dst[:, :], a["dst"].rearrange("(p c) -> p c", p=EP)).then_inc(dst_in, 16)
            sp.dma_start(src[:, :], a["src"].rearrange("(p c) -> p c", p=EP)).then_inc(code_in, 16)
            sp.dma_start(typ[:, :], a["edge_type_4"].rearrange("(p c) -> p c", p=EP)).then_inc(code_in, 16)
            sp.dma_start(xd[:, :, :], a["x"].rearrange("(p c) d -> p c d", p=NP_)).then_inc(x_in, 16)
            sp.wait_ge(codes_made, 1)
            sp.dma_start(k.codes[0:E].rearrange("(p c) -> p c", p=EP), src[:, :]).then_inc(codes_out, 16)
            sp.dma_start(k.codes[E:E + WIDE].rearrange("(a c) -> a c", a=1),
                         k.zeros[0:1, 0:WIDE].bitcast(I32)).then_inc(codes_out, 16)
            sp.wait_ge(codes_out, 32)
            overlapped = bass.AP(k.codes.tensor, 0, [[1, E], [1, WIDE]])
            sp.dma_start(k.runs[:, :], overlapped).then_inc(runs_out, 16)
            sp.dma_start(k.hn_tab[N:N + P, :], k.zeros[:, 0:D]).then_inc(h_out, 16)
            sp.dma_start(k.hn_tab[N + P:ROWS, :], k.zeros[0:ROWS - N - P, 0:D]).then_inc(h_out, 16)
            sp.dma_start(k.hh_tab[N:NPAD, :], k.zeros[0:NPAD - N, 0:2 * D]).then_inc(h_out, 16)
            sp.dma_start(k.x1_tab[N:NPAD, :], k.zeros[0:NPAD - N, 0:D]).then_inc(h_out, 16)
            for s in range(SLOTS):
                sp.dma_start(k.sums[s].rearrange("(p c) d -> p c d", p=P),
                             bc(k.zeros[:, 0:D + 1].unsqueeze(1), [P, ROWS // P, D + 1])).then_inc(h_out, 16)
            sp.wait_ge(h_made, 1)
            sp.dma_start(k.hn_tab[0:N, :].rearrange("(p c) d -> p c d", p=NP_), sq[:, :, :]).then_inc(h_out, 16)
            sp.dma_start(k.hh_tab[0:N, :].rearrange("(p c) d -> p c d", p=NP_), hh[:, :, :]).then_inc(h_out, 16)
            sp.wait_ge(runs_out, 16)
            sp.wait_ge(h_out, 16 * (6 + SLOTS))

        @block.vector
        def _(dve):
            ch = Chain(dve, step)
            ch.add(nc.vector.tensor_copy(iota_b[:, :], k.iota[:, :]))
            ch.add(nc.vector.memset(zero_b[:, :], 0.0))
            dve.wait_ge(dst_in, 16)
            ch.add(nc.vector.tensor_single_scalar(lo_i[:, :], dst[:, :], P - 1, ALU.bitwise_and))
            ch.link(nc.vector.tensor_single_scalar(hi_i[:, :], dst[:, :], 7, ALU.logical_shift_right))
            ch.add(nc.vector.tensor_copy(lo[:, :], lo_i[:, :]))
            ch.add(nc.vector.tensor_copy(hi[:, :], hi_i[:, :]))
            dve.wait_ge(code_in, 32)
            nc.vector.scalar_tensor_tensor(out=src[:, :], in0=src[:, :], scalar=float(TYPES), in1=typ[:, :],
                                           op0=ALU.mult, op1=ALU.add).then_inc(codes_made, 1)
            ch.wait()
            dve.sem_inc(hot_used[0], 1)
            dve.sem_inc(hot_used[1], 1)
            with dve.Fori(0, EC // (2 * T)) as i:
                for h in range(2):
                    cols = bass.ds(i * (2 * T) + h * T, T)
                    dve.wait_ge(hot_used[h], i + 1)
                    nc.vector.tensor_tensor(hot[:, h, :, 0:P], bc(lo[:, cols].unsqueeze(2), [EP, T, P]),
                                            bc(iota_b[0:EP, :].unsqueeze(1), [EP, T, P]), ALU.is_equal)\
                        .then_inc(hot_ready[h], 1)
                    nc.vector.tensor_tensor(hot[:, h, :, P:P + BLOCKS],
                                            bc(hi[:, cols].unsqueeze(2), [EP, T, BLOCKS]),
                                            bc(iota_b[0:EP, 0:BLOCKS].unsqueeze(1), [EP, T, BLOCKS]),
                                            ALU.is_equal).then_inc(hot_ready[h], 1)
            dve.wait_ge(counted, 1)
            ch.link(nc.vector.tensor_copy(k.deg[:, :], counts[:, :]))
            dve.wait_ge(x_in, 16)
            h = hh[:, :, 0:D]
            relu_norm(nc, dve, ch, xd[:, :, :], h, sq[:, :, :], st, [NP_, NC, D], var_ready, std_ready, 1)
            ch.link(nc.vector.tensor_tensor(sq[:, :, :], h, h, ALU.mult))
            ch.link(nc.vector.tensor_reduce(st[:, 0, :], sq[:, :, :], AX, ALU.add))
            nc.vector.tensor_copy(st[:, 1, :], st[:, 0, :]).then_inc(var_ready, 1)
            dve.wait_ge(std_ready, 2)
            ch.link(nc.vector.tensor_scalar(st[:, 0, :], st[:, 2, :], 1e-12, None, ALU.max))
            ch.link(nc.vector.reciprocal(st[:, 3, :], st[:, 0, :]))
            ch.link(nc.vector.tensor_tensor(hh[:, :, D:2 * D], h, bc(st[:, 3, :].unsqueeze(2), [NP_, NC, D]),
                                            ALU.mult))
            nc.vector.tensor_copy(sq[:, :, :], hh[:, :, D:2 * D]).then_inc(h_made, 1)
            dve.wait_ge(h_made, 1)

        @block.scalar
        def _(act):
            for n in range(2):
                act.wait_ge(var_ready, n + 1)
                nc.scalar.activation(st[:, 2, :], st[:, 1, :], ACT.Sqrt).then_inc(std_ready, 1)

        @block.tensor
        def _(pe):
            pe.wait_ge(step, 2)
            nc.tensor.matmul(counts[:, :], zero_b[0:EP, 0:P], zero_b[0:EP, P:P + BLOCKS], start=True, stop=False,
                             skip_group_check=True)
            with pe.Fori(0, EC // (2 * T)) as i:
                for h in range(2):
                    pe.wait_ge(hot_ready[h], i * 2 + 2)
                    for t in range(T):
                        last = nc.tensor.matmul(counts[:, :], hot[:, h, t, 0:P], hot[:, h, t, P:P + BLOCKS],
                                                start=False, stop=False, skip_group_check=True)
                    last.then_inc(hot_used[h], 1)
            nc.tensor.matmul(counts[:, :], zero_b[0:EP, 0:P], zero_b[0:EP, P:P + BLOCKS], start=False, stop=True,
                             skip_group_check=True).then_inc(counted, 1)


def relu_norm(nc, dve, ch, x, h, sq, st, shape, var_ready, std_ready, n):
    wide = lambda j: bc(st[:, j, :].unsqueeze(2), shape)
    ch.link(nc.vector.tensor_reduce(st[:, 0, :], x, AX, ALU.add))
    ch.link(nc.vector.tensor_scalar(st[:, 3, :], st[:, 0, :], 1.0 / D, None, ALU.mult))
    ch.link(nc.vector.tensor_tensor(h, x, wide(3), ALU.subtract))
    ch.link(nc.vector.tensor_tensor(sq, h, h, ALU.mult))
    ch.link(nc.vector.tensor_reduce(st[:, 0, :], sq, AX, ALU.add))
    nc.vector.tensor_scalar(st[:, 1, :], st[:, 0, :], 1.0 / D, LN_EPS, ALU.mult, ALU.add).then_inc(var_ready, 1)
    dve.wait_ge(std_ready, n)
    ch.link(nc.vector.reciprocal(st[:, 3, :], st[:, 2, :]))
    ch.link(nc.vector.tensor_scalar(sq, h, 0.0, None, ALU.max))
    ch.link(nc.vector.tensor_tensor(h, sq, wide(3), ALU.mult))


def rank_nodes(nc, k):
    with ExitStack() as ctx:
        m = Mem(nc, ctx)
        tot = m.sb("tot", [P, BLOCKS])
        incl = m.sb("incl", [P, BLOCKS])
        binned = m.sb("binned", [P, BLOCKS])
        same = m.sb("same", [P, BINS, BLOCKS])
        upto = m.sb("upto", [P, BINS, BLOCKS])
        cnt = m.sb("cnt", [P, BINS])
        cum = m.sb("cum", [P, BINS])
        btot = m.sb("btot", [P, BINS])
        off = m.sb("off", [P, BINS])
        rank = m.sb("rank", [P, BLOCKS])
        rank_i = m.sb("rank_i", [P, BLOCKS], I32)
        info = m.sb("info", [P, BLOCKS, 4], I32)
        p_tot = m.ps("p_tot", [P, BLOCKS])
        p_pre = m.ps("p_pre", [P, BLOCKS])
        p_btot = m.ps("p_btot", [P, BINS])
        p_bpre = m.ps("p_bpre", [P, BINS])
        step, summed, cnt_ready, bsummed = m.sem("step"), m.sem("summed"), m.sem("cnt_ready"), m.sem("bsummed")
        ranked, scattered = m.sem("ranked"), m.sem("scattered")
        block = ctx.enter_context(nc.Block())

        @block.tensor
        def _(pe):
            nc.tensor.matmul(p_tot[:, :], k.ones[:, :], k.deg[:, :], start=True, stop=True)
            nc.tensor.matmul(p_pre[:, :], k.before[:, :], k.deg[:, :], start=True, stop=True).then_inc(summed, 1)
            pe.wait_ge(cnt_ready, 1)
            nc.tensor.matmul(p_btot[:, :], k.ones[:, :], cnt[:, :], start=True, stop=True)
            nc.tensor.matmul(p_bpre[:, :], k.before[:, :], cnt[:, :], start=True, stop=True).then_inc(bsummed, 1)

        @block.vector
        def _(dve):
            ch = Chain(dve, step)
            ch.link(nc.vector.tensor_scalar(binned[:, :], k.deg[:, :], float(BINS - 1), None, ALU.min))
            ch.link(nc.vector.tensor_tensor(same[:, :, :], bc(binned[:, :].unsqueeze(1), [P, BINS, BLOCKS]),
                                            bc(k.iota[:, 0:BINS].unsqueeze(2), [P, BINS, BLOCKS]), ALU.is_equal))
            ch.link(nc.vector.tensor_reduce(cnt[:, :], same[:, :, :], AX, ALU.add))
            dve.sem_inc(cnt_ready, 1)
            flat = same[:, :, :].rearrange("p v j -> p (v j)")
            ch.add(nc.vector.tensor_tensor_scan(upto[:, :, :].rearrange("p v j -> p (v j)"), flat, flat, 0.0,
                                                ALU.add, ALU.max))
            ch.link(nc.vector.tensor_tensor_scan(cum[:, :], cnt[:, :], cnt[:, :], 0.0, ALU.add, ALU.max))
            ch.link(nc.vector.tensor_tensor(off[:, :], cnt[:, :], cum[:, :], ALU.subtract))
            dve.wait_ge(bsummed, 1)
            ch.link(nc.vector.tensor_copy(btot[:, :], p_btot[:, :]))
            ch.link(nc.vector.tensor_tensor_scan(cum[:, :], btot[:, :], btot[:, :], 0.0, ALU.add, ALU.max))
            ch.link(nc.vector.tensor_tensor(cum[:, :], cum[:, :], btot[:, :], ALU.subtract))
            ch.link(nc.vector.tensor_tensor(off[:, :], off[:, :], cum[:, :], ALU.add))
            ch.link(nc.vector.tensor_tensor(off[:, :], off[:, :], p_bpre[:, :], ALU.add))
            ch.link(nc.vector.tensor_tensor(upto[:, :, :], upto[:, :, :],
                                            bc(off[:, :].unsqueeze(2), [P, BINS, BLOCKS]), ALU.add))
            ch.link(nc.vector.tensor_tensor(upto[:, :, :], upto[:, :, :], same[:, :, :], ALU.mult))
            ch.link(nc.vector.tensor_reduce(rank[:, :], upto[:, :, :].rearrange("p v j -> p j v"), AX, ALU.add))
            ch.link(nc.vector.tensor_scalar(rank_i[:, :], rank[:, :], -1.0, None, ALU.add))
            dve.wait_ge(summed, 1)
            ch.link(nc.vector.tensor_copy(tot[:, :], p_tot[:, :]))
            ch.link(nc.vector.tensor_tensor_scan(incl[:, :], tot[:, :], tot[:, :], 0.0, ALU.add, ALU.max))
            ch.link(nc.vector.tensor_tensor(incl[:, :], incl[:, :], tot[:, :], ALU.subtract))
            ch.add(nc.vector.tensor_tensor(info[:, :, 1], incl[:, :], p_pre[:, :], ALU.add))
            ch.add(nc.vector.tensor_copy(info[:, :, 0], k.node_i[:, :]))
            ch.add(nc.vector.tensor_copy(info[:, :, 2], k.deg[:, :]))
            ch.link(nc.vector.memset(info[:, :, 3], 0))
            dve.sem_inc(ranked, 1)

        @block.gpsimd
        def _(pool):
            pool.wait_ge(ranked, 1)
            for j in range(BLOCKS):
                pool.indirect_dma_start(k.info_tab[:, :], at(rank_i[:, j:j + 1]), info[:, j, :], None)\
                    .then_inc(scattered, 16)
            pool.wait_ge(scattered, 16 * BLOCKS)


def build_chunks(nc, k):
    with ExitStack() as ctx:
        m = Mem(nc, ctx)
        info = m.sb("info_r", [P, BLOCKS, 4], I32)
        first = m.sb("first", [P, BLOCKS])
        first_i = m.sb("first_i", [P, BLOCKS], I32)
        wide = m.sb("wide", [P, BLOCKS, WIDE], I32)
        valid = m.sb("valid", [P, BLOCKS, WIDE])
        code = m.sb("code", [P, BLOCKS, WIDE])
        code_i = m.sb("code_i", [P, BLOCKS, WIDE], I32)
        rows = m.sb("rows", [P, BLOCKS, WCH, CROW], I32)
        tail = m.sb("tail", [P, 1, CROW], I32)
        dmax = m.sb("dmax", [BLOCKS, 4])
        nch_i = m.sb("nch_i", [BLOCKS, 1], I32)
        row = m.sb("row", [1, 4, BLOCKS])
        one = m.sb("one", [1, BLOCKS])
        ctl = m.sb("ctl", [1, 8])
        x_first = m.sb("x_first", [P, 1])
        x_first_i = m.sb("x_first_i", [P, 1], I32)
        x_wide = m.sb("x_wide", [P, WIDE], I32)
        x_valid = m.sb("x_valid", [P, SLOTS])
        x_code = m.sb("x_code", [P, SLOTS])
        x_code_i = m.sb("x_code_i", [P, SLOTS], I32)
        x_pos = m.sb("x_pos", [P, 1])
        x_row = m.sb("x_row", [P, 1, CROW], I32)
        p_deg = m.ps("p_deg", [BLOCKS, P])
        p_start = m.ps("p_start", [BLOCKS, 1])
        p_row = m.ps("p_row", [1, 4, BLOCKS])
        info_in, step, deg_ready, degT = m.sem("info_in"), m.sem("step"), m.sem("deg_ready"), m.sem("degT")
        nch_ready, start_ready, cols_ready, rows_ready = (m.sem("nch_ready"), m.sem("start_ready"),
                                                          m.sem("cols_ready"), m.sem("rows_ready"))
        first_ready, wide_in, blocks_ready = m.sem("first_ready"), m.sem("wide_in"), m.sem("blocks_ready")
        chunk_rows, written = m.sem("chunk_rows"), m.sem("written")
        x_asked, x_in, x_made, x_out, x_turn = (m.sem("x_asked"), m.sem("x_in"), m.sem("x_made"), m.sem("x_out"),
                                                m.sem("x_turn"))
        tail_out, in_row, x_step, tick = m.sem("tail_out"), m.sem("in_row"), m.sem("x_step"), m.sem("tick")
        block = ctx.enter_context(nc.Block())

        @block.gpsimd
        def _(pool):
            pool.iota(rows[:, :, :, CROW - 1], [[1, BLOCKS], [0, WCH]], base=0, channel_multiplier=0)\
                .then_inc(blocks_ready, 1)
            pool.wait_ge(first_ready, 1)
            for b in range(BLOCKS):
                pool.indirect_dma_start(wide[:, b, :], None, k.runs[:, :], at(first_i[:, b:b + 1])).then_inc(wide_in, 16)
            pool.wait_ge(rows_ready, 1)
            n_x = pool.value_load(k.ctl_i[0:1, 3:4], min_val=1, max_val=CHUNKS)
            with pool.Fori(0, n_x) as t:
                pool.wait_ge(x_asked, t + 1)
                pool.sem_inc(x_turn, 1)
                pool.indirect_dma_start(x_wide[:, :], None, k.runs[:, :], at(x_first_i[:, :])).then_inc(x_in, 16)

        @block.tensor
        def _(pe):
            pe.wait_ge(deg_ready, 1)
            nc.tensor.transpose(p_deg[:, :], k.deg_r[:, :], k.ident[:, :]).then_inc(degT, 1)
            pe.wait_ge(nch_ready, 1)
            nc.tensor.matmul(p_start[:, :], k.before[0:BLOCKS, 0:BLOCKS], dmax[:, 1:2], start=True, stop=True)\
                .then_inc(start_ready, 1)
            pe.wait_ge(cols_ready, 1)
            for j in range(2):
                last = nc.tensor.matmul(p_row[:, j, :], dmax[:, 1 + j:2 + j], k.ident[0:BLOCKS, 0:BLOCKS],
                                        start=True, stop=True)
            last.then_inc(in_row, 1)

        @block.vector
        def _(dve):
            ch = Chain(dve, step)
            dve.wait_ge(info_in, 16)
            ch.add(nc.vector.tensor_copy(k.node_r[:, :], info[:, :, 0]))
            ch.add(nc.vector.tensor_copy(first[:, :], info[:, :, 1]))
            ch.add(nc.vector.memset(tail[:, :, :], 0))
            ch.link(nc.vector.tensor_copy(k.deg_r[:, :], info[:, :, 2]))
            dve.sem_inc(deg_ready, 1)
            nc.vector.tensor_scalar(first_i[:, :], first[:, :], float(E - 1), None, ALU.min).then_inc(first_ready, 1)
            dve.wait_ge(degT, 1)
            ch.link(nc.vector.tensor_reduce(dmax[:, 0:1], p_deg[:, :], AX, ALU.max))
            ch.link(nc.vector.tensor_scalar(nch_i[:, :], dmax[:, 0:1], float(SLOTS - 1), None, ALU.add))
            ch.link(nc.vector.tensor_single_scalar(nch_i[:, :], nch_i[:, :], 2, ALU.logical_shift_right))
            ch.link(nc.vector.tensor_scalar(dmax[:, 1:2], nch_i[:, :], 1.0, None, ALU.max))
            dve.sem_inc(nch_ready, 1)
            dve.wait_ge(start_ready, 1)
            ch.link(nc.vector.tensor_copy(dmax[:, 2:3], p_start[:, :]))
            dve.sem_inc(cols_ready, 1)
            dve.wait_ge(in_row, 1)
            ch.link(nc.vector.tensor_copy(row[:, 0:2, :], p_row[:, 0:2, :]))
            ch.add(nc.vector.tensor_scalar(row[:, 2, :], row[:, 0, :], float(WCH), None, ALU.min))
            ch.link(nc.vector.tensor_scalar(one[:, :], row[:, 0, :], float(WCH), None, ALU.is_le))
            ch.link(nc.vector.tensor_reduce(ctl[:, 2:3], one[:, :], AX, ALU.add))
            ch.link(nc.vector.tensor_scalar(ctl[:, 2:3], ctl[:, 2:3], float(BLOCKS - 1), None, ALU.min))
            ch.link(nc.vector.tensor_scalar(one[:, :], row[:, 0, :], float(-WCH), 0.0, ALU.add, ALU.max))
            ch.link(nc.vector.tensor_scalar(one[:, BLOCKS - 1:BLOCKS], one[:, BLOCKS - 1:BLOCKS], 1.0, None, ALU.max))
            ch.link(nc.vector.tensor_tensor_scan(row[:, 3, :], one[:, :], one[:, :], 0.0, ALU.add, ALU.max))
            ch.add(nc.vector.tensor_copy(ctl[:, 3:4], row[:, 3, BLOCKS - 1:BLOCKS]))
            ch.link(nc.vector.tensor_reduce(ctl[:, 4:5], row[:, 2, :], AX, ALU.add))
            ch.add(nc.vector.tensor_tensor(row[:, 3, :], row[:, 3, :], one[:, :], ALU.subtract))
            ch.add(nc.vector.memset(ctl[:, 5:8], 0.0))
            ch.link(nc.vector.tensor_tensor(ctl[:, 1:2], row[:, 0, BLOCKS - 1:BLOCKS], row[:, 1, BLOCKS - 1:BLOCKS],
                                            ALU.add))
            ch.link(nc.vector.tensor_scalar(ctl[:, 0:1], ctl[:, 1:2], float(RING - 1), None, ALU.add))
            ch.link(nc.vector.tensor_copy(k.ctl_i[:, :], ctl[:, :]))
            ch.add(nc.vector.tensor_single_scalar(k.ctl_i[:, 0:1], k.ctl_i[:, 0:1], 2, ALU.logical_shift_right))
            ch.link(nc.vector.tensor_copy(k.row_i[:, :, :], row[:, :, :]))
            dve.sem_inc(rows_ready, 1)
            ch.add(nc.vector.tensor_tensor(valid[:, :, :], bc(k.iota[:, 0:WIDE].unsqueeze(1), [P, BLOCKS, WIDE]),
                                           bc(k.deg_r[:, :].unsqueeze(2), [P, BLOCKS, WIDE]), ALU.is_lt))
            dve.wait_ge(wide_in, 16 * BLOCKS)
            ch.link(nc.vector.tensor_copy(code[:, :, :], wide[:, :, :]))
            v2 = lambda z: z[:, :, :].rearrange("p b w -> p (b w)")
            ch.link(nc.vector.scalar_tensor_tensor(out=v2(code), in0=v2(code), scalar=k.dummy4[:, :], in1=v2(valid),
                                                   op0=ALU.subtract, op1=ALU.mult))
            ch.link(nc.vector.tensor_scalar(v2(code_i), v2(code), k.dummy4[:, :], None, ALU.add))
            ch.add(nc.vector.tensor_copy(rows[:, :, :, SLOTS:2 * SLOTS],
                                         code_i[:, :, :].rearrange("p b (c s) -> p b c s", s=SLOTS)))
            ch.link(nc.vector.tensor_single_scalar(v2(wide), v2(code_i), 2, ALU.logical_shift_right))
            ch.add(nc.vector.tensor_copy(rows[:, :, :, 0:SLOTS],
                                         wide[:, :, :].rearrange("p b (c s) -> p b c s", s=SLOTS)))
            ch.add(nc.vector.tensor_copy(tail[:, 0, 0:SLOTS], bc(k.dummy[:, :], [P, SLOTS])))
            ch.add(nc.vector.tensor_copy(tail[:, 0, SLOTS:2 * SLOTS], bc(k.dummy4[:, :], [P, SLOTS])))
            ch.link(nc.vector.memset(tail[:, 0, CROW - 1:CROW], BLOCKS - 1))
            dve.sem_inc(chunk_rows, 1)
            dve.wait_ge(blocks_ready, 1)
            b0 = dve.value_load(k.ctl_i[0:1, 2:3], min_val=0, max_val=BLOCKS - 1)
            with dve.Fori(b0, BLOCKS) as b:
                n_c = dve.value_load(k.row_i[0:1, 0, bass.ds(b, 1)], min_val=1, max_val=CHUNKS)
                t0 = dve.value_load(k.row_i[0:1, 3, bass.ds(b, 1)], min_val=0, max_val=CHUNKS)
                dve.sem_clear(x_step)
                xs = Chain(dve, x_step)
                xs.link(nc.vector.memset(x_pos[:, :], float(WIDE)))
                with dve.Fori(WCH, n_c) as c:
                    dve.sem_clear(x_step)
                    xs = Chain(dve, x_step)
                    xs.link(nc.vector.tensor_tensor(x_first[:, :], first[:, bass.ds(b, 1)], x_pos[:, :], ALU.add))
                    nc.vector.tensor_scalar(x_first_i[:, :], x_first[:, :], float(E - 1), None, ALU.min)\
                        .then_inc(x_asked, 1)
                    xs.link(nc.vector.tensor_scalar(x_valid[:, :], k.iota[:, 0:SLOTS], x_pos[:, :], None, ALU.add))
                    xs.link(nc.vector.tensor_tensor(x_valid[:, :], x_valid[:, :],
                                                    bc(k.deg_r[:, bass.ds(b, 1)], [P, SLOTS]), ALU.is_lt))
                    xs.link(nc.vector.tensor_scalar(x_pos[:, :], x_pos[:, :], float(SLOTS), None, ALU.add))
                    dve.wait_ge(x_in, (t0 + (c - WCH)) * 16 + 16)
                    xs.link(nc.vector.tensor_copy(x_code[:, :], x_wide[:, 0:SLOTS]))
                    xs.link(nc.vector.scalar_tensor_tensor(out=x_code[:, :], in0=x_code[:, :], scalar=k.dummy4[:, :],
                                                           in1=x_valid[:, :], op0=ALU.subtract, op1=ALU.mult))
                    xs.link(nc.vector.tensor_scalar(x_code_i[:, :], x_code[:, :], k.dummy4[:, :], None, ALU.add))
                    xs.add(nc.vector.tensor_copy(x_row[:, 0, SLOTS:2 * SLOTS], x_code_i[:, :]))
                    xs.add(nc.vector.tensor_single_scalar(x_row[:, 0, 0:SLOTS], x_code_i[:, :], 2,
                                                          ALU.logical_shift_right))
                    xs.link(nc.vector.tensor_copy(x_row[:, 0, CROW - 1:CROW], rows[:, bass.ds(b, 1), 0, CROW - 1]))
                    dve.sem_inc(x_made, 1)
                    dve.wait_ge(x_out, (t0 + (c - WCH)) * 16 + 16)
                    dve.sem_inc(tick, 1)

        @block.sync
        def _(sp):
            sp.dma_start(info[:, :, :], k.info_tab[:, :].rearrange("(b p) c -> p b c", p=P)).then_inc(info_in, 16)
            sp.wait_ge(rows_ready, 1)
            n_w = sp.value_load(k.ctl_i[0:1, 4:5], min_val=1, max_val=BLOCKS * WCH)
            total = sp.value_load(k.ctl_i[0:1, 1:2], min_val=1, max_val=CHUNKS - 16)
            b0 = sp.value_load(k.ctl_i[0:1, 2:3], min_val=0, max_val=BLOCKS - 1)
            sp.wait_ge(chunk_rows, 1)
            sp.wait_ge(blocks_ready, 1)
            with sp.Fori(0, BLOCKS) as b:
                n_b = sp.value_load(k.row_i[0:1, 2, bass.ds(b, 1)], min_val=1, max_val=WCH)
                c_b = sp.value_load(k.row_i[0:1, 1, bass.ds(b, 1)], min_val=0, max_val=CHUNKS - 16)
                with sp.Fori(0, n_b) as c:
                    sp.dma_start(k.chunk_tab[bass.ds(chunk_at(nc, c_b + c), 1)].rearrange("a p c -> p a c"),
                                 rows[:, bass.ds(b, 1), bass.ds(c, 1), :].rearrange("p a b c -> p (a b) c"))\
                        .then_inc(written, 16)
            with sp.Fori(b0, BLOCKS) as b:
                n_c = sp.value_load(k.row_i[0:1, 0, bass.ds(b, 1)], min_val=1, max_val=CHUNKS)
                c_b = sp.value_load(k.row_i[0:1, 1, bass.ds(b, 1)], min_val=0, max_val=CHUNKS - 16)
                t0 = sp.value_load(k.row_i[0:1, 3, bass.ds(b, 1)], min_val=0, max_val=CHUNKS)
                with sp.Fori(WCH, n_c) as c:
                    sp.wait_ge(x_made, t0 + (c - WCH) + 1)
                    sp.sem_inc(tick, 1)
                    sp.dma_start(k.chunk_tab[bass.ds(chunk_at(nc, c_b + c), 1)].rearrange("a p c -> p a c"), x_row[:, :, :])\
                        .then_inc(x_out, 16)
                    sp.wait_ge(x_out, (t0 + (c - WCH)) * 16 + 16)
                    sp.sem_inc(tick, 1)
            for j in range(8):
                sp.dma_start(k.chunk_tab[bass.ds(chunk_at(nc, total + j), 1)].rearrange("a p c -> p a c"), tail[:, :, :])\
                    .then_inc(tail_out, 16)
            sp.wait_ge(written, n_w * 16)
            sp.sem_inc(tick, 1)
            sp.wait_ge(tail_out, 16 * 8)


def fetch_rows(nc, k, table, width, parts):
    with ExitStack() as ctx:
        m = Mem(nc, ctx)
        held = [m.sb(f"held{j}", [P, width]) for j in range(GROUP)]
        landed = [m.sem(f"landed{j}") for j in range(GROUP)]
        copied = [m.sem(f"copied{j}") for j in range(GROUP)]
        index = m.sb("index", [P, GROUP], I32)
        block = ctx.enter_context(nc.Block())

        @block.gpsimd
        def _(pool):
            for b in range(BLOCKS):
                j = b % GROUP
                if b >= GROUP:
                    pool.wait_ge(copied[j], (b // GROUP) * len(parts))
                pool.indirect_dma_start(held[j][:, :], None, table, at(k.node_r[:, b:b + 1])).then_inc(landed[j], 16)

        @block.vector
        def _(dve):
            with dve.Fori(0, TURNS) as t:
                for j in range(GROUP):
                    dve.wait_ge(landed[j], t * 16 + 16)
                    for buf, c0, n in parts:
                        nc.vector.tensor_copy(buf[:, bass.ds(t * GROUP + j, 1), 0:n],
                                              held[j][:, c0:c0 + n].unsqueeze(1)).then_inc(copied[j], 1)
            for j in range(GROUP):
                dve.wait_ge(copied[j], TURNS * len(parts))


def cosine_edges(nc, k, own_hn, own_v):
    W = D + 2
    with ExitStack() as ctx:
        m = Mem(nc, ctx)
        lists = [m.sb(f"list{s}", [P, PER_STAGE, SLOTS], I32) for s in range(STAGES)]
        meta = m.sb("meta", [1, RING], I32)
        got = m.sb("got", [P, RING, SLOTS, D])
        prod = m.sb("prod", [P, SLOTS, D])
        score = m.sb("score", [P, 2, SLOTS])
        ex = m.sb("ex", [P, 2, SLOTS])
        idx = m.sb("idx", [P, RING, SLOTS])
        vals = m.sb("vals", [P, 2, SLOTS, W])
        eq = m.sb("eq", [P, 2, SLOTS, P])
        firsts = m.sb("firsts", [P, SLOTS])
        moved = m.sb("moved", [P, SLOTS])
        to = m.sb("to", [P, RING, SLOTS], I32)
        out = m.sb("out_rows", [P, RING, SLOTS, W])
        weight = m.sb("weight", [P, 2])
        wexp = m.sb("wexp", [P, P])
        p_idx = [m.ps(f"p_idx{j}", [P, SLOTS, P]) for j in range(2)]
        p_sum = [m.ps(f"p_sum{j}", [P, SLOTS, 128]) for j in range(2)]
        list_in = [m.sem(f"list_in{s}") for s in range(STAGES)]
        list_used = [m.sem(f"list_used{s}") for s in range(STAGES)]
        meta_in, meta_used = m.sem("meta_in"), m.sem("meta_used")
        landed = [m.sem(f"landed{q}") for q in range(RING)]
        got_free = [m.sem(f"got_free{q}") for q in range(RING)]
        step, turn_step, pool_turn = m.sem("step"), m.sem("turn_step"), m.sem("pool_turn")
        idx_ready, spread, eq_ready = m.sem("idx_ready"), m.sem("spread"), m.sem("eq_ready")
        score_ready, ex_ready, vals_ready = m.sem("score_ready"), m.sem("ex_ready"), m.sem("vals_ready")
        summed, sum_copied, tick = m.sem("summed"), m.sem("sum_copied"), m.sem("tick")
        scattered = m.sem("scattered")
        rows_ready, to_ready = m.sem("rows_ready"), m.sem("to_ready")
        added = [m.sem(f"added{s}") for s in range(SLOTS)]
        block = ctx.enter_context(nc.Block())

        @block.sync
        def _(sp):
            n = sp.value_load(k.ctl_i[0:1, 0:1], min_val=1, max_val=CHUNKS // RING - 2)
            for s in range(STAGES):
                sp.dma_start(lists[s][:, :, :], k.chunk_tab[s * PER_STAGE:(s + 1) * PER_STAGE, :, 0:SLOTS]
                             .rearrange("a p c -> p a c")).then_inc(list_in[s], 16)
            sp.dma_start(meta[:, :], k.chunk_tab[0:RING, 0, CROW - 1:CROW].rearrange("a c -> c a"),
                         allow_slow_non_contiguous=True)\
                .then_inc(meta_in, 16)
            with sp.Fori(0, n) as i:
                for s in range(STAGES):
                    sp.wait_ge(list_used[s], (i + 1) * 2 * PER_STAGE)
                    sp.sem_inc(tick, 1)
                    sp.dma_start(lists[s][:, :, :], k.chunk_tab[bass.ds(i * RING + RING + s * PER_STAGE, PER_STAGE),
                                                                :, 0:SLOTS].rearrange("a p c -> p a c"))\
                        .then_inc(list_in[s], 16)
                    if s == 0:
                        sp.wait_ge(meta_used, i + 1)
                        sp.sem_inc(tick, 1)
                        sp.dma_start(meta[:, :], k.chunk_tab[bass.ds(i * RING + RING, RING), 0, CROW - 1:CROW]
                                     .rearrange("a c -> c a"), allow_slow_non_contiguous=True).then_inc(meta_in, 16)
            sp.wait_ge(list_in[0], n * 16 + 16)
            sp.wait_ge(list_in[1], n * 16 + 16)
            sp.wait_ge(meta_in, n * 16 + 16)
            sp.sem_inc(tick, 1)

        @block.gpsimd
        def _(pool):
            n = pool.value_load(k.ctl_i[0:1, 0:1], min_val=1, max_val=CHUNKS // RING - 2)

            def gather(q):
                s, c = divmod(q, PER_STAGE)
                for j in range(SLOTS):
                    pool.indirect_dma_start(got[:, q, j, :], None, k.hn_tab[:, :], at(lists[s][:, c, j:j + 1]))\
                        .then_inc(landed[q], 16)

            def scatter(q):
                for j in range(SLOTS):
                    pool.indirect_dma_start(k.sums[j][:, :], at(to[:, q, j:j + 1]), out[:, q, j, 0:D + 1], None,
                                            compute_op=ALU.add).then_inc(added[j], 16)

            pool.sem_inc(scattered, RING - 1)
            for j in range(SLOTS):
                pool.indirect_dma_start(k.sums[j][:, :], at(k.dummy_i[:, :]), k.zeros[:, 0:D + 1], None,
                                        compute_op=ALU.add).then_inc(added[j], 16)
            pool.wait_ge(list_in[0], 16)
            gather(0)
            gather(1)
            with pool.Fori(0, n) as i:
                def gather_turn(q, ahead):
                    if q % PER_STAGE == 0:
                        pool.wait_ge(list_in[q // PER_STAGE], (i + ahead + 1) * 16)
                    pool.wait_ge(got_free[q], i + ahead + 1)
                    pool.sem_inc(pool_turn, 1)
                    gather(q)

                def scatter_turn(q):
                    pool.wait_ge(to_ready, i * RING + q + 1)
                    pool.wait_ge(rows_ready, i * RING + q + 1)
                    for j in range(SLOTS):
                        pool.wait_ge(added[j], (i * RING + q + 1) * 16)
                    pool.sem_inc(scattered, 1)
                    scatter(q)

                gather_turn(2, 0)
                scatter_turn(0)
                gather_turn(3, 0)
                scatter_turn(1)
                gather_turn(0, 1)
                scatter_turn(2)
                gather_turn(1, 1)
                scatter_turn(3)
            for j in range(SLOTS):
                pool.wait_ge(added[j], n * (16 * RING) + 16)
            for q in range(2):
                pool.wait_ge(landed[q], n * 64 + 64)

        @block.vector
        def _(dve):
            n = dve.value_load(k.ctl_i[0:1, 0:1], min_val=1, max_val=CHUNKS // RING - 2)
            ch = Chain(dve, step)
            ch.link(nc.vector.memset(wexp[:, :], 0.5))
            ch.link(nc.vector.tensor_tensor_scan(wexp[:, :], wexp[:, :], wexp[:, :], 2.0 ** 61, ALU.mult, ALU.bypass))
            ch.link(nc.vector.tensor_tensor(eq[:, 0, 0, :], wexp[:, :], k.ident[:, :], ALU.mult))
            ch.link(nc.vector.tensor_reduce(weight[:, 0:1], eq[:, 0, 0, :], AX, ALU.add))
            ch.link(nc.vector.tensor_scalar(weight[:, 1:2], weight[:, 0:1], 2.0, None, ALU.mult))
            for z in range(2):
                ch.add(nc.vector.tensor_copy(vals[:, z, :, D + 1:D + 2], bc(weight[:, 0:1].unsqueeze(1), [P, SLOTS, 1])))
            ch.wait()
            for q in range(RING):
                dve.sem_inc(got_free[q], 1)
            with dve.Fori(0, n) as i:
                dve.sem_clear(turn_step)
                ts = Chain(dve, turn_step)
                dve.wait_ge(meta_in, i * 16 + 16)
                dve.sem_inc(tick, 1)
                _, b = nc.values_load_multi_w_load_instructions(meta[0:1, 0:RING], engines=DVE, min_val=0,
                                                                max_val=BLOCKS - 1)
                dve.sem_inc(meta_used, 1)

                def indices(s):
                    dve.wait_ge(list_in[s], i * 16 + 16)
                    nc.vector.tensor_copy(idx[:, s * PER_STAGE:(s + 1) * PER_STAGE, :], lists[s][:, :, :])\
                        .then_inc(idx_ready, 1)
                    dve.wait_ge(idx_ready, i * 2 + s + 1)
                    dve.sem_inc(list_used[s], PER_STAGE)

                def first_half(q):
                    dve.wait_ge(landed[q], i * 64 + 64)
                    dve.sem_inc(list_used[q // PER_STAGE], 1)
                    ts.add(nc.vector.tensor_tensor(prod[:, :, :], got[:, q, :, :],
                                                   bc(own_hn[:, bass.ds(b[q], 1), :], [P, SLOTS, D]), ALU.mult))
                    ts.wait()
                    dve.sem_inc(got_free[q], 1)
                    nc.vector.tensor_reduce(score[:, q % 2, :], prod[:, :, :], AX, ALU.add).then_inc(score_ready, 1)
                    dve.wait_ge(score_ready, i * RING + q + 1)
                    dve.wait_ge(spread, i * RING + q + 1)
                    nc.vector.tensor_tensor(eq[:, q % 2, :, :], p_idx[q % 2][:, :, :],
                                            bc(idx[:, q, :].unsqueeze(2), [P, SLOTS, P]), ALU.is_equal)\
                        .then_inc(eq_ready, 1)

                def second_half(q):
                    dve.wait_ge(ex_ready, i * RING + q + 1)
                    nc.vector.tensor_tensor(vals[:, q % 2, :, 0:D + 1],
                                            bc(own_v[:, bass.ds(b[q], 1), :], [P, SLOTS, D + 1]),
                                            bc(ex[:, q % 2, :].unsqueeze(2), [P, SLOTS, D + 1]), ALU.mult)\
                        .then_inc(vals_ready, 1)

                def third_half(q):
                    dve.wait_ge(rows_ready, i * RING + q + 1)
                    ts.link(nc.vector.tensor_scalar(firsts[:, :], out[:, q, :, D + 1], weight[:, 1:2], None,
                                                    ALU.is_le))
                    ts.link(nc.vector.scalar_tensor_tensor(out=moved[:, :], in0=idx[:, q, :], scalar=k.dummy[:, :],
                                                           in1=firsts[:, :], op0=ALU.subtract, op1=ALU.mult))
                    dve.wait_ge(scattered, i * RING + q + 1)
                    nc.vector.tensor_scalar(to[:, q, :], moved[:, :], k.dummy[:, :], None, ALU.add)\
                        .then_inc(to_ready, 1)
                    dve.wait_ge(to_ready, i * RING + q + 1)

                indices(0)
                first_half(0)
                first_half(1)
                second_half(0)
                indices(1)
                third_half(0)
                second_half(1)
                first_half(2)
                third_half(1)
                second_half(2)
                first_half(3)
                third_half(2)
                second_half(3)
                third_half(3)

        @block.scalar
        def _(act):
            n = act.value_load(k.ctl_i[0:1, 0:1], min_val=1, max_val=CHUNKS // RING - 2)
            act.sem_inc(sum_copied, 2)
            with act.Fori(0, n) as i:
                def exps(q):
                    act.wait_ge(score_ready, i * RING + q + 1)
                    nc.scalar.activation(ex[:, q % 2, :], score[:, q % 2, :], ACT.Exp).then_inc(ex_ready, 1)

                def rows(q):
                    act.wait_ge(summed, i * RING + q + 1)
                    act.wait_ge(scattered, i * RING + q + 1)
                    nc.scalar.activation(out[:, q, :, :], p_sum[q % 2][:, :, 0:W], ACT.Copy).then_inc(rows_ready, 1)
                    act.wait_ge(rows_ready, i * RING + q + 1)
                    act.sem_inc(sum_copied, 1)

                exps(0)
                exps(1)
                rows(0)
                exps(2)
                rows(1)
                exps(3)
                rows(2)
                rows(3)

        @block.tensor
        def _(pe):
            n = pe.value_load(k.ctl_i[0:1, 0:1], min_val=1, max_val=CHUNKS // RING - 2)
            with pe.Fori(0, n) as i:
                def spread_idx(q):
                    pe.wait_ge(idx_ready, i * 2 + q // PER_STAGE + 1)
                    if q >= 2:
                        pe.wait_ge(eq_ready, i * RING + q - 1)
                    for j in range(SLOTS):
                        last = nc.tensor.matmul(p_idx[q % 2][:, j, :], bc(idx[:, q, j:j + 1], [P, P]), k.ident[:, :],
                                                start=True, stop=True)
                    last.then_inc(spread, 1)

                def sum_equal(q):
                    pe.wait_ge(eq_ready, i * RING + q + 1)
                    pe.wait_ge(vals_ready, i * RING + q + 1)
                    pe.wait_ge(sum_copied, i * RING + q + 1)
                    for j in range(SLOTS):
                        last = nc.tensor.matmul(p_sum[q % 2][:, j, 0:W], eq[:, q % 2, j, :], vals[:, q % 2, j, :],
                                                start=True, stop=True)
                    last.then_inc(summed, 1)

                spread_idx(0)
                spread_idx(1)
                sum_equal(0)
                spread_idx(2)
                sum_equal(1)
                spread_idx(3)
                sum_equal(2)
                sum_equal(3)



def cosine_close(nc, k, a):
    with ExitStack() as ctx:
        m = Mem(nc, ctx)
        x = m.sb("x_close", [NP_, NC, D])
        part = [m.sb(f"part{j}", [NP_, NC, D + 1]) for j in range(SLOTS)]
        den = m.sb("den", [NP_, NC])
        inv = m.sb("inv", [NP_, NC])
        x_in, stored, step, done = m.sem("x_in"), m.sem("stored"), m.sem("step"), m.sem("done")
        part_in = [m.sem(f"part_in{j}") for j in range(SLOTS)]
        block = ctx.enter_context(nc.Block())

        @block.sync
        def _(sp):
            for j in range(SLOTS):
                sp.dma_start(part[j][:, :, :], k.sums[j][0:N, :].rearrange("(p c) d -> p c d", p=NP_))\
                    .then_inc(part_in[j], 16)
            sp.dma_start(x[:, :, :], a["x"].rearrange("(p c) d -> p c d", p=NP_)).then_inc(x_in, 16)
            sp.wait_ge(done, 1)
            sp.dma_start(k.x1_tab[0:N, :].rearrange("(p c) d -> p c d", p=NP_), x[:, :, :]).then_inc(stored, 16)
            sp.wait_ge(stored, 16)

        @block.vector
        def _(dve):
            ch = Chain(dve, step)
            dve.wait_ge(part_in[0], 16)
            for j in range(1, SLOTS):
                dve.wait_ge(part_in[j], 16)
                ch.link(nc.vector.tensor_tensor(part[0][:, :, :], part[0][:, :, :], part[j][:, :, :], ALU.add))
            ch.link(nc.vector.tensor_scalar(den[:, :], part[0][:, :, D], 1e-30, None, ALU.max))
            ch.link(nc.vector.reciprocal(inv[:, :], den[:, :]))
            ch.link(nc.vector.tensor_tensor(part[1][:, :, 0:D], part[0][:, :, 0:D],
                                            bc(inv[:, :].unsqueeze(2), [NP_, NC, D]), ALU.mult))
            dve.wait_ge(x_in, 16)
            nc.vector.tensor_tensor(x[:, :, :], x[:, :, :], part[1][:, :, 0:D], ALU.add).then_inc(done, 1)


def load_weights(nc, k, a):
    HW = H1 * (C1 + 1)
    with ExitStack() as ctx:
        m = Mem(nc, ctx)
        plain1, plain2 = m.sb("plain1", [P, D]), m.sb("plain2", [P, D])
        att = {n: m.sb("att_" + n, [P, D]) for n in ("a1_src", "a1_dst", "a2_src", "a2_dst")}
        prod, lin = m.sb("prod", [P, D]), m.sb("lin", [P, 1])
        wide = {n: m.sb("wide_" + n, [D, 2, 2, D]) for n in ("Wa_w", "lin_w")}
        p_w = [m.ps(f"p_w{j}", [P, D]) for j in range(4)]
        loaded, step, turned = m.sem("loaded"), m.sem("step"), m.sem("turned")
        block = ctx.enter_context(nc.Block())
        both = ((0, D), (D, P))

        @block.sync
        def _(sp):
            n = 0

            def load(dst, src):
                nonlocal n
                sp.dma_start(dst, src).then_inc(loaded, 16)
                n += 1

            for lo, hi in both:
                load(plain1[lo:hi, :], a["L1_gnn_W1"])
                load(plain2[lo:hi, :], a["L1_gnn_W2"])
                load(k.w_gcn[lo:hi, :], a["L2_gnn_W"])
                for t in range(TYPES):
                    load(k.w_src[lo:hi, AW + t * D:AW + (t + 1) * D], a["L3_gnn_r"][t, D:2 * D, :])
                    load(k.w_own[lo:hi, AW + t * D:AW + (t + 1) * D], a["L3_gnn_r"][t, 0:D, :])
            for name, tile in att.items():
                load(tile[:, :], a["L1_gnn_" + name].rearrange("h c -> (h c)").partition_broadcast(P))
            for name, tile in k.vec.items():
                load(tile[:, :], a[name].partition_broadcast(P))
            load(k.att_a[:, :], a["L3_gnn_a"][0, :].partition_broadcast(P))
            for name, tile in wide.items():
                for c in range(2):
                    load(tile[:, :, c, :], a["L3_gnn_" + name].rearrange("o (h i) -> o h i", h=2))
            k.weights_loaded = n * 16
            sp.wait_ge(loaded, k.weights_loaded)
            sp.sem_inc(turned, 1)

        @block.tensor
        def _(pe):
            pe.wait_ge(turned, 1)
            for j, name in enumerate(("Wa_w", "lin_w")):
                for h in range(2):
                    last = nc.tensor.transpose(p_w[2 * j + h][:, :], wide[name][:, h, :, :].rearrange("o c i -> o (c i)"),
                                               k.ident[0:D, 0:D])
            last.then_inc(turned, 1)

        @block.vector
        def _(dve):
            ch = Chain(dve, step)
            ch.link(nc.vector.memset(k.w_gat1[:, :], 0.0))
            ch.link(nc.vector.memset(k.w_gat2[:, :], 0.0))
            dve.wait_ge(turned, 1)
            for plain, w, heads, c, names in ((plain1, k.w_gat1, H1, C1, ("a1_src", "a1_dst")),
                                              (plain2, k.w_gat2, 1, D, ("a2_src", "a2_dst"))):
                ch.link(nc.vector.tensor_copy(w[:, 0:heads * (c + 1)].rearrange("p (h c) -> p h c", h=heads)[:, :, 0:c],
                                              plain[:, :].rearrange("p (h c) -> p h c", h=heads)))
                for n, name in enumerate(names):
                    at0 = heads * (c + 1) + n * heads
                    ch.link(nc.vector.tensor_tensor(prod[:, :], plain[:, :], att[name][:, :], ALU.mult))
                    ch.link(nc.vector.tensor_reduce(w[:, at0:at0 + heads],
                                                    prod[:, :].rearrange("p (h c) -> p h c", h=heads), AX, ALU.add))
            dve.wait_ge(turned, 2)
            for j, dst in enumerate((k.w_own[:, 0:D], k.w_src[:, 0:D], k.w_lin[:, 0, :], k.w_lin[:, 1, :])):
                ch.link(nc.vector.tensor_copy(dst, p_w[j][:, :]))
            bias_a = k.vec["L3_gnn_Wa_b"]
            for src, dst in ((k.w_own[:, 0:D], k.w_own[:, D:AW]), (k.w_src[:, 0:D], k.w_src[:, D:AW]),
                             (bias_a[:, :], k.own_bias[:, D:AW])):
                ch.link(nc.vector.tensor_tensor(prod[:, :], src, k.att_a[:, :], ALU.mult))
                ch.link(nc.vector.tensor_reduce(lin[:, :], prod[:, :], AX, ALU.add))
                ch.link(nc.vector.tensor_scalar(dst, lin[:, :], REL_SLOPE, None, ALU.mult))
            ch.add(nc.vector.tensor_copy(k.own_bias[:, 0:D], bias_a[:, :]))
            ch.add(nc.vector.memset(k.own_bias[:, AW:OROW], 0.0))
            ch.link(nc.vector.tensor_scalar(k.att_a99[:, :], k.att_a[:, :], 1.0 - REL_SLOPE, None, ALU.mult))


def open_layer(nc, k, x, h):
    with ExitStack() as ctx:
        m = Mem(nc, ctx)
        sq, st = m.sb("sq", [P, BLOCKS, D]), m.sb("st", [P, 4, BLOCKS])
        step, var_ready, std_ready = m.sem("step"), m.sem("var_ready"), m.sem("std_ready")
        block = ctx.enter_context(nc.Block())

        @block.vector
        def _(dve):
            relu_norm(nc, dve, Chain(dve, step), x[:, :, :], h[:, :, :], sq[:, :, :], st, [P, BLOCKS, D],
                      var_ready, std_ready, 1)

        @block.scalar
        def _(act):
            act.wait_ge(var_ready, 1)
            nc.scalar.activation(st[:, 2, :], st[:, 1, :], ACT.Sqrt).then_inc(std_ready, 1)


def project(nc, k, h, weights, width, rows):
    with ExitStack() as ctx:
        m = Mem(nc, ctx)
        p_t = [m.ps(f"p_t{j}", [P, P]) for j in range(2)]
        p_o = [m.ps(f"p_o{j}", [P, 2, 512]) for j in range(2)]
        staged = m.sb("staged", [P, 2, 2, D])
        hT = m.sb("hT", [P, 2, P])
        tr, copied, made, stored = m.sem("transposed"), m.sem("copied"), m.sem("made"), m.sem("stored")
        stage_ready, stage_free, tick = m.sem("stage_ready"), m.sem("stage_free"), m.sem("tick")
        block = ctx.enter_context(nc.Block())
        PAIRS = BLOCKS // 2
        TP = 7

        @block.gpsimd
        def _(pool):
            with pool.Fori(0, PAIRS // TP) as t:
                for j in range(TP):
                    n = t * TP + j
                    pool.wait_ge(stage_free, n + (1 if j else 2))
                    pool.sem_inc(tick, 1)
                    nc.gpsimd.tensor_copy(staged[:, j % 2, :, :], h[:, bass.ds(n * 2, 2), :]).then_inc(stage_ready, 1)

        @block.tensor
        def _(pe):
            pe.sem_inc(stage_free, 2)
            with pe.Fori(0, PAIRS // TP) as t:
                for j in range(TP):
                    n, z = t * TP + j, j % 2
                    pe.wait_ge(stored, n + (1 if j else 2))
                    pe.wait_ge(stage_ready, n + 1)
                    nc.tensor.transpose(p_t[z][:, :], staged[:, z, :, :].rearrange("p b d -> p (b d)"),
                                        k.ident[:, :]).then_inc(tr, 1)
                    pe.wait_ge(copied, n + 1)
                    pe.sem_inc(stage_free, 1)
                    for y in range(2):
                        last = nc.tensor.matmul(p_o[z][:, y, 0:width], hT[y * D:(y + 1) * D, z, :],
                                                weights[y * D:(y + 1) * D, 0:width], start=True, stop=True)
                    last.then_inc(made, 1)

        @block.scalar
        def _(act):
            with act.Fori(0, PAIRS // TP) as t:
                for j in range(TP):
                    act.wait_ge(tr, t * TP + j + 1)
                    nc.scalar.activation(hT[:, j % 2, :], p_t[j % 2][:, :], ACT.Copy).then_inc(copied, 1)

        @block.vector
        def _(dve):
            dve.sem_inc(stored, 2)
            with dve.Fori(0, PAIRS // TP) as t:
                for j in range(TP):
                    n = t * TP + j
                    dve.wait_ge(made, n + 1)
                    nc.vector.tensor_copy(rows[:, bass.ds(n * 2, 2), 0:width], p_o[j % 2][:, :, 0:width])\
                        .then_inc(stored, 1)
            dve.wait_ge(stored, PAIRS + 2)


def spread_rows(nc, k, rows, width, table, dummy_col):
    with ExitStack() as ctx:
        m = Mem(nc, ctx)
        dummy = m.sb("dummy", [P, width])
        set_, out = m.sem("dummy_set"), m.sem("rows_out")
        spread = m.sem("spread")
        block = ctx.enter_context(nc.Block())

        @block.vector
        def _(dve):
            nc.vector.memset(dummy[:, :], 0.0).then_inc(set_, 1)
            dve.wait_ge(set_, 1)
            if dummy_col is not None:
                nc.vector.memset(dummy[:, dummy_col:width], MINUS).then_inc(set_, 1)
                dve.wait_ge(set_, 2)
            dve.sem_inc(set_, 1)

        @block.sync
        def _(sp):
            sp.wait_ge(set_, 2 if dummy_col is None else 3)
            sp.dma_start(table[NPAD:ROWS, :], dummy[:, :]).then_inc(out, 16)
            sp.wait_ge(out, 16)

        @block.gpsimd
        def _(pool):
            for b in range(BLOCKS):
                pool.indirect_dma_start(table, at(k.node_r[:, b:b + 1]), rows[:, b, 0:width], None)\
                    .then_inc(spread, 16)
            pool.wait_ge(spread, 16 * BLOCKS)


def ring_buffers(m, width, stages=STAGES):
    r = type("Ring", (), {})()
    r.per_stage = RING // stages
    r.lists = [m.sb(f"list{s}", [P, r.per_stage, SLOTS], I32) for s in range(stages)]
    r.meta = m.sb("meta", [1, RING], I32)
    r.got = m.sb("got", [P, RING, SLOTS, width])
    r.list_in = [m.sem(f"list_in{s}") for s in range(stages)]
    r.list_used = [m.sem(f"list_used{s}") for s in range(stages)]
    r.meta_in, r.meta_used = m.sem("meta_in"), m.sem("meta_used")
    r.landed = [m.sem(f"landed{q}") for q in range(RING)]
    r.got_free = [m.sem(f"got_free{q}") for q in range(RING)]
    r.tick, r.turn_step = m.sem("tick"), m.sem("turn_step")
    return r


def turns(eng, k):
    return eng.value_load(k.ctl_i[0:1, 0:1], min_val=1, max_val=CHUNKS // RING - 2)


def load_lists(nc, sp, k, r, i, first, own=None):
    for s in range(STAGES):
        sp.wait_ge(r.list_used[s], (i + 1) * PER_STAGE)
        sp.sem_inc(r.tick, 1)
        sp.dma_start(r.lists[s][:, :, :], k.chunk_tab[bass.ds(i * RING + s * PER_STAGE, PER_STAGE), :,
                                                      first:first + SLOTS].rearrange("a p c -> p a c"))\
            .then_inc(r.list_in[s], 16)
    sp.wait_ge(r.meta_used, i + 1)
    sp.sem_inc(r.tick, 1)
    sp.dma_start(r.meta[:, :], k.chunk_tab[bass.ds(i * RING, RING), 0, CROW - 1:CROW].rearrange("a c -> c a"),
                 allow_slow_non_contiguous=True).then_inc(r.meta_in, 16)


def gather_all(nc, pool, k, r, table):
    n = turns(pool, k)
    with pool.Fori(0, n) as i:
        for q in range(RING):
            s, c = divmod(q, r.per_stage)
            if c == 0:
                pool.wait_ge(r.list_in[s], i * 16 + 16)
            pool.wait_ge(r.got_free[q], i + 1)
            pool.sem_inc(r.tick, 1)
            for j in range(SLOTS):
                pool.indirect_dma_start(r.got[:, q, j, :], None, table, at(r.lists[s][:, c, j:j + 1]))\
                    .then_inc(r.landed[q], 16)


def ring_credits(dve, r, readers=1, free=RING):
    for q in range(free):
        dve.sem_inc(r.got_free[q], 1)
    for used in r.list_used:
        dve.sem_inc(used, r.per_stage)
    dve.sem_inc(r.meta_used, readers)


def turn_blocks(nc, eng, engines, r, i):
    eng.wait_ge(r.meta_in, i * 16 + 16)
    eng.sem_inc(r.tick, 1)
    _, b = nc.values_load_multi_w_load_instructions(r.meta[0:1, 0:RING], engines=engines, min_val=0,
                                                    max_val=BLOCKS - 1)
    eng.sem_inc(r.meta_used, 1)
    return b


def gat_edges(nc, k, heads, c, state, top, own_dst, table):
    HW = heads * (c + 1)
    W = HW + heads
    with ExitStack() as ctx:
        m = Mem(nc, ctx)
        r = ring_buffers(m, W)
        e = m.sb("e", [P, 2, SLOTS + 1, heads])
        p = m.sb("p", [P, 2, SLOTS + 1, heads])
        prod = m.sb("prod", [P, SLOTS, HW])
        part = m.sb("part", [P, HW])
        old = m.sb("old", [P, HW])
        e_ready, p_ready = m.sem("e_ready"), m.sem("p_ready")
        block = ctx.enter_context(nc.Block())

        @block.sync
        def _(sp):
            n = turns(sp, k)
            with sp.Fori(0, n) as i:
                load_lists(nc, sp, k, r, i, 0)

        @block.gpsimd
        def _(pool):
            gather_all(nc, pool, k, r, table)

        @block.vector
        def _(dve):
            n = turns(dve, k)
            ring_credits(dve, r)
            with dve.Fori(0, n) as i:
                dve.sem_clear(r.turn_step)
                ts = Chain(dve, r.turn_step)
                b = turn_blocks(nc, dve, DVE, r, i)

                def scores(q):
                    z = q % 2
                    dve.wait_ge(r.landed[q], i * 64 + 64)
                    dve.sem_inc(r.list_used[q // PER_STAGE], 1)
                    blk = bass.ds(b[q], 1)
                    ts.add(nc.vector.tensor_copy(e[:, z, SLOTS, :], top[:, blk, :].rearrange("p b h -> p (b h)")))
                    ts.link(nc.vector.tensor_tensor(e[:, z, 0:SLOTS, :], r.got[:, q, :, HW:W],
                                                    bc(own_dst[:, blk, :], [P, SLOTS, heads]), ALU.add))
                    ts.link(nc.vector.scalar_tensor_tensor(out=e[:, z, 0:SLOTS, :], in0=e[:, z, 0:SLOTS, :],
                                                           scalar=SLOPE, in1=e[:, z, 0:SLOTS, :],
                                                           op0=ALU.mult, op1=ALU.max))
                    ts.link(nc.vector.tensor_reduce(top[:, blk, :].rearrange("p b h -> p (b h)"),
                                                    e[:, z, :, :].rearrange("p s h -> p h s"), AX, ALU.max))
                    n_e = nc.vector.tensor_tensor(e[:, z, :, :], e[:, z, :, :],
                                                  bc(top[:, blk, :], [P, SLOTS + 1, heads]), ALU.subtract)
                    n_e.then_inc(e_ready, 1)

                def sums(q):
                    z = q % 2
                    blk = bass.ds(b[q], 1)
                    dve.wait_ge(p_ready, i * RING + q + 1)
                    hc = "p s (h c) -> p s h c"
                    ts.add(nc.vector.tensor_tensor(prod[:, :, :].rearrange(hc, h=heads),
                                                   r.got[:, q, :, 0:HW].rearrange(hc, h=heads),
                                                   bc(p[:, z, 0:SLOTS, :].unsqueeze(3), [P, SLOTS, heads, c + 1]),
                                                   ALU.mult))
                    ts.link(nc.vector.tensor_tensor(old[:, :].rearrange("p (h c) -> p h c", h=heads),
                                                    state[:, blk, 0:HW].rearrange("p b (h c) -> p (b h) c", h=heads),
                                                    bc(p[:, z, SLOTS, :].unsqueeze(2), [P, heads, c + 1]), ALU.mult))
                    dve.sem_inc(r.got_free[q], 1)
                    ts.link(nc.vector.tensor_reduce(part[:, :], prod[:, :, :].rearrange("p s f -> p f s"), AX, ALU.add))
                    ts.link(nc.vector.tensor_tensor(state[:, blk, 0:HW].rearrange("p b f -> p (b f)"), part[:, :],
                                                    old[:, :], ALU.add))

                scores(0)
                for q in range(1, RING):
                    scores(q)
                    sums(q - 1)
                sums(RING - 1)
                dve.wait_ge(e_ready, i * RING + RING)

        @block.scalar
        def _(act):
            n = turns(act, k)
            with act.Fori(0, n) as i:
                for q in range(RING):
                    act.wait_ge(e_ready, i * RING + q + 1)
                    nc.scalar.activation(p[:, q % 2, :, :], e[:, q % 2, :, :], ACT.Exp).then_inc(p_ready, 1)


def gcn_edges(nc, k, state, table):
    with ExitStack() as ctx:
        m = Mem(nc, ctx)
        r = ring_buffers(m, D)
        part = m.sb("part", [P, D])
        block = ctx.enter_context(nc.Block())

        @block.sync
        def _(sp):
            n = turns(sp, k)
            with sp.Fori(0, n) as i:
                load_lists(nc, sp, k, r, i, 0)

        @block.gpsimd
        def _(pool):
            gather_all(nc, pool, k, r, table)

        @block.vector
        def _(dve):
            n = turns(dve, k)
            ring_credits(dve, r)
            with dve.Fori(0, n) as i:
                dve.sem_clear(r.turn_step)
                ts = Chain(dve, r.turn_step)
                b = turn_blocks(nc, dve, DVE, r, i)
                for q in range(RING):
                    own = state[:, bass.ds(b[q], 1), :].rearrange("p b d -> p (b d)")
                    dve.wait_ge(r.landed[q], i * 64 + 64)
                    dve.sem_inc(r.list_used[q // PER_STAGE], 1)
                    ts.link(nc.vector.tensor_reduce(part[:, :], r.got[:, q, :, :].rearrange("p s f -> p f s"), AX,
                                                    ALU.add))
                    dve.sem_inc(r.got_free[q], 1)
                    ts.link(nc.vector.tensor_tensor(own, own, part[:, :], ALU.add))


def gat_open(nc, k, heads, c, state, own_dst, top):
    HW = heads * (c + 1)
    with ExitStack() as ctx:
        m = Mem(nc, ctx)
        step = m.sem("step")
        block = ctx.enter_context(nc.Block())

        @block.vector
        def _(dve):
            ch = Chain(dve, step)
            ones = state[:, :, 0:HW].rearrange("p b (h c) -> p b h c", h=heads)[:, :, :, c:c + 1]
            ch.add(nc.vector.memset(ones, 1.0))
            ch.add(nc.vector.tensor_copy(own_dst[:, :, :], state[:, :, HW + heads:HW + 2 * heads]))
            ch.link(nc.vector.tensor_tensor(top[:, :, :], state[:, :, HW:HW + heads],
                                            state[:, :, HW + heads:HW + 2 * heads], ALU.add))
            ch.link(nc.vector.scalar_tensor_tensor(out=top[:, :, :], in0=top[:, :, :], scalar=SLOPE,
                                                   in1=top[:, :, :], op0=ALU.mult, op1=ALU.max))


def gat_close(nc, k, heads, c, state, bias, gain, shift, y, x_add):
    HW = heads * (c + 1)
    with ExitStack() as ctx:
        m = Mem(nc, ctx)
        sq, ex = m.sb("sq", [P, BLOCKS, D]), m.sb("ex", [P, BLOCKS, D])
        st = m.sb("st", [P, 4, BLOCKS])
        den = m.sb("den", [P, 2, BLOCKS, heads])
        step, var_ready, std_ready = m.sem("step"), m.sem("var_ready"), m.sem("std_ready")
        low_ready, ex_ready = m.sem("low_ready"), m.sem("ex_ready")
        block = ctx.enter_context(nc.Block())
        full = [P, BLOCKS, D]

        @block.vector
        def _(dve):
            ch = Chain(dve, step)
            tt, ts = nc.vector.tensor_tensor, nc.vector.tensor_scalar
            cols = state[:, :, 0:HW].rearrange("p b (h c) -> p b h c", h=heads)
            wide = lambda j: bc(st[:, j, :].unsqueeze(2), full)
            vec = lambda t: bc(t[:, :].unsqueeze(1), full)
            Y, SQ = y[:, :, :], sq[:, :, :]
            ch.link(ts(den[:, 0, :, :], cols[:, :, :, c], SM_EPS, None, ALU.add))
            ch.link(nc.vector.reciprocal(den[:, 1, :, :], den[:, 0, :, :]))
            ch.link(tt(y[:, :, :].rearrange("p b (h c) -> p b h c", h=heads), cols[:, :, :, 0:c],
                       bc(den[:, 1, :, :].unsqueeze(3), [P, BLOCKS, heads, c]), ALU.mult))
            ch.link(tt(Y, Y, vec(bias), ALU.add))
            ch.link(nc.vector.tensor_reduce(st[:, 0, :], Y, AX, ALU.add))
            ch.link(ts(st[:, 3, :], st[:, 0, :], 1.0 / D, None, ALU.mult))
            ch.link(tt(Y, Y, wide(3), ALU.subtract))
            ch.link(tt(SQ, Y, Y, ALU.mult))
            ch.link(nc.vector.tensor_reduce(st[:, 0, :], SQ, AX, ALU.add))
            ts(st[:, 1, :], st[:, 0, :], 1.0 / D, LN_EPS, ALU.mult, ALU.add).then_inc(var_ready, 1)
            dve.wait_ge(std_ready, 1)
            ch.link(nc.vector.reciprocal(st[:, 3, :], st[:, 2, :]))
            ch.link(tt(Y, Y, wide(3), ALU.mult))
            ch.link(tt(Y, Y, vec(gain), ALU.mult))
            ch.link(tt(Y, Y, vec(shift), ALU.add))
            ts(SQ, Y, 0.0, None, ALU.min).then_inc(low_ready, 1)
            ch.link(ts(Y, Y, 0.0, -1.0, ALU.max, ALU.add))
            dve.wait_ge(ex_ready, 1)
            ch.link(tt(Y, Y, ex[:, :, :], ALU.add))
            if x_add is not None:
                ch.link(tt(x_add[:, :, :], x_add[:, :, :], Y, ALU.add))

        @block.scalar
        def _(act):
            act.wait_ge(var_ready, 1)
            nc.scalar.activation(st[:, 2, :], st[:, 1, :], ACT.Sqrt).then_inc(std_ready, 1)
            act.wait_ge(low_ready, 1)
            nc.scalar.activation(ex[:, :, :], sq[:, :, :], ACT.Exp).then_inc(ex_ready, 1)


def gcn_scale(nc, k, state, dis):
    with ExitStack() as ctx:
        m = Mem(nc, ctx)
        root = m.sb("root", [P, 2, BLOCKS])
        step, deg_ready, root_ready = m.sem("step"), m.sem("deg_ready"), m.sem("root_ready")
        block = ctx.enter_context(nc.Block())

        @block.vector
        def _(dve):
            ch = Chain(dve, step)
            nc.vector.tensor_scalar(root[:, 0, :], k.deg_r[:, :], 1.0, None, ALU.add).then_inc(deg_ready, 1)
            dve.wait_ge(root_ready, 1)
            ch.link(nc.vector.reciprocal(dis[:, :], root[:, 1, :]))
            ch.link(nc.vector.tensor_tensor(state[:, :, :], state[:, :, :],
                                            bc(dis[:, :].unsqueeze(2), [P, BLOCKS, D]), ALU.mult))

        @block.scalar
        def _(act):
            act.wait_ge(deg_ready, 1)
            nc.scalar.activation(root[:, 1, :], root[:, 0, :], ACT.Sqrt).then_inc(root_ready, 1)


def gcn_close(nc, k, state, dis, bias, x):
    with ExitStack() as ctx:
        m = Mem(nc, ctx)
        step = m.sem("step")
        block = ctx.enter_context(nc.Block())

        @block.vector
        def _(dve):
            ch = Chain(dve, step)
            S, full = state[:, :, :], [P, BLOCKS, D]
            ch.link(nc.vector.tensor_tensor(S, S, bc(dis[:, :].unsqueeze(2), full), ALU.mult))
            ch.link(nc.vector.tensor_tensor(S, S, bc(bias[:, :].unsqueeze(1), full), ALU.add))
            ch.link(nc.vector.scalar_tensor_tensor(out=x[:, :, :].rearrange("p b d -> p (b d)"),
                                                   in0=state[:, :, :].rearrange("p b d -> p (b d)"), scalar=0.0,
                                                   in1=x[:, :, :].rearrange("p b d -> p (b d)"),
                                                   op0=ALU.max, op1=ALU.add))


def rel_tables(nc, k, h):
    with ExitStack() as ctx:
        m = Mem(nc, ctx)
        p_t = [m.ps(f"p_t{j}", [P, P]) for j in range(2)]
        p_s = [m.ps(f"p_s{j}", [P, OROW]) for j in range(2)]
        p_w = [m.ps(f"p_w{j}", [P, OROW]) for j in range(2)]
        staged = m.sb("staged", [P, 2, 2, D])
        stage_ready = m.sem("stage_ready")
        hT = m.sb("hT", [P, 2, P])
        rows = [m.sb(f"rows{j}", [P, TYPES, RROW]) for j in range(GROUP)]
        own = [m.sb(f"own{j}", [P, OROW]) for j in range(GROUP)]
        dummy = m.sb("dummy", [P, TYPES, RROW])
        tr, copied, made_s, made_w = m.sem("tr"), m.sem("copied"), m.sem("made_s"), m.sem("made_w")
        src_done, own_done = m.sem("src_done"), m.sem("own_done")
        half_done = m.sem("half_done")
        spread = [m.sem(f"spread{j}") for j in range(GROUP)]
        own_out = [m.sem(f"own_out{j}") for j in range(GROUP)]
        set_, dummy_out, tick = m.sem("set"), m.sem("dummy_out"), m.sem("tick")
        rows_free, own_free = m.sem("rows_free"), m.sem("own_free")
        block = ctx.enter_context(nc.Block())

        @block.tensor
        def _(pe):
            pe.wait_ge(copied, 1)
            with pe.Fori(0, TURNS) as t:
                for j in range(GROUP):
                    n, z = t * GROUP + j, j % 2
                    if z == 0:
                        pe.wait_ge(stage_ready, t * (GROUP // 2) + j // 2 + 1)
                        nc.tensor.transpose(p_t[(j // 2) % 2][:, :], staged[:, (j // 2) % 2, :, :]
                                            .rearrange("p b d -> p (b d)"), k.ident[:, :]).then_inc(tr, 1)
                        pe.wait_ge(copied, t * (GROUP // 2) + j // 2 + 2)
                    lhsT = hT[z * D:(z + 1) * D, (j // 2) % 2, :]
                    pe.wait_ge(src_done, n + 1)
                    nc.tensor.matmul(p_s[z][:, :], lhsT, k.w_src[z * D:(z + 1) * D, :],
                                     start=True, stop=True).then_inc(made_s, 1)
                    pe.wait_ge(own_done, n + 1)
                    nc.tensor.matmul(p_w[z][:, :], lhsT, k.w_own[z * D:(z + 1) * D, :],
                                     start=True, stop=True).then_inc(made_w, 1)

        @block.scalar
        def _(act):
            act.sem_inc(copied, 1)
            act.sem_inc(src_done, 2)
            with act.Fori(0, TURNS) as t:
                for j in range(GROUP):
                    n, z = t * GROUP + j, j % 2
                    if z == 0:
                        act.wait_ge(tr, t * (GROUP // 2) + j // 2 + 1)
                        nc.scalar.activation(hT[:, (j // 2) % 2, :], p_t[(j // 2) % 2][:, :], ACT.Copy)\
                            .then_inc(copied, 1)
                    act.wait_ge(made_s, n + 1)
                    act.wait_ge(rows_free, n + 1)
                    nc.scalar.activation(rows[j][:, :, 0:AW], bc(p_s[z][:, 0:AW].unsqueeze(1), [P, TYPES, AW]), ACT.Copy)
                    nc.scalar.activation(rows[j][:, :, AW:AW + D],
                                         p_s[z][:, AW:].rearrange("p (t d) -> p t d", t=TYPES), ACT.Copy)\
                        .then_inc(src_done, 1)

        @block.vector
        def _(dve):
            nc.vector.memset(dummy[:, :, :], 0.0).then_inc(set_, 1)
            dve.wait_ge(set_, 1)
            nc.vector.memset(dummy[:, :, D:AW], MINUS).then_inc(set_, 1)
            dve.sem_inc(own_done, 2)
            with dve.Fori(0, TURNS) as t:
                for j in range(GROUP):
                    n, z = t * GROUP + j, j % 2
                    dve.wait_ge(rows_free, n + 1)
                    nc.vector.tensor_scalar(rows[j][:, :, AW + D:RROW], bc(h[:, bass.ds(n, 1), :], [P, TYPES, D]), 0.5,
                                            None, ALU.mult).then_inc(half_done, 1)
                    dve.wait_ge(own_free, n + 1)
                    dve.wait_ge(made_w, n + 1)
                    nc.vector.tensor_tensor(own[j][:, :], p_w[z][:, :], k.own_bias[:, :], ALU.add)\
                        .then_inc(own_done, 1)

        @block.gpsimd
        def _(pool):
            pool.sem_inc(rows_free, GROUP)

            def stage(pair):
                z = pair % (GROUP // 2) % 2
                if pair >= 2:
                    pool.wait_ge(tr, pair - (pair % (GROUP // 2) > 0))
                nc.gpsimd.tensor_copy(staged[:, z, :, :], h[:, 2 * pair:2 * pair + 2, :]).then_inc(stage_ready, 1)

            stage(0)
            for b in range(BLOCKS):
                if b % 2 == 0 and b + 2 < BLOCKS:
                    stage(b // 2 + 1)
                pool.wait_ge(src_done, b + 3)
                pool.wait_ge(half_done, b + 1)
                pool.indirect_dma_start(k.rel_tab[0:NPAD, :], at(k.node_r[:, b:b + 1]),
                                        rows[b % GROUP][:, :, :].rearrange("p t c -> p (t c)"), None)\
                    .then_inc(spread[b % GROUP], 16)
                if b >= 4:
                    c = b - 4
                    pool.wait_ge(spread[c % GROUP], 16 * (c // GROUP + 1))
                    pool.sem_inc(rows_free, 1)
            for j in range(GROUP):
                pool.wait_ge(spread[j], 16 * TURNS)

        @block.sync
        def _(sp):
            sp.wait_ge(set_, 2)
            sp.dma_start(k.rel_tab[NPAD:ROWS, :], dummy[:, :, :].rearrange("p t c -> p (t c)")).then_inc(dummy_out, 16)
            sp.sem_inc(own_free, GROUP)
            with sp.Fori(0, TURNS) as t:
                for j in range(GROUP):
                    sp.wait_ge(own_done, t * GROUP + j + 3)
                    sp.sem_inc(tick, 1)
                    sp.dma_start(k.own_tab[bass.ds(t * GROUP + j, 1)].rearrange("a p c -> p (a c)"), own[j][:, :])\
                        .then_inc(own_out[j], 16)
                    if j % 2:
                        for c in (j - 1, j):
                            sp.wait_ge(own_out[c], t * 16 + 16)
                            sp.sem_inc(own_free, 1)
            sp.wait_ge(dummy_out, 16)


def rel_edges(nc, k, state, top):
    AHEAD, LATE = 1, 2
    with ExitStack() as ctx:
        m = Mem(nc, ctx)
        r = ring_buffers(m, RROW, stages=RING)
        codes = m.sb("codes_of_turn", [P, RING, SLOTS], I32)
        own = m.sb("own", [P, RING, OROW])
        is_t = m.sb("is_t", [P, 3, RING, SLOTS], I32)
        feat, relu = m.sb("feat", [P, RING, SLOTS, D]), m.sb("relu", [P, RING, SLOTS, D])
        score = m.sb("score", [P, RING, SLOTS, AW])
        e = m.sb("e", [P, RING, SLOTS + 1])
        gate, th = m.sb("gate", [P, RING, SLOTS, D]), m.sb("th", [P, RING, SLOTS, D])
        value = m.sb("value", [P, RING, SLOTS, D])
        msg = m.sb("msg", [P, RING, SLOTS + 1, AW])
        p_gate = [m.ps(f"p_gate{z}", [P, SLOTS, D]) for z in range(2)]
        p_part = [m.ps(f"p_part{z}", [P, AW]) for z in range(2)]
        own_in = [m.sem(f"own_in{q}") for q in range(RING)]
        own_free = [m.sem(f"own_free{q}") for q in range(RING)]
        feat_ready, relu_ready, first_ready = m.sem("feat_ready"), m.sem("relu_ready"), m.sem("first_ready")
        e_ready, p_ready, value_ready = m.sem("e_ready"), m.sem("p_ready"), m.sem("value_ready")
        own_gate, gate_ready, th_ready = m.sem("own_gate"), m.sem("gate_ready"), m.sem("th_ready")
        codes_in, codes_used, start = m.sem("codes_in"), m.sem("codes_used"), m.sem("start")
        msg_ready, part_ready, added = m.sem("msg_ready"), m.sem("part_ready"), m.sem("added")
        block = ctx.enter_context(nc.Block())

        @block.sync
        def _(sp):
            n = turns(sp, k)
            with sp.Fori(0, n) as i:
                sp.wait_ge(r.meta_used, i * 2 + 2)
                sp.sem_inc(r.tick, 1)
                sp.dma_start(r.meta[:, :], k.chunk_tab[bass.ds(i * RING, RING), 0, CROW - 1:CROW]
                             .rearrange("a c -> c a"), allow_slow_non_contiguous=True).then_inc(r.meta_in, 16)
                b = turn_blocks(nc, sp, [mybir.EngineType.SP], r, i)
                sp.wait_ge(codes_used, i + 1)
                sp.sem_inc(r.tick, 1)
                sp.dma_start(codes[:, :, :], k.chunk_tab[bass.ds(i * RING, RING), :, SLOTS:2 * SLOTS]
                             .rearrange("a p c -> p a c")).then_inc(codes_in, 16)

                def load_list(q):
                    sp.wait_ge(r.landed[q], i * 64)
                    sp.sem_inc(r.tick, 1)
                    sp.dma_start(r.lists[q][:, :, :], k.chunk_tab[bass.ds(i * RING + q, 1), :, SLOTS:2 * SLOTS]
                                 .rearrange("a p c -> p a c")).then_inc(r.list_in[q], 16)

                def load_own(q):
                    sp.wait_ge(own_free[q], i + 1)
                    sp.sem_inc(r.tick, 1)
                    sp.dma_start(own[:, q, :], k.own_tab[bass.ds(b[q], 1)].rearrange("a p c -> p (a c)"))\
                        .then_inc(own_in[q], 16)

                load_list(0)
                for q in range(1, RING):
                    load_list(q)
                    load_own(q - 1)
                load_own(RING - 1)

        @block.gpsimd
        def _(pool):
            gather_all(nc, pool, k, r, k.rel_tab.rearrange("n (t c) -> (n t) c", t=TYPES))

        @block.vector
        def _(dve):
            n = turns(dve, k)
            ring_credits(dve, r, readers=2, free=RING - 1)
            for q in range(RING - 1):
                dve.sem_inc(own_free[q], 1)
            dve.sem_inc(codes_used, 1)
            regs = [dve.alloc_register(f"rel_block{q}") for q in range(RING + 1)]
            for reg in regs:
                dve.reg_mov(reg, 0)
            b = [bass.RuntimeValue.of_register_unchecked(reg, min_val=0, max_val=BLOCKS - 1) for reg in regs]
            nc.vector.memset(th[:, RING - 1, :, :], 0.0).then_inc(start, 1)
            nc.vector.memset(value[:, RING - 1, :, :], 0.0).then_inc(start, 1)
            nc.vector.memset(msg[:, RING - 2:RING, :, :], 0.0).then_inc(start, 1)
            dve.wait_ge(start, 3)
            nc.vector.memset(msg[:, RING - 2:RING, SLOTS, D:AW], 1.0).then_inc(start, 1)
            dve.wait_ge(start, 4)
            dve.sem_inc(start, 1)
            dve.sem_inc(msg_ready, 1)
            def gated(q):
                nc.vector.scalar_tensor_tensor(out=msg[:, q, 0:SLOTS, 0:D], in0=th[:, q, :, :], scalar=1.0,
                                               in1=value[:, q, :, :], op0=ALU.add, op1=ALU.mult)\
                    .then_inc(msg_ready, 1)

            def add_part(q, blk):
                row = state[:, bass.ds(blk, 1), :].rearrange("p b f -> p (b f)")
                nc.vector.scalar_tensor_tensor(out=row, in0=row, scalar=msg[:, q, SLOTS, D:AW],
                                               in1=p_part[q % 2][:, :], op0=ALU.mult, op1=ALU.add)\
                    .then_inc(added, 1)

            with dve.Fori(0, n) as i:
                dve.sem_clear(r.turn_step)
                ts = Chain(dve, r.turn_step)
                at_chunk = lambda q: i * RING + q + 1

                def types():
                    dve.wait_ge(codes_in, i * 16 + 16)
                    for t in range(2):
                        ts.add(nc.vector.tensor_single_scalar(is_t[:, t, :, :], codes[:, :, :], 1 + t,
                                                              ALU.bitwise_and))
                    ts.wait()
                    dve.sem_inc(codes_used, 1)
                    ts.link(nc.vector.tensor_tensor(is_t[:, 2, :, :], is_t[:, 0, :, :], is_t[:, 1, :, :], ALU.mult))

                def features(q):
                    z = q % 2
                    dve.wait_ge(r.landed[q], i * 64 + 64)
                    dve.wait_ge(own_in[q], i * 16 + 16)
                    nc.vector.tensor_tensor(feat[:, q, :, :], r.got[:, q, :, 0:D],
                                            bc(own[:, q, 0:D].unsqueeze(1), [P, SLOTS, D]), ALU.add)\
                        .then_inc(feat_ready, 1)

                def own_part(q, t):
                    ins = nc.vector.copy_predicated(gate[:, q, :, :],
                                                    bc(is_t[:, t, q, :].unsqueeze(2), [P, SLOTS, D]),
                                                    bc(own[:, q, AW + (t + 1) * D:AW + (t + 2) * D].unsqueeze(1),
                                                       [P, SLOTS, D]))
                    if t == TYPES - 2:
                        ins.then_inc(own_gate, 1)
                        return 0
                    return ts.add(ins)

                def scores(q):
                    blk = bass.ds(b[q], 1)
                    ts.add(nc.vector.tensor_copy(e[:, q, SLOTS:SLOTS + 1], top[:, blk]))
                    ts.add(nc.vector.tensor_tensor(score[:, q, :, D], r.got[:, q, :, D],
                                                   bc(own[:, q, D:AW], [P, SLOTS]), ALU.add))
                    dve.wait_ge(relu_ready, at_chunk(q))
                    return ts.add(nc.vector.tensor_tensor(score[:, q, :, 0:D], relu[:, q, :, :],
                                                          bc(k.att_a99[:, :].unsqueeze(1), [P, SLOTS, D]), ALU.mult))

                def score_sums(q, after):
                    ts.wait(after)
                    return ts.add(nc.vector.tensor_reduce(e[:, q, 0:SLOTS], score[:, q, :, :], AX, ALU.add))

                def maxima(q, after):
                    ts.wait(after)
                    return ts.add(nc.vector.tensor_reduce(top[:, bass.ds(b[q], 1)], e[:, q, :], AX, ALU.max))

                def below_top(q, after):
                    ts.wait(after)
                    nc.vector.tensor_tensor(e[:, q, :], e[:, q, :], bc(top[:, bass.ds(b[q], 1)], [P, SLOTS + 1]),
                                            ALU.subtract).then_inc(e_ready, 1)

                def messages(q, number):
                    dve.wait_ge(value_ready, i * RING + (number + 1 + AHEAD))
                    dve.wait_ge(th_ready, i * RING + (number + 1 + AHEAD))
                    dve.sem_inc(r.got_free[q], 1)
                    dve.sem_inc(own_free[q], 1)
                    gated(q)

                def accumulate(q, number):
                    dve.wait_ge(part_ready, i * RING + (number + 1 + LATE))
                    if number > -2:
                        dve.wait_ge(added, i * RING + (number + LATE))
                    add_part(q, b[RING] if number == -1 else b[q])

                def own_start(q):
                    dve.wait_ge(first_ready, at_chunk(q))
                    dve.sem_inc(r.tick, 1)
                    return own_part(q, 0)

                types()
                features(0)
                accumulate(RING - 2, -2)
                dve.reg_mov(regs[RING], regs[RING - 1])
                dve.wait_ge(r.meta_in, i * 16 + 16)
                dve.sem_inc(r.tick, 1)
                dve.reg_load(regs[0:RING], r.meta[0:1, 0:RING])
                dve.sem_inc(r.meta_used, 1)
                n0 = own_start(0)
                messages(RING - 1, -1)
                ts.wait(n0)
                n1 = own_part(0, 1)
                ts.wait(n1)
                own_part(0, 2)
                for q in range(RING):
                    nxt = q + 1 < RING
                    if nxt:
                        features(q + 1)
                    n_s = scores(q)
                    if nxt:
                        n0 = own_start(q + 1)
                    n_e = score_sums(q, n_s)
                    if nxt:
                        ts.wait(n0)
                        n1 = own_part(q + 1, 1)
                    n_m = maxima(q, n_e)
                    if q:
                        accumulate((q - 2) % RING, q - 2)
                    below_top(q, n_m)
                    if q:
                        messages(q - 1, q - 1)
                    if nxt:
                        ts.wait(n1)
                        own_part(q + 1, 2)
                dve.sem_inc(r.tick, 1)
            dve.wait_ge(part_ready, n * RING + (LATE - 1))
            add_part(RING - 2, b[RING - 2])
            dve.wait_ge(value_ready, n * RING + AHEAD)
            dve.wait_ge(th_ready, n * RING + AHEAD)
            gated(RING - 1)
            dve.wait_ge(part_ready, n * RING + LATE)
            dve.wait_ge(added, n * RING + (LATE - 1))
            add_part(RING - 1, b[RING - 1])
            dve.wait_ge(added, n * RING + LATE)
            dve.sem_inc(r.tick, 1)

        @block.scalar
        def _(act):
            n = turns(act, k)
            act.wait_ge(start, 5)
            act.sem_inc(value_ready, AHEAD)
            act.sem_inc(th_ready, AHEAD)
            with act.Fori(0, n) as i:
                def first_types(q):
                    act.wait_ge(own_in[q], i * 16 + 16)
                    nc.scalar.activation(gate[:, q, :, :],
                                         bc(own[:, q, AW:AW + D].unsqueeze(1), [P, SLOTS, D]), ACT.Copy)\
                        .then_inc(first_ready, 1)

                def relus(q):
                    act.wait_ge(feat_ready, i * RING + q + 1)
                    nc.scalar.activation(relu[:, q, :, :], feat[:, q, :, :], ACT.Relu).then_inc(relu_ready, 1)

                def weights(q):
                    z = q % 2
                    act.wait_ge(e_ready, i * RING + q + 1)
                    nc.scalar.activation(msg[:, q, :, D], e[:, q, :], ACT.Exp).then_inc(p_ready, 1)
                    act.wait_ge(p_ready, i * RING + q + 1)
                    for j in range(SLOTS):
                        last = nc.scalar.activation(value[:, q, j, :], r.got[:, q, j, AW + D:RROW], ACT.Copy,
                                                    scale=msg[:, q, j, D:AW])
                    last.then_inc(value_ready, 1)

                def tanhs(q):
                    act.wait_ge(gate_ready, i * RING + q + 1)
                    nc.scalar.activation(th[:, q, :, :], p_gate[q % 2][:, :, :], ACT.Tanh, scale=0.5)\
                        .then_inc(th_ready, 1)

                first_types(0)
                relus(0)
                first_types(1)
                for q in range(RING):
                    if q + 1 < RING:
                        relus(q + 1)
                    if q + 2 < RING:
                        first_types(q + 2)
                    weights(q)
                    tanhs(q)

        @block.tensor
        def _(pe):
            n = turns(pe, k)

            def add_up(q):
                for j in range(SLOTS):
                    last = nc.tensor.matmul(p_part[q % 2][:, :], k.ident[:, :], msg[:, q, j, :], start=(j == 0),
                                            stop=(j == SLOTS - 1))
                last.then_inc(part_ready, 1)

            pe.wait_ge(msg_ready, 1)
            add_up(RING - 2)
            with pe.Fori(0, n) as i:
                def gates(q):
                    z = q % 2
                    pe.wait_ge(own_gate, i * RING + q + 1)
                    pe.wait_ge(th_ready, i * RING + (q - 1 + AHEAD))
                    nc.tensor.matmul(p_gate[z][:, :, :], k.ident[:, :], r.got[:, q, :, AW:AW + D], start=True,
                                     stop=False)
                    nc.tensor.matmul(p_gate[z][:, :, :], k.ident[:, :], gate[:, q, :, :], start=False, stop=True)\
                        .then_inc(gate_ready, 1)

                def parts(q, number):
                    pe.wait_ge(msg_ready, i * RING + (number + 1 + LATE))
                    pe.wait_ge(added, i * RING + (number - 1 + LATE))
                    add_up(q)

                parts(RING - 1, -1)
                gates(0)
                gates(1)
                for q in range(RING - 1):
                    parts(q, q)
                    if q + 2 < RING:
                        gates(q + 2)
            pe.wait_ge(msg_ready, n * RING + LATE)
            add_up(RING - 1)


def rel_close(nc, k, h, state, x, out):
    with ExitStack() as ctx:
        m = Mem(nc, ctx)
        den, inv = m.sb("den", [P, BLOCKS]), m.sb("inv", [P, BLOCKS])
        hn = m.sb("hn", [P, BLOCKS, D])
        p_t = [m.ps(f"p_t{j}", [P, 2, P]) for j in range(2)]
        p_o = [m.ps(f"p_o{j}", [P, 2, 512]) for j in range(2)]
        staged = m.sb("staged", [P, 2, 2, 2, D])
        stage_ready = m.sem("stage_ready")
        hT = m.sb("hT", [P, 2, 2, P])
        lin = m.sb("lin", [P, 2, 2, D])
        step, hn_ready = m.sem("step"), m.sem("hn_ready")
        tr, copied, made, read, stored, spread = (m.sem("tr"), m.sem("copied"), m.sem("made"), m.sem("read"),
                                                  m.sem("stored"), m.sem("spread"))
        turn_step = m.sem("turn_step")
        block = ctx.enter_context(nc.Block())
        PAIRS, TP = BLOCKS // 2, 7

        @block.vector
        def _(dve):
            ch = Chain(dve, step)
            ch.link(nc.vector.tensor_scalar(den[:, :], state[:, :, D], 1e-30, None, ALU.max))
            ch.link(nc.vector.reciprocal(inv[:, :], den[:, :]))
            nc.vector.tensor_tensor(hn[:, :, :], state[:, :, 0:D], bc(inv[:, :].unsqueeze(2), [P, BLOCKS, D]),
                                    ALU.mult).then_inc(hn_ready, 1)
            dve.sem_inc(read, 2)
            with dve.Fori(0, PAIRS // TP) as t:
                dve.sem_clear(turn_step)
                ts = Chain(dve, turn_step)
                for j in range(TP):
                    n, z = t * TP + j, j % 2
                    L = lin[:, z, :, :].rearrange("p b d -> p (b d)")
                    xb = x[:, bass.ds(n * 2, 2), :].rearrange("p b d -> p (b d)")
                    dve.wait_ge(made, n + 1)
                    ts.link(nc.vector.tensor_tensor(lin[:, z, :, :], p_o[z][:, :, 0:D],
                                                    bc(k.vec["L3_gnn_lin_b"][:, :].unsqueeze(1), [P, 2, D]), ALU.add))
                    dve.sem_inc(read, 1)
                    ts.link(nc.vector.scalar_tensor_tensor(out=L, in0=L, scalar=0.01, in1=L, op0=ALU.mult,
                                                           op1=ALU.max))
                    nc.vector.tensor_tensor(xb, xb, L, ALU.add).then_inc(stored, 1)
                    dve.wait_ge(stored, n + 1)

        @block.tensor
        def _(pe):
            pe.wait_ge(hn_ready, 1)
            with pe.Fori(0, PAIRS // TP) as t:
                for j in range(TP):
                    n, z = t * TP + j, j % 2
                    pe.wait_ge(read, n + (1 if j else 2))
                    pe.wait_ge(stage_ready, n * 2 + 2)
                    for w in range(2):
                        last = nc.tensor.transpose(p_t[z][:, w, :], staged[:, z, w, :, :]
                                                   .rearrange("p b d -> p (b d)"), k.ident[:, :])
                    last.then_inc(tr, 1)
                    pe.wait_ge(copied, n + 1)
                    for y in range(2):
                        for w in range(2):
                            last = nc.tensor.matmul(p_o[z][:, y, 0:D], hT[y * D:(y + 1) * D, z, w, :],
                                                    k.w_lin[y * D:(y + 1) * D, w, :], start=(w == 0), stop=(w == 1))
                    last.then_inc(made, 1)

        @block.scalar
        def _(act):
            with act.Fori(0, PAIRS // TP) as t:
                for j in range(TP):
                    act.wait_ge(tr, t * TP + j + 1)
                    nc.scalar.activation(hT[:, j % 2, :, :], p_t[j % 2][:, :, :], ACT.Copy).then_inc(copied, 1)

        @block.gpsimd
        def _(pool):
            def stage(pair):
                z = pair % (GROUP // 2) % 2
                if pair >= 2:
                    pool.wait_ge(tr, pair - (pair % (GROUP // 2) > 0))
                for w, buf in enumerate((h, hn)):
                    nc.gpsimd.tensor_copy(staged[:, z, w, :, :], buf[:, 2 * pair:2 * pair + 2, :])\
                        .then_inc(stage_ready, 1)

            pool.wait_ge(hn_ready, 1)
            stage(0)
            for b in range(BLOCKS):
                if b % 2 == 0 and b + 2 < BLOCKS:
                    stage(b // 2 + 1)
                pool.wait_ge(stored, b // 2 + 1)
                pool.indirect_dma_start(out, at(k.node_r[:, b:b + 1]), x[:, b, :], None, bounds_check=N - 1,
                                        oob_is_err=False).then_inc(spread, 16)
            pool.wait_ge(spread, 16 * BLOCKS)


def gnn_program(nc, a, out):
    ctx = ExitStack()
    with ctx:
        k = type("Kept", (), {})()
        m = Mem(nc, ctx)
        k.ident, k.ones, k.before = m.sb("ident", [P, P]), m.sb("ones", [P, P]), m.sb("before", [P, P])
        k.zeros = m.sb("zeros", [P, 2 * D])
        k.iota_i, k.iota = m.sb("iota_i", [P, P], I32), m.sb("iota", [P, P])
        k.node_i = m.sb("node_i", [P, BLOCKS], I32)
        k.dummy_i, k.dummy, k.dummy4 = m.sb("dummy_i", [P, 1], I32), m.sb("dummy_row", [P, 1]), m.sb("dummy4", [P, 1])
        k.deg, k.deg_r = m.sb("deg", [P, BLOCKS]), m.sb("deg_r", [P, BLOCKS])
        k.node_r = m.sb("node_r", [P, BLOCKS], I32)
        k.ctl_i, k.row_i = m.sb("ctl_i", [1, 8], I32), m.sb("row_i", [1, 4, BLOCKS], I32)
        k.const_ready = m.sem("const_ready")

        def dram(name, shape, dt=F32):
            return nc.dram_tensor(name, shape, dt, kind="Internal").ap()

        k.codes = dram("codes", [E + WIDE], I32)
        k.runs = dram("runs", [E, WIDE], I32)
        k.info_tab = dram("info_tab", [NPAD, 4], I32)
        k.chunk_tab = dram("chunk_tab", [CHUNKS, P, CROW], I32)
        k.hn_tab, k.hh_tab = dram("hn_tab", [ROWS, D]), dram("hh_tab", [NPAD, 2 * D])
        k.sums = [dram(f"sums{j}", [ROWS, D + 1]) for j in range(SLOTS)]
        k.x1_tab = dram("x1_tab", [NPAD, D])
        k.gat1_tab = dram("gat1_tab", [ROWS, H1 * (C1 + 2)])
        k.gat2_tab = dram("gat2_tab", [ROWS, D + 2])
        k.gcn_tab = dram("gcn_tab", [ROWS, D])
        k.rel_tab = dram("rel_tab", [ROWS, TYPES * RROW])
        k.own_tab = dram("own_tab", [BLOCKS, P, OROW])
        k.w_gat1, k.w_gat2 = m.sb("w_gat1", [P, H1 * (C1 + 3)]), m.sb("w_gat2", [P, D + 3])
        k.w_gcn = m.sb("w_gcn", [P, D])
        k.w_src, k.w_own = m.sb("w_src", [P, OROW]), m.sb("w_own", [P, OROW])
        k.w_lin = m.sb("w_lin", [P, 2, D])
        k.att_a, k.att_a99 = m.sb("att_a", [P, D]), m.sb("att_a99", [P, D])
        k.own_bias = m.sb("own_bias", [P, OROW])
        k.vec = {n: m.sb("v_" + n, [P, D]) for n in _VECS}
        constants(nc, k)
        count_and_open(nc, k, a)
        rank_nodes(nc, k)
        build_chunks(nc, k)
        layers(nc, k, a, out)


def clear(nc, pairs):
    with ExitStack() as ctx:
        cleared = Mem(nc, ctx).sem("cleared")
        block = ctx.enter_context(nc.Block())

        @block.vector
        def _(dve):
            for buf, value in pairs:
                nc.vector.memset(buf, value).then_inc(cleared, 1)
            dve.wait_ge(cleared, len(pairs))


def layers(nc, k, a, out):
    load_weights(nc, k, a)
    with ExitStack() as ctx:
        m = Mem(nc, ctx)
        own_hn, own_v = m.sb("own_hn", [P, BLOCKS, D]), m.sb("own_v", [P, BLOCKS, D + 1])
        fetch_rows(nc, k, k.hh_tab, 2 * D, [(own_v, 0, D), (own_hn, D, D)])
        clear(nc, [(own_v[:, :, D:D + 1], 1.0)])
        cosine_edges(nc, k, own_hn, own_v)
    cosine_close(nc, k, a)
    with ExitStack() as ctx:
        m = Mem(nc, ctx)
        x, h = m.sb("x", [P, BLOCKS, D]), m.sb("h", [P, BLOCKS, D])
        fetch_rows(nc, k, k.x1_tab, D, [(x, 0, D)])
        open_layer(nc, k, x, h)
        for step, heads, c, w, tab, res in ((1, H1, C1, k.w_gat1, k.gat1_tab, None), (2, 1, D, k.w_gat2, k.gat2_tab, x)):
            HW = heads * (c + 1)
            with ExitStack() as ctx2:
                m2 = Mem(nc, ctx2)
                state = m2.sb(f"state{step}", [P, BLOCKS, HW + 2 * heads])
                own_dst, top = m2.sb(f"own_dst{step}", [P, BLOCKS, heads]), m2.sb(f"top{step}", [P, BLOCKS, heads])
                project(nc, k, h, w, HW + 2 * heads, state)
                gat_open(nc, k, heads, c, state, own_dst, top)
                spread_rows(nc, k, state, HW + heads, tab, HW)
                gat_edges(nc, k, heads, c, state, top, own_dst, tab)
                v = lambda n: k.vec["L1_gnn_" + n]
                gat_close(nc, k, heads, c, state, v(f"b{step}"), v(f"ln{step}_g"), v(f"ln{step}_b"), h, res)
        open_layer(nc, k, x, h)
        with ExitStack() as ctx2:
            m2 = Mem(nc, ctx2)
            state, dis = m2.sb("gcn_state", [P, BLOCKS, D]), m2.sb("dis", [P, BLOCKS])
            project(nc, k, h, k.w_gcn, D, state)
            gcn_scale(nc, k, state, dis)
            spread_rows(nc, k, state, D, k.gcn_tab, None)
            gcn_edges(nc, k, state, k.gcn_tab)
            gcn_close(nc, k, state, dis, k.vec["L2_gnn_b"], x)
        open_layer(nc, k, x, h)
        rel_tables(nc, k, h)
        with ExitStack() as ctx2:
            m2 = Mem(nc, ctx2)
            state, top = m2.sb("rel_state", [P, BLOCKS, AW]), m2.sb("rel_top", [P, BLOCKS])
            clear(nc, [(state[:, :, :], 0.0), (top[:, :], MINUS)])
            rel_edges(nc, k, state, top)
            rel_close(nc, k, h, state, x, out)


_VECS = ["L1_gnn_b1", "L1_gnn_b2", "L1_gnn_ln1_g", "L1_gnn_ln1_b", "L1_gnn_ln2_g", "L1_gnn_ln2_b", "L2_gnn_b",
         "L3_gnn_Wa_b", "L3_gnn_lin_b"]
_INS = ["x", "src", "dst", "edge_type_4", "L1_gnn_W1", "L1_gnn_a1_src", "L1_gnn_a1_dst", "L1_gnn_W2",
        "L1_gnn_a2_src", "L1_gnn_a2_dst", "L2_gnn_W", "L3_gnn_r", "L3_gnn_a", "L3_gnn_Wa_w", "L3_gnn_lin_w"] + _VECS


def kernel(**inputs):
    import numpy as _np
    import concourse.bacc as _bacc
    from concourse import mybir as _mybir
    from concourse.bass_utils import run_bass_kernel_spmd as _run

    nc = _bacc.Bacc("TRN2", target_bir_lowering=False, num_devices=1)
    arrays, args = {}, {}
    for name in _INS:
        arr = _np.ascontiguousarray(inputs[name])
        arrays[f"in_{name}_dram"] = arr
        args[name] = nc.dram_tensor(f"in_{name}_dram", arr.shape, _mybir.dt.from_np(arr.dtype),
                                    kind="ExternalInput").ap()
    out = nc.dram_tensor("out_dram", (N, D), F32, kind="ExternalOutput").ap()
    gnn_program(nc, args, out)
    r = _run(nc, [arrays], core_ids=[0])
    return r.results[0]["out_dram"]
```

```python
from contextlib import ExitStack

import concourse.bass as bass
from concourse import mybir

F32, BF16, I32 = mybir.dt.float32, mybir.dt.bfloat16, mybir.dt.int32
ALU = mybir.AluOpType
ACT = mybir.ActivationFunctionType
AX = mybir.AxisListType.X
DVE = [mybir.EngineType.DVE]

N, E, D, TYPES = 12500, 212500, 64, 4
P = 128
BLOCKS = -(-N // P)
NPAD = BLOCKS * P
ROWS = NPAD + P
SLOTS = 4
RING = 4
STAGES = 2
PER_STAGE = RING // STAGES
WIDE = 32
WCH = WIDE // SLOTS
LEAST = 2
CHUNKS = E // SLOTS + LEAST * BLOCKS + 16
CROW = 2 * SLOTS + 1
SHORT = 2
SHORT_AT = CHUNKS
UNUSED_AT = BLOCKS + 16
TABLE = SHORT_AT + UNUSED_AT + BLOCKS
EP, EC = 125, 1700
NP_, NC = 125, 100
BINS = 64
H1, C1 = 4, 16
SLOPE, REL_SLOPE, LN_EPS, SM_EPS = 0.2, 0.01, 1e-5, 1e-16
MINUS = -1e30
WRITTEN = RING // LEAST
FIRST = BLOCKS - 42 * WRITTEN
WRITE_TURNS = (BLOCKS - FIRST) // WRITTEN
GROUP = 14
TURNS = BLOCKS // GROUP
AW = D + 1
RROW = AW + 2 * D
OROW = AW + TYPES * D


class Part:

    def __init__(self, slots, base, ctl, most, writes):
        self.slots, self.base, self.ctl, self.most, self.writes = slots, base, ctl, most, writes


PARTS = (Part(SLOTS, 0, 0, CHUNKS // RING - 2, True), Part(SHORT, SHORT_AT, 5, -(-BLOCKS // RING), False))


class Mem:

    def __init__(self, nc, ctx):
        self.nc, self.ctx = nc, ctx
        self.stage = nc.next_id()
        self.sems = []
        ctx.callback(self.close)

    def close(self):
        if self.sems:
            self.nc.clear_and_free_semaphores(self.sems)
            self.nc.all_engine_barrier()

    def name(self, name):
        return f"{name}_{self.stage}"

    def sb(self, name, shape, dt=F32):
        return self.ctx.enter_context(self.nc.sbuf_tensor(self.name(name), shape, dt))

    def ps(self, name, shape, dt=F32):
        return self.ctx.enter_context(self.nc.psum_tensor(self.name(name), shape, dt))

    def sem(self, name):
        self.sems.append(self.nc.alloc_semaphore(self.name(name)))
        return self.sems[-1]


class Chain:

    def __init__(self, eng, sem):
        self.eng, self.sem, self.n = eng, sem, 0

    def add(self, ins):
        ins.then_inc(self.sem, 1)
        self.n += 1
        return self.n

    def wait(self, n=None):
        self.eng.wait_ge(self.sem, self.n if n is None else n)

    def link(self, ins):
        self.add(ins)
        self.wait()


def chunk_at(nc, c):
    return nc.s_assert_within(c, 0, TABLE - 1, skip_runtime_bounds_check_because="CHUNKS holds "
                              "the chunks of any degrees: their blocks' largest add up to at most E")




def at(ap, axis=0):
    return bass.IndirectOffsetOnAxis(ap=ap, axis=axis)


def bc(ap, shape):
    return ap.to_broadcast(shape)


def constants(nc, k):
    with ExitStack() as ctx:
        made = Mem(nc, ctx).sem("const_made")
        block = ctx.enter_context(nc.Block())

        @block.gpsimd
        def _(pool):
            ch = Chain(pool, made)
            ch.add(pool.memset(k.ident[:, :], 0.0))
            ch.add(pool.memset(k.ones[:, :], 1.0))
            ch.add(pool.memset(k.before[:, :], 1.0))
            ch.add(pool.memset(k.zeros[:, :], 0.0))
            ch.add(pool.iota(k.iota_i[:, :], [[1, P]], base=0, channel_multiplier=0))
            ch.add(pool.iota(k.node_i[:, :], [[P, BLOCKS]], base=0, channel_multiplier=1))
            ch.link(pool.iota(k.dummy_i[:, :], [[0, 1]], base=NPAD, channel_multiplier=1))
            ch.add(pool.affine_select(out=k.ident[:, :], in_=k.ident[:, :], compare_op=ALU.not_equal,
                                      fill=1.0, base=0, pattern=[[-1, P]], channel_multiplier=1))
            ch.link(pool.affine_select(out=k.before[:, :], in_=k.before[:, :], compare_op=ALU.is_gt,
                                       fill=0.0, base=0, pattern=[[1, P]], channel_multiplier=-1))

        @block.vector
        def _(dve):
            dve.wait_ge(made, 9)
            nc.vector.tensor_copy(k.iota[:, :], k.iota_i[:, :]).then_inc(k.const_ready, 1)
            nc.vector.tensor_copy(k.dummy[:, :], k.dummy_i[:, :]).then_inc(k.const_ready, 1)
            nc.vector.tensor_scalar(k.dummy4[:, :], k.dummy_i[:, :], 4.0, None, ALU.mult)\
                .then_inc(k.const_ready, 1)
            dve.wait_ge(k.const_ready, 3)


def count_edges(nc, k, a):
    T = 34
    with ExitStack() as ctx:
        m = Mem(nc, ctx)
        src = m.sb("src_sb", [EP, EC], I32)
        dst = m.sb("dst_sb", [EP, EC], I32)
        typ = m.sb("typ_sb", [EP, EC], I32)
        lo_i = m.sb("lo_i", [EP, EC], I32)
        hi_i = m.sb("hi_i", [EP, EC], I32)
        lo = m.sb("lo", [EP, EC], BF16)
        hi = m.sb("hi", [EP, EC], BF16)
        digits = m.sb("digits", [EP, P, T], BF16)
        hot = m.sb("hot", [EP, 2, P + BLOCKS, T], BF16)
        zero_b = m.sb("zero_b", [P, P + BLOCKS], BF16)
        counts = m.ps("counts", [P, BLOCKS])
        dst_in, code_in = m.sem("dst_in"), m.sem("code_in")
        codes_out, runs_out = m.sem("codes_out"), m.sem("runs_out")
        step, codes_made = m.sem("dve_step"), m.sem("codes_made")
        hot_ready = [m.sem("hot_ready0"), m.sem("hot_ready1")]
        hot_used = [m.sem("hot_used0"), m.sem("hot_used1")]
        turn_step = m.sem("turn_step")
        counted = m.sem("counted")
        block = ctx.enter_context(nc.Block())

        @block.sync
        def _(sp):
            sp.dma_start(dst[:, :], a["dst"].rearrange("(p c) -> p c", p=EP)).then_inc(dst_in, 16)
            sp.dma_start(src[:, :], a["src"].rearrange("(p c) -> p c", p=EP)).then_inc(code_in, 16)
            sp.dma_start(typ[:, :], a["edge_type_4"].rearrange("(p c) -> p c", p=EP)).then_inc(code_in, 16)
            sp.wait_ge(codes_made, 1)
            sp.dma_start(k.codes[0:E].rearrange("(p c) -> p c", p=EP), src[:, :]).then_inc(codes_out, 16)
            sp.dma_start(k.codes[E:E + WIDE].rearrange("(a c) -> a c", a=1),
                         k.zeros[0:1, 0:WIDE].bitcast(I32)).then_inc(codes_out, 16)
            sp.wait_ge(codes_out, 32)
            overlapped = bass.AP(k.codes.tensor, 0, [[1, E], [1, WIDE]])
            sp.dma_start(k.runs[:, :], overlapped).then_inc(runs_out, 16)
            sp.wait_ge(runs_out, 16)

        @block.vector
        def _(dve):
            ch = Chain(dve, step)
            ch.add(nc.vector.tensor_copy(digits[:, :, :], bc(k.iota[0:EP, :].unsqueeze(2), [EP, P, T])))
            ch.add(nc.vector.memset(zero_b[:, :], 0.0))
            dve.wait_ge(dst_in, 16)
            ch.add(nc.vector.tensor_single_scalar(lo_i[:, :], dst[:, :], P - 1, ALU.bitwise_and))
            ch.link(nc.vector.tensor_single_scalar(hi_i[:, :], dst[:, :], 7, ALU.logical_shift_right))
            ch.add(nc.vector.tensor_copy(lo[:, :], lo_i[:, :]))
            ch.add(nc.vector.tensor_copy(hi[:, :], hi_i[:, :]))
            dve.wait_ge(code_in, 32)
            nc.vector.scalar_tensor_tensor(out=src[:, :], in0=src[:, :], scalar=float(TYPES), in1=typ[:, :],
                                           op0=ALU.mult, op1=ALU.add).then_inc(codes_made, 1)
            ch.wait()
            dve.sem_inc(hot_used[0], 1)
            dve.sem_inc(hot_used[1], 1)
            with dve.Fori(0, EC // (2 * T)) as i:
                for h in range(2):
                    cols = bass.ds(i * (2 * T) + h * T, T)
                    dve.wait_ge(hot_used[h], i + 1)
                    nc.vector.tensor_tensor(hot[:, h, 0:P, :], bc(lo[:, cols].unsqueeze(1), [EP, P, T]),
                                            digits[:, :, :], ALU.is_equal).then_inc(hot_ready[h], 1)
                    nc.vector.tensor_tensor(hot[:, h, P:P + BLOCKS, :],
                                            bc(hi[:, cols].unsqueeze(1), [EP, BLOCKS, T]),
                                            digits[:, 0:BLOCKS, :], ALU.is_equal).then_inc(hot_ready[h], 1)
            dve.wait_ge(counted, 1)
            ch.link(nc.vector.tensor_copy(k.deg[:, :], counts[:, :]))

        @block.tensor
        def _(pe):
            pe.wait_ge(step, 2)
            nc.tensor.matmul(counts[:, :], zero_b[0:EP, 0:P], zero_b[0:EP, P:P + BLOCKS], start=True, stop=False,
                             skip_group_check=True)
            with pe.Fori(0, EC // (2 * T)) as i:
                for h in range(2):
                    pe.wait_ge(hot_ready[h], i * 2 + 2)
                    for t in range(T):
                        last = nc.tensor.matmul(counts[:, :], hot[:, h, 0:P, t], hot[:, h, P:P + BLOCKS, t],
                                                start=False, stop=False, skip_group_check=True)
                    last.then_inc(hot_used[h], 1)
            nc.tensor.matmul(counts[:, :], zero_b[0:EP, 0:P], zero_b[0:EP, P:P + BLOCKS], start=False, stop=True,
                             skip_group_check=True).then_inc(counted, 1)


def relu_norm(nc, dve, ch, x, h, sq, st, shape, var_ready, std_ready, n):
    wide = lambda j: bc(st[:, j, :].unsqueeze(2), shape)
    ch.link(nc.vector.tensor_reduce(st[:, 0, :], x, AX, ALU.add))
    ch.link(nc.vector.tensor_scalar(st[:, 3, :], st[:, 0, :], 1.0 / D, None, ALU.mult))
    ch.link(nc.vector.tensor_tensor(h, x, wide(3), ALU.subtract))
    ch.link(nc.vector.tensor_tensor(sq, h, h, ALU.mult))
    ch.link(nc.vector.tensor_reduce(st[:, 0, :], sq, AX, ALU.add))
    nc.vector.tensor_scalar(st[:, 1, :], st[:, 0, :], 1.0 / D, LN_EPS, ALU.mult, ALU.add).then_inc(var_ready, 1)
    dve.wait_ge(std_ready, n)
    ch.link(nc.vector.reciprocal(st[:, 3, :], st[:, 2, :]))
    ch.link(nc.vector.tensor_scalar(sq, h, 0.0, None, ALU.max))
    ch.link(nc.vector.tensor_tensor(h, sq, wide(3), ALU.mult))


def rank_nodes(nc, k, a):
    with ExitStack() as ctx:
        m = Mem(nc, ctx)
        tot = m.sb("tot", [P, BLOCKS])
        incl = m.sb("incl", [P, BLOCKS])
        binned = m.sb("binned", [P, BLOCKS])
        same = m.sb("same", [P, BINS, BLOCKS])
        upto = m.sb("upto", [P, BINS, BLOCKS])
        cnt = m.sb("cnt", [P, BINS])
        cum = m.sb("cum", [P, BINS])
        btot = m.sb("btot", [P, BINS])
        off = m.sb("off", [P, BINS])
        rank = m.sb("rank", [P, BLOCKS])
        rank_i = m.sb("rank_i", [P, BLOCKS], I32)
        info = m.sb("info", [P, BLOCKS, 4], I32)
        p_tot = m.ps("p_tot", [P, BLOCKS])
        p_pre = m.ps("p_pre", [P, BLOCKS])
        p_btot = m.ps("p_btot", [P, BINS])
        p_bpre = m.ps("p_bpre", [P, BINS])
        step, summed, cnt_ready, bsummed = m.sem("step"), m.sem("summed"), m.sem("cnt_ready"), m.sem("bsummed")
        ranked, scattered = m.sem("ranked"), m.sem("scattered")
        xd = m.sb("xd", [NP_, NC, D])
        hh = m.sb("hh", [NP_, NC, 2 * D])
        sq = m.sb("sq", [NP_, NC, D])
        st = m.sb("st", [NP_, 4, NC])
        x_in, h_out, h_made = m.sem("x_in"), m.sem("h_out"), m.sem("h_made")
        var_ready, std_ready = m.sem("var_ready"), m.sem("std_ready")
        block = ctx.enter_context(nc.Block())

        @block.sync
        def _(sp):
            sp.dma_start(xd[:, :, :], a["x"].rearrange("(p c) d -> p c d", p=NP_)).then_inc(x_in, 16)
            sp.dma_start(k.hn_tab[N:N + P, :], k.zeros[:, 0:D]).then_inc(h_out, 16)
            sp.dma_start(k.hn_tab[N + P:ROWS, :], k.zeros[0:ROWS - N - P, 0:D]).then_inc(h_out, 16)
            sp.dma_start(k.hh_tab[N:NPAD, :], k.zeros[0:NPAD - N, 0:2 * D]).then_inc(h_out, 16)
            sp.dma_start(k.x1_tab[N:NPAD, :], k.zeros[0:NPAD - N, 0:D]).then_inc(h_out, 16)
            for s in range(SLOTS):
                sp.dma_start(k.sums[s].rearrange("(p c) d -> p c d", p=P),
                             bc(k.zeros[:, 0:D + 1].unsqueeze(1), [P, ROWS // P, D + 1])).then_inc(h_out, 16)
            sp.wait_ge(h_made, 1)
            sp.dma_start(k.hn_tab[0:N, :].rearrange("(p c) d -> p c d", p=NP_), sq[:, :, :]).then_inc(h_out, 16)
            sp.dma_start(k.hh_tab[0:N, :].rearrange("(p c) d -> p c d", p=NP_), hh[:, :, :]).then_inc(h_out, 16)
            sp.wait_ge(h_out, 16 * (6 + SLOTS))

        @block.scalar
        def _(act):
            for n in range(2):
                act.wait_ge(var_ready, n + 1)
                nc.scalar.activation(st[:, 2, :], st[:, 1, :], ACT.Sqrt).then_inc(std_ready, 1)

        @block.tensor
        def _(pe):
            nc.tensor.matmul(p_tot[:, :], k.ones[:, :], k.deg[:, :], start=True, stop=True)
            nc.tensor.matmul(p_pre[:, :], k.before[:, :], k.deg[:, :], start=True, stop=True).then_inc(summed, 1)
            pe.wait_ge(cnt_ready, 1)
            nc.tensor.matmul(p_btot[:, :], k.ones[:, :], cnt[:, :], start=True, stop=True)
            nc.tensor.matmul(p_bpre[:, :], k.before[:, :], cnt[:, :], start=True, stop=True).then_inc(bsummed, 1)

        @block.vector
        def _(dve):
            ch = Chain(dve, step)
            ch.link(nc.vector.tensor_scalar(binned[:, :], k.deg[:, :], float(BINS - 1), None, ALU.min))
            ch.link(nc.vector.tensor_tensor(same[:, :, :], bc(binned[:, :].unsqueeze(1), [P, BINS, BLOCKS]),
                                            bc(k.iota[:, 0:BINS].unsqueeze(2), [P, BINS, BLOCKS]), ALU.is_equal))
            ch.link(nc.vector.tensor_reduce(cnt[:, :], same[:, :, :], AX, ALU.add))
            dve.sem_inc(cnt_ready, 1)
            flat = same[:, :, :].rearrange("p v j -> p (v j)")
            ch.add(nc.vector.tensor_tensor_scan(upto[:, :, :].rearrange("p v j -> p (v j)"), flat, flat, 0.0,
                                                ALU.add, ALU.max))
            ch.link(nc.vector.tensor_tensor_scan(cum[:, :], cnt[:, :], cnt[:, :], 0.0, ALU.add, ALU.max))
            ch.link(nc.vector.tensor_tensor(off[:, :], cnt[:, :], cum[:, :], ALU.subtract))
            dve.wait_ge(bsummed, 1)
            ch.link(nc.vector.tensor_copy(btot[:, :], p_btot[:, :]))
            ch.link(nc.vector.tensor_tensor_scan(cum[:, :], btot[:, :], btot[:, :], 0.0, ALU.add, ALU.max))
            ch.link(nc.vector.tensor_tensor(cum[:, :], cum[:, :], btot[:, :], ALU.subtract))
            ch.link(nc.vector.tensor_tensor(off[:, :], off[:, :], cum[:, :], ALU.add))
            ch.link(nc.vector.tensor_tensor(off[:, :], off[:, :], p_bpre[:, :], ALU.add))
            ch.link(nc.vector.tensor_tensor(upto[:, :, :], upto[:, :, :],
                                            bc(off[:, :].unsqueeze(2), [P, BINS, BLOCKS]), ALU.add))
            ch.link(nc.vector.tensor_tensor(upto[:, :, :], upto[:, :, :], same[:, :, :], ALU.mult))
            ch.link(nc.vector.tensor_reduce(rank[:, :], upto[:, :, :].rearrange("p v j -> p j v"), AX, ALU.add))
            ch.link(nc.vector.tensor_scalar(rank_i[:, :], rank[:, :], -1.0, None, ALU.add))
            dve.wait_ge(summed, 1)
            ch.link(nc.vector.tensor_copy(tot[:, :], p_tot[:, :]))
            ch.link(nc.vector.tensor_tensor_scan(incl[:, :], tot[:, :], tot[:, :], 0.0, ALU.add, ALU.max))
            ch.link(nc.vector.tensor_tensor(incl[:, :], incl[:, :], tot[:, :], ALU.subtract))
            ch.add(nc.vector.tensor_tensor(info[:, :, 1], incl[:, :], p_pre[:, :], ALU.add))
            ch.add(nc.vector.tensor_copy(info[:, :, 0], k.node_i[:, :]))
            ch.add(nc.vector.tensor_copy(info[:, :, 2], k.deg[:, :]))
            ch.link(nc.vector.memset(info[:, :, 3], 0))
            dve.sem_inc(ranked, 1)
            dve.wait_ge(x_in, 16)
            h = hh[:, :, 0:D]
            relu_norm(nc, dve, ch, xd[:, :, :], h, sq[:, :, :], st, [NP_, NC, D], var_ready, std_ready, 1)
            ch.link(nc.vector.tensor_tensor(sq[:, :, :], h, h, ALU.mult))
            ch.link(nc.vector.tensor_reduce(st[:, 0, :], sq[:, :, :], AX, ALU.add))
            nc.vector.tensor_copy(st[:, 1, :], st[:, 0, :]).then_inc(var_ready, 1)
            dve.wait_ge(std_ready, 2)
            ch.link(nc.vector.tensor_scalar(st[:, 0, :], st[:, 2, :], 1e-12, None, ALU.max))
            ch.link(nc.vector.reciprocal(st[:, 3, :], st[:, 0, :]))
            ch.link(nc.vector.tensor_tensor(hh[:, :, D:2 * D], h, bc(st[:, 3, :].unsqueeze(2), [NP_, NC, D]),
                                            ALU.mult))
            nc.vector.tensor_copy(sq[:, :, :], hh[:, :, D:2 * D]).then_inc(h_made, 1)
            dve.wait_ge(h_made, 1)

        @block.gpsimd
        def _(pool):
            pool.wait_ge(ranked, 1)
            for j in range(BLOCKS):
                pool.indirect_dma_start(k.info_tab[:, :], at(rank_i[:, j:j + 1]), info[:, j, :], None)\
                    .then_inc(scattered, 16)
            pool.wait_ge(scattered, 16 * BLOCKS)


def build_chunks(nc, k):
    with ExitStack() as ctx:
        m = Mem(nc, ctx)
        info = m.sb("info_r", [P, BLOCKS, 4], I32)
        first = m.sb("first", [P, BLOCKS])
        first_i = m.sb("first_i", [P, BLOCKS], I32)
        wide = m.sb("wide", [P, BLOCKS, WIDE], I32)
        valid = m.sb("valid", [P, BLOCKS, WIDE])
        code = m.sb("code", [P, BLOCKS, WIDE])
        code_i = m.sb("code_i", [P, BLOCKS, WIDE], I32)
        rows = k.rows
        tail = m.sb("tail", [P, 1, CROW], I32)
        dmax = m.sb("dmax", [BLOCKS, 5])
        nch2_i = m.sb("nch2_i", [BLOCKS, 1], I32)
        nch = m.sb("nch", [BLOCKS, 3])
        nch_i = m.sb("nch_i", [BLOCKS, 1], I32)
        row = m.sb("row", [1, 8, BLOCKS])
        unused = m.sb("unused", [1, BLOCKS])
        one = m.sb("one", [1, BLOCKS])
        ctl = m.sb("ctl", [1, 8])
        x_first = m.sb("x_first", [P, 1])
        x_first_i = m.sb("x_first_i", [P, 1], I32)
        x_wide = m.sb("x_wide", [P, WIDE], I32)
        x_valid = m.sb("x_valid", [P, SLOTS])
        x_code = m.sb("x_code", [P, SLOTS])
        x_code_i = m.sb("x_code_i", [P, SLOTS], I32)
        x_pos = m.sb("x_pos", [P, 1])
        x_row = m.sb("x_row", [P, 1, CROW], I32)
        p_deg = m.ps("p_deg", [BLOCKS, P])
        p_start = m.ps("p_start", [BLOCKS, 2])
        p_row = m.ps("p_row", [1, 4, BLOCKS])
        info_in, step, deg_ready, degT = m.sem("info_in"), m.sem("step"), m.sem("deg_ready"), m.sem("degT")
        nch_ready, start_ready, cols_ready, rows_ready = (m.sem("nch_ready"), m.sem("start_ready"),
                                                          m.sem("cols_ready"), m.sem("rows_ready"))
        first_ready, wide_in, blocks_ready = m.sem("first_ready"), m.sem("wide_in"), m.sem("blocks_ready")
        chunk_rows = m.sem("chunk_rows")
        x_asked, x_in, x_made, x_out, x_turn = (m.sem("x_asked"), m.sem("x_in"), m.sem("x_made"), m.sem("x_out"),
                                                m.sem("x_turn"))
        tail_out, in_row, x_step, tick = m.sem("tail_out"), m.sem("in_row"), m.sem("x_step"), m.sem("tick")
        block = ctx.enter_context(nc.Block())

        @block.gpsimd
        def _(pool):
            pool.iota(rows[:, :, :, CROW - 1], [[1, BLOCKS], [0, WCH]], base=0, channel_multiplier=0)\
                .then_inc(blocks_ready, 1)
            pool.wait_ge(first_ready, 1)
            for b in range(BLOCKS):
                pool.indirect_dma_start(wide[:, b, :], None, k.runs[:, :], at(first_i[:, b:b + 1])).then_inc(wide_in, 16)
            pool.wait_ge(rows_ready, 1)
            n_x = pool.value_load(k.ctl_i[0:1, 3:4], min_val=1, max_val=CHUNKS)
            with pool.Fori(0, n_x) as t:
                pool.wait_ge(x_asked, t + 1)
                pool.sem_inc(x_turn, 1)
                pool.indirect_dma_start(x_wide[:, :], None, k.runs[:, :], at(x_first_i[:, :])).then_inc(x_in, 16)

        @block.tensor
        def _(pe):
            pe.wait_ge(deg_ready, 1)
            nc.tensor.transpose(p_deg[:, :], k.deg_r[:, :], k.ident[:, :]).then_inc(degT, 1)
            pe.wait_ge(nch_ready, 1)
            nc.tensor.matmul(p_start[:, :], k.before[0:BLOCKS, 0:BLOCKS], dmax[:, 1:3], start=True, stop=True)\
                .then_inc(start_ready, 1)
            pe.wait_ge(cols_ready, 1)
            for j in range(4):
                last = nc.tensor.matmul(p_row[:, j, :], dmax[:, 1 + j:2 + j], k.ident[0:BLOCKS, 0:BLOCKS],
                                        start=True, stop=True)
            last.then_inc(in_row, 1)

        @block.vector
        def _(dve):
            ch = Chain(dve, step)
            dve.wait_ge(info_in, 16)
            ch.add(nc.vector.tensor_copy(k.node_r[:, :], info[:, :, 0]))
            ch.add(nc.vector.tensor_copy(first[:, :], info[:, :, 1]))
            ch.add(nc.vector.memset(tail[:, :, :], 0))
            ch.link(nc.vector.tensor_copy(k.deg_r[:, :], info[:, :, 2]))
            dve.sem_inc(deg_ready, 1)
            nc.vector.tensor_scalar(first_i[:, :], first[:, :], float(E - 1), None, ALU.min).then_inc(first_ready, 1)
            dve.wait_ge(degT, 1)
            ch.link(nc.vector.tensor_reduce(dmax[:, 0:1], p_deg[:, :], AX, ALU.max))
            ch.add(nc.vector.tensor_scalar(nch_i[:, :], dmax[:, 0:1], float(SLOTS - 1), None, ALU.add))
            ch.link(nc.vector.tensor_scalar(nch2_i[:, :], dmax[:, 0:1], float(SLOTS - 1 - SHORT), None, ALU.add))
            ch.add(nc.vector.tensor_single_scalar(nch_i[:, :], nch_i[:, :], 2, ALU.logical_shift_right))
            ch.link(nc.vector.tensor_single_scalar(nch2_i[:, :], nch2_i[:, :], 2, ALU.logical_shift_right))
            ch.add(nc.vector.tensor_scalar(nch[:, 0:1], nch_i[:, :], float(LEAST), None, ALU.max))
            ch.add(nc.vector.tensor_scalar(nch[:, 1:2], nch2_i[:, :], float(LEAST), None, ALU.max))
            ch.link(nc.vector.tensor_scalar(nch[:, 2:3], dmax[:, 0:1], float(WIDE), None, ALU.is_ge))
            ch.link(nc.vector.tensor_tensor(nch[:, 0:1], nch[:, 0:1], nch[:, 1:2], ALU.subtract))
            ch.link(nc.vector.tensor_tensor(nch[:, 0:1], nch[:, 0:1], nch[:, 2:3], ALU.mult))
            ch.link(nc.vector.tensor_tensor(dmax[:, 1:2], nch[:, 0:1], nch[:, 1:2], ALU.add))
            ch.link(nc.vector.tensor_scalar(nch[:, 0:1], dmax[:, 1:2], float(SLOTS), None, ALU.mult))
            ch.link(nc.vector.tensor_tensor(dmax[:, 2:3], nch[:, 0:1], dmax[:, 0:1], ALU.is_lt))
            dve.sem_inc(nch_ready, 1)
            dve.wait_ge(start_ready, 1)
            ch.link(nc.vector.tensor_copy(dmax[:, 3:5], p_start[:, :]))
            dve.sem_inc(cols_ready, 1)
            dve.wait_ge(in_row, 1)
            ch.add(nc.vector.tensor_copy(row[:, 0, :], p_row[:, 0, :]))
            ch.add(nc.vector.tensor_copy(row[:, 1, :], p_row[:, 2, :]))
            ch.link(nc.vector.tensor_scalar(unused[:, :], k.iota[0:1, 0:BLOCKS], float(UNUSED_AT), None, ALU.add))
            ch.add(nc.vector.tensor_scalar(row[:, 7, :], row[:, 0, :], float(WCH - 1), None, ALU.min))
            ch.link(nc.vector.tensor_tensor(row[:, 6, :], p_row[:, 3, :], unused[:, :], ALU.subtract))
            ch.link(nc.vector.tensor_tensor(row[:, 6, :], row[:, 6, :], p_row[:, 1, :], ALU.mult))
            ch.link(nc.vector.tensor_tensor(row[:, 6, :], row[:, 6, :], unused[:, :], ALU.add))
            ch.link(nc.vector.tensor_scalar(row[:, 6, :], row[:, 6, :], float(SHORT_AT), None, ALU.add))
            ch.add(nc.vector.tensor_scalar(row[:, 2, :], row[:, 0, :], float(WCH), None, ALU.min))
            ch.link(nc.vector.tensor_scalar(one[:, :], row[:, 0, :], float(WCH), None, ALU.is_le))
            ch.link(nc.vector.tensor_reduce(ctl[:, 2:3], one[:, :], AX, ALU.add))
            ch.link(nc.vector.tensor_scalar(ctl[:, 2:3], ctl[:, 2:3], float(BLOCKS - 1), None, ALU.min))
            ch.link(nc.vector.tensor_scalar(one[:, :], row[:, 0, :], float(-WCH), 0.0, ALU.add, ALU.max))
            ch.link(nc.vector.tensor_scalar(one[:, BLOCKS - 1:BLOCKS], one[:, BLOCKS - 1:BLOCKS], 1.0, None, ALU.max))
            ch.link(nc.vector.tensor_tensor_scan(row[:, 3, :], one[:, :], one[:, :], 0.0, ALU.add, ALU.max))
            ch.link(nc.vector.tensor_copy(ctl[:, 3:4], row[:, 3, BLOCKS - 1:BLOCKS]))
            ch.add(nc.vector.tensor_tensor(row[:, 3, :], row[:, 3, :], one[:, :], ALU.subtract))
            ch.add(nc.vector.tensor_reduce(ctl[:, 6:7], p_row[:, 1, :], AX, ALU.add))
            ch.link(nc.vector.tensor_scalar(unused[:, :], row[:, 2, :], 1.0, None, ALU.add))
            ch.link(nc.vector.tensor_tensor_scan(row[:, 4, :], unused[:, :], unused[:, :], 0.0, ALU.add, ALU.max))
            ch.add(nc.vector.tensor_scalar(ctl[:, 5:6], ctl[:, 6:7], float(RING - 1), None, ALU.add))
            ch.link(nc.vector.memset(ctl[:, 4:5], 0.0))
            ch.add(nc.vector.tensor_scalar(row[:, 5, :], row[:, 4, :], row[:, 4, FIRST - 1:FIRST], 0.0, ALU.subtract,
                                           ALU.max))
            ch.add(nc.vector.memset(ctl[:, 7:8], 0.0))
            ch.link(nc.vector.tensor_tensor(ctl[:, 1:2], row[:, 0, BLOCKS - 1:BLOCKS], row[:, 1, BLOCKS - 1:BLOCKS],
                                            ALU.add))
            ch.link(nc.vector.tensor_scalar(ctl[:, 0:1], ctl[:, 1:2], float(RING - 1), None, ALU.add))
            ch.link(nc.vector.tensor_copy(k.ctl_i[:, :], ctl[:, :]))
            for col in (0, 5):
                ch.add(nc.vector.tensor_single_scalar(k.ctl_i[:, col:col + 1], k.ctl_i[:, col:col + 1], 2,
                                                      ALU.logical_shift_right))
            ch.wait()
            ch.link(nc.vector.tensor_scalar(k.ctl_i[:, 5:6], k.ctl_i[:, 5:6], 1.0, None, ALU.max))
            ch.link(nc.vector.tensor_copy(k.row_i[:, :, :], row[:, :, :]))
            dve.sem_inc(rows_ready, 1)
            ch.add(nc.vector.tensor_tensor(valid[:, :, :], bc(k.iota[:, 0:WIDE].unsqueeze(1), [P, BLOCKS, WIDE]),
                                           bc(k.deg_r[:, :].unsqueeze(2), [P, BLOCKS, WIDE]), ALU.is_lt))
            dve.wait_ge(wide_in, 16 * BLOCKS)
            ch.link(nc.vector.tensor_copy(code[:, :, :], wide[:, :, :]))
            v2 = lambda z: z[:, :, :].rearrange("p b w -> p (b w)")
            ch.link(nc.vector.scalar_tensor_tensor(out=v2(code), in0=v2(code), scalar=k.dummy4[:, :], in1=v2(valid),
                                                   op0=ALU.subtract, op1=ALU.mult))
            ch.link(nc.vector.tensor_scalar(v2(code_i), v2(code), k.dummy4[:, :], None, ALU.add))
            ch.add(nc.vector.tensor_copy(rows[:, :, :, SLOTS:2 * SLOTS],
                                         code_i[:, :, :].rearrange("p b (c s) -> p b c s", s=SLOTS)))
            ch.link(nc.vector.tensor_single_scalar(v2(wide), v2(code_i), 2, ALU.logical_shift_right))
            ch.add(nc.vector.tensor_copy(rows[:, :, :, 0:SLOTS],
                                         wide[:, :, :].rearrange("p b (c s) -> p b c s", s=SLOTS)))
            ch.add(nc.vector.tensor_copy(tail[:, 0, 0:SLOTS], bc(k.dummy[:, :], [P, SLOTS])))
            ch.add(nc.vector.tensor_copy(tail[:, 0, SLOTS:2 * SLOTS], bc(k.dummy4[:, :], [P, SLOTS])))
            ch.link(nc.vector.memset(tail[:, 0, CROW - 1:CROW], BLOCKS - 1))
            dve.sem_inc(chunk_rows, 1)
            dve.wait_ge(blocks_ready, 1)
            b0 = dve.value_load(k.ctl_i[0:1, 2:3], min_val=0, max_val=BLOCKS - 1)
            with dve.Fori(b0, BLOCKS) as b:
                n_c = dve.value_load(k.row_i[0:1, 0, bass.ds(b, 1)], min_val=1, max_val=CHUNKS)
                t0 = dve.value_load(k.row_i[0:1, 3, bass.ds(b, 1)], min_val=0, max_val=CHUNKS)
                dve.sem_clear(x_step)
                xs = Chain(dve, x_step)
                xs.link(nc.vector.memset(x_pos[:, :], float(WIDE)))
                with dve.Fori(WCH, n_c) as c:
                    dve.sem_clear(x_step)
                    xs = Chain(dve, x_step)
                    xs.link(nc.vector.tensor_tensor(x_first[:, :], first[:, bass.ds(b, 1)], x_pos[:, :], ALU.add))
                    nc.vector.tensor_scalar(x_first_i[:, :], x_first[:, :], float(E - 1), None, ALU.min)\
                        .then_inc(x_asked, 1)
                    xs.link(nc.vector.tensor_scalar(x_valid[:, :], k.iota[:, 0:SLOTS], x_pos[:, :], None, ALU.add))
                    xs.link(nc.vector.tensor_tensor(x_valid[:, :], x_valid[:, :],
                                                    bc(k.deg_r[:, bass.ds(b, 1)], [P, SLOTS]), ALU.is_lt))
                    xs.link(nc.vector.tensor_scalar(x_pos[:, :], x_pos[:, :], float(SLOTS), None, ALU.add))
                    dve.wait_ge(x_in, (t0 + (c - WCH)) * 16 + 16)
                    xs.link(nc.vector.tensor_copy(x_code[:, :], x_wide[:, 0:SLOTS]))
                    xs.link(nc.vector.scalar_tensor_tensor(out=x_code[:, :], in0=x_code[:, :], scalar=k.dummy4[:, :],
                                                           in1=x_valid[:, :], op0=ALU.subtract, op1=ALU.mult))
                    xs.link(nc.vector.tensor_scalar(x_code_i[:, :], x_code[:, :], k.dummy4[:, :], None, ALU.add))
                    xs.add(nc.vector.tensor_copy(x_row[:, 0, SLOTS:2 * SLOTS], x_code_i[:, :]))
                    xs.add(nc.vector.tensor_single_scalar(x_row[:, 0, 0:SLOTS], x_code_i[:, :], 2,
                                                          ALU.logical_shift_right))
                    xs.link(nc.vector.tensor_copy(x_row[:, 0, CROW - 1:CROW], rows[:, bass.ds(b, 1), 0, CROW - 1]))
                    dve.sem_inc(x_made, 1)
                    dve.wait_ge(x_out, (t0 + (c - WCH)) * 16 + 16)
                    dve.sem_inc(tick, 1)

        @block.sync
        def _(sp):
            sp.dma_start(info[:, :, :], k.info_tab[:, :].rearrange("(b p) c -> p b c", p=P)).then_inc(info_in, 16)
            sp.wait_ge(rows_ready, 1)
            total = sp.value_load(k.ctl_i[0:1, 1:2], min_val=1, max_val=CHUNKS - 16)
            b0 = sp.value_load(k.ctl_i[0:1, 2:3], min_val=0, max_val=BLOCKS - 1)
            sp.wait_ge(chunk_rows, 1)
            sp.wait_ge(blocks_ready, 1)
            with sp.Fori(b0, BLOCKS) as b:
                n_c = sp.value_load(k.row_i[0:1, 0, bass.ds(b, 1)], min_val=1, max_val=CHUNKS)
                c_b = sp.value_load(k.row_i[0:1, 1, bass.ds(b, 1)], min_val=0, max_val=CHUNKS - 16)
                t0 = sp.value_load(k.row_i[0:1, 3, bass.ds(b, 1)], min_val=0, max_val=CHUNKS)
                with sp.Fori(WCH, n_c) as c:
                    sp.wait_ge(x_made, t0 + (c - WCH) + 1)
                    sp.sem_inc(tick, 1)
                    sp.dma_start(k.chunk_tab[bass.ds(chunk_at(nc, c_b + c), 1)].rearrange("a p c -> p a c"), x_row[:, :, :])\
                        .then_inc(x_out, 16)
                    sp.wait_ge(x_out, (t0 + (c - WCH)) * 16 + 16)
                    sp.sem_inc(tick, 1)
            shorts = sp.value_load(k.ctl_i[0:1, 6:7], min_val=0, max_val=BLOCKS)
            for end in (total, shorts + SHORT_AT):
                for j in range(2 * RING):
                    sp.dma_start(k.chunk_tab[bass.ds(chunk_at(nc, end + j), 1)].rearrange("a p c -> p a c"),
                                 tail[:, :, :]).then_inc(tail_out, 16)
            sp.wait_ge(tail_out, 16 * 4 * RING)


def write_blocks(nc, sp, k, lo, hi, written):
    with sp.Fori(lo, hi) as b:
        n_b = sp.value_load(k.row_i[0:1, 2, bass.ds(b, 1)], min_val=1, max_val=WCH)
        c_b = sp.value_load(k.row_i[0:1, 1, bass.ds(b, 1)], min_val=0, max_val=CHUNKS - 16)
        with sp.Fori(0, n_b) as c:
            sp.dma_start(k.chunk_tab[bass.ds(chunk_at(nc, c_b + c), 1)].rearrange("a p c -> p a c"),
                         k.rows[:, bass.ds(b, 1), bass.ds(c, 1), :].rearrange("p a b c -> p (a b) c"))\
                .then_inc(written, 16)
        place = sp.value_load(k.row_i[0:1, 7, bass.ds(b, 1)], min_val=1, max_val=WCH - 1)
        short = sp.value_load(k.row_i[0:1, 6, bass.ds(b, 1)], min_val=SHORT_AT, max_val=TABLE - 1)
        sp.dma_start(k.chunk_tab[bass.ds(short, 1)].rearrange("a p c -> p a c"),
                     k.rows[:, bass.ds(b, 1), bass.ds(place, 1), :].rearrange("p a b c -> p (a b) c"))\
            .then_inc(written, 16)


def written_before(sp, k, b, row):
    return sp.value_load(k.row_i[0:1, row, bass.ds(b - 1, 1)], min_val=0, max_val=BLOCKS * (WCH + 1))


def fetch_and_open(nc, k, x, h):
    with ExitStack() as ctx:
        m = Mem(nc, ctx)
        sq, st = m.sb("sq", [P, GROUP, D]), m.sb("st", [P, 4, GROUP])
        landed = [m.sem(f"landed{t}") for t in range(TURNS)]
        step, var_ready, std_ready = m.sem("step"), m.sem("var_ready"), m.sem("std_ready")
        block = ctx.enter_context(nc.Block())

        @block.gpsimd
        def _(pool):
            for b in range(BLOCKS):
                pool.indirect_dma_start(x[:, b, :], None, k.x1_tab[:, :], at(k.node_r[:, b:b + 1]))\
                    .then_inc(landed[b // GROUP], 16)

        @block.vector
        def _(dve):
            ch = Chain(dve, step)
            for t in range(TURNS):
                blocks = slice(t * GROUP, (t + 1) * GROUP)
                dve.wait_ge(landed[t], 16 * GROUP)
                relu_norm(nc, dve, ch, x[:, blocks, :], h[:, blocks, :], sq[:, :, :], st, [P, GROUP, D],
                          var_ready, std_ready, t + 1)

        @block.scalar
        def _(act):
            for t in range(TURNS):
                act.wait_ge(var_ready, t + 1)
                nc.scalar.activation(st[:, 2, :], st[:, 1, :], ACT.Sqrt).then_inc(std_ready, 1)


def fetch_rows(nc, k, table, width, parts, first_blocks=0):
    with ExitStack() as ctx:
        m = Mem(nc, ctx)
        held = [m.sb(f"held{j}", [P, width]) for j in range(GROUP)]
        landed = [m.sem(f"landed{j}") for j in range(GROUP)]
        copied = [m.sem(f"copied{j}") for j in range(GROUP)]
        written, tick = m.sem("written"), m.sem("tick")
        block = ctx.enter_context(nc.Block())

        if first_blocks:
            @block.sync
            def _(sp):
                write_blocks(nc, sp, k, 0, first_blocks, written)
                sp.wait_ge(written, written_before(sp, k, first_blocks, 4) * 16)
                sp.sem_inc(tick, 1)

        @block.gpsimd
        def _(pool):
            for b in range(BLOCKS):
                j = b % GROUP
                if b >= GROUP:
                    pool.wait_ge(copied[j], (b // GROUP) * len(parts))
                pool.indirect_dma_start(held[j][:, :], None, table, at(k.node_r[:, b:b + 1])).then_inc(landed[j], 16)

        @block.vector
        def _(dve):
            with dve.Fori(0, TURNS) as t:
                for j in range(GROUP):
                    dve.wait_ge(landed[j], t * 16 + 16)
                    for buf, c0, n in parts:
                        nc.vector.tensor_copy(buf[:, bass.ds(t * GROUP + j, 1), 0:n],
                                              held[j][:, c0:c0 + n].unsqueeze(1)).then_inc(copied[j], 1)
            for j in range(GROUP):
                dve.wait_ge(copied[j], TURNS * len(parts))


def cosine_edges(nc, k, part, own_hn, own_v):
    S, base = part.slots, part.base
    W = D + 2
    with ExitStack() as ctx:
        m = Mem(nc, ctx)
        lists = [m.sb(f"list{s}", [P, PER_STAGE, S], I32) for s in range(STAGES)]
        meta = m.sb("meta", [1, RING], I32)
        got = m.sb("got", [P, RING, S, D])
        prod = m.sb("prod", [P, S, D])
        score = m.sb("score", [P, 2, S])
        ex = m.sb("ex", [P, 2, S])
        idx = m.sb("idx", [P, RING, S])
        vals = m.sb("vals", [P, 2, S, W])
        eq = m.sb("eq", [P, 2, S, P])
        firsts = m.sb("firsts", [P, S])
        moved = m.sb("moved", [P, S])
        to = m.sb("to", [P, RING, S], I32)
        out = m.sb("out_rows", [P, RING, S, W])
        weight = m.sb("weight", [P, 2])
        wexp = m.sb("wexp", [P, P])
        p_idx = [m.ps(f"p_idx{j}", [P, S, P]) for j in range(2)]
        p_sum = [m.ps(f"p_sum{j}", [P, S, 128]) for j in range(2)]
        list_in = [m.sem(f"list_in{s}") for s in range(STAGES)]
        list_used = [m.sem(f"list_used{s}") for s in range(STAGES)]
        meta_in, meta_used = m.sem("meta_in"), m.sem("meta_used")
        landed = [m.sem(f"landed{q}") for q in range(RING)]
        got_free = [m.sem(f"got_free{q}") for q in range(RING)]
        step, turn_step, pool_turn = m.sem("step"), m.sem("turn_step"), m.sem("pool_turn")
        idx_ready, spread, eq_ready = m.sem("idx_ready"), m.sem("spread"), m.sem("eq_ready")
        score_ready, ex_ready, vals_ready = m.sem("score_ready"), m.sem("ex_ready"), m.sem("vals_ready")
        summed, sum_copied, tick = m.sem("summed"), m.sem("sum_copied"), m.sem("tick")
        scattered, written = m.sem("scattered"), m.sem("written")
        rows_ready, to_ready = m.sem("rows_ready"), m.sem("to_ready")
        added = [m.sem(f"added{s}") for s in range(S)]
        block = ctx.enter_context(nc.Block())

        @block.sync
        def _(sp):
            n = turns(sp, k, part)
            for s in range(STAGES):
                sp.dma_start(lists[s][:, :, :], k.chunk_tab[base + s * PER_STAGE:base + (s + 1) * PER_STAGE, :, 0:S]
                             .rearrange("a p c -> p a c")).then_inc(list_in[s], 16)
            sp.dma_start(meta[:, :], k.chunk_tab[base:base + RING, 0, CROW - 1:CROW].rearrange("a c -> c a"),
                         allow_slow_non_contiguous=True)\
                .then_inc(meta_in, 16)

            def load_stage(i, s):
                sp.wait_ge(list_used[s], (i + 1) * 2 * PER_STAGE)
                sp.sem_inc(tick, 1)
                ahead = bass.ds(i * RING + (base + RING + s * PER_STAGE), PER_STAGE)
                sp.dma_start(lists[s][:, :, :], k.chunk_tab[ahead, :, 0:S].rearrange("a p c -> p a c"))\
                    .then_inc(list_in[s], 16)
                if s == 0:
                    sp.wait_ge(meta_used, i + 1)
                    sp.sem_inc(tick, 1)
                    sp.dma_start(meta[:, :], k.chunk_tab[bass.ds(i * RING + (base + RING), RING), 0, CROW - 1:CROW]
                                 .rearrange("a c -> c a"), allow_slow_non_contiguous=True).then_inc(meta_in, 16)

            if part.writes:
                with sp.Fori(0, WRITE_TURNS) as i:
                    for s in range(STAGES):
                        b = FIRST + i * WRITTEN + s * (WRITTEN // STAGES)
                        sp.wait_ge(written, written_before(sp, k, b, 5) * 16)
                        sp.sem_inc(tick, 1)
                        load_stage(i, s)
                        write_blocks(nc, sp, k, b, b + WRITTEN // STAGES, written)
                sp.wait_ge(written, written_before(sp, k, BLOCKS, 5) * 16)
                sp.sem_inc(tick, 1)
            with sp.Fori(WRITE_TURNS if part.writes else 0, n) as i:
                for s in range(STAGES):
                    load_stage(i, s)
            sp.wait_ge(list_in[0], n * 16 + 16)
            sp.wait_ge(list_in[1], n * 16 + 16)
            sp.wait_ge(meta_in, n * 16 + 16)
            sp.sem_inc(tick, 1)

        @block.gpsimd
        def _(pool):
            n = turns(pool, k, part)

            def gather(q):
                s, c = divmod(q, PER_STAGE)
                for j in range(S):
                    pool.indirect_dma_start(got[:, q, j, :], None, k.hn_tab[:, :], at(lists[s][:, c, j:j + 1]))\
                        .then_inc(landed[q], 16)

            def scatter(q):
                for j in range(S):
                    pool.indirect_dma_start(k.sums[j][:, :], at(to[:, q, j:j + 1]), out[:, q, j, 0:D + 1], None,
                                            compute_op=ALU.add).then_inc(added[j], 16)

            pool.sem_inc(scattered, RING - 1)
            for j in range(S):
                pool.indirect_dma_start(k.sums[j][:, :], at(k.dummy_i[:, :]), k.zeros[:, 0:D + 1], None,
                                        compute_op=ALU.add).then_inc(added[j], 16)
            pool.wait_ge(list_in[0], 16)
            gather(0)
            gather(1)
            with pool.Fori(0, n) as i:
                def gather_turn(q, ahead):
                    if q % PER_STAGE == 0:
                        pool.wait_ge(list_in[q // PER_STAGE], (i + ahead + 1) * 16)
                    pool.wait_ge(got_free[q], i + ahead + 1)
                    pool.sem_inc(pool_turn, 1)
                    gather(q)

                def scatter_turn(q):
                    pool.wait_ge(to_ready, i * RING + q + 1)
                    pool.wait_ge(rows_ready, i * RING + q + 1)
                    for j in range(S):
                        pool.wait_ge(added[j], (i * RING + q + 1) * 16)
                    pool.sem_inc(scattered, 1)
                    scatter(q)

                gather_turn(2, 0)
                scatter_turn(0)
                gather_turn(3, 0)
                scatter_turn(1)
                gather_turn(0, 1)
                scatter_turn(2)
                gather_turn(1, 1)
                scatter_turn(3)
            for j in range(S):
                pool.wait_ge(added[j], n * (16 * RING) + 16)
            for q in range(2):
                pool.wait_ge(landed[q], n * (16 * S) + 16 * S)

        @block.vector
        def _(dve):
            n = turns(dve, k, part)
            ch = Chain(dve, step)
            ch.link(nc.vector.memset(wexp[:, :], 0.5))
            ch.link(nc.vector.tensor_tensor_scan(wexp[:, :], wexp[:, :], wexp[:, :], 2.0 ** 61, ALU.mult, ALU.bypass))
            ch.link(nc.vector.tensor_tensor(eq[:, 0, 0, :], wexp[:, :], k.ident[:, :], ALU.mult))
            ch.link(nc.vector.tensor_reduce(weight[:, 0:1], eq[:, 0, 0, :], AX, ALU.add))
            ch.link(nc.vector.tensor_scalar(weight[:, 1:2], weight[:, 0:1], 2.0, None, ALU.mult))
            for z in range(2):
                ch.add(nc.vector.tensor_copy(vals[:, z, :, D + 1:D + 2], bc(weight[:, 0:1].unsqueeze(1), [P, S, 1])))
            ch.wait()
            for q in range(RING):
                dve.sem_inc(got_free[q], 1)
            with dve.Fori(0, n) as i:
                dve.sem_clear(turn_step)
                ts = Chain(dve, turn_step)
                dve.wait_ge(meta_in, i * 16 + 16)
                dve.sem_inc(tick, 1)
                _, b = nc.values_load_multi_w_load_instructions(meta[0:1, 0:RING], engines=DVE, min_val=0,
                                                                max_val=BLOCKS - 1)
                dve.sem_inc(meta_used, 1)

                def indices(s):
                    dve.wait_ge(list_in[s], i * 16 + 16)
                    nc.vector.tensor_copy(idx[:, s * PER_STAGE:(s + 1) * PER_STAGE, :], lists[s][:, :, :])\
                        .then_inc(idx_ready, 1)
                    dve.wait_ge(idx_ready, i * 2 + s + 1)
                    dve.sem_inc(list_used[s], PER_STAGE)

                def first_half(q):
                    dve.wait_ge(landed[q], i * (16 * S) + 16 * S)
                    dve.sem_inc(list_used[q // PER_STAGE], 1)
                    ts.add(nc.vector.tensor_tensor(prod[:, :, :], got[:, q, :, :],
                                                   bc(own_hn[:, bass.ds(b[q], 1), :], [P, S, D]), ALU.mult))
                    ts.wait()
                    dve.sem_inc(got_free[q], 1)
                    nc.vector.tensor_reduce(score[:, q % 2, :], prod[:, :, :], AX, ALU.add).then_inc(score_ready, 1)
                    dve.wait_ge(score_ready, i * RING + q + 1)
                    dve.wait_ge(spread, i * RING + q + 1)
                    nc.vector.tensor_tensor(eq[:, q % 2, :, :], p_idx[q % 2][:, :, :],
                                            bc(idx[:, q, :].unsqueeze(2), [P, S, P]), ALU.is_equal)\
                        .then_inc(eq_ready, 1)

                def second_half(q):
                    dve.wait_ge(ex_ready, i * RING + q + 1)
                    nc.vector.tensor_tensor(vals[:, q % 2, :, 0:D + 1],
                                            bc(own_v[:, bass.ds(b[q], 1), :], [P, S, D + 1]),
                                            bc(ex[:, q % 2, :].unsqueeze(2), [P, S, D + 1]), ALU.mult)\
                        .then_inc(vals_ready, 1)

                def third_half(q):
                    dve.wait_ge(rows_ready, i * RING + q + 1)
                    ts.link(nc.vector.tensor_scalar(firsts[:, :], out[:, q, :, D + 1], weight[:, 1:2], None,
                                                    ALU.is_le))
                    ts.link(nc.vector.scalar_tensor_tensor(out=moved[:, :], in0=idx[:, q, :], scalar=k.dummy[:, :],
                                                           in1=firsts[:, :], op0=ALU.subtract, op1=ALU.mult))
                    dve.wait_ge(scattered, i * RING + q + 1)
                    nc.vector.tensor_scalar(to[:, q, :], moved[:, :], k.dummy[:, :], None, ALU.add)\
                        .then_inc(to_ready, 1)
                    dve.wait_ge(to_ready, i * RING + q + 1)

                indices(0)
                first_half(0)
                first_half(1)
                second_half(0)
                indices(1)
                third_half(0)
                second_half(1)
                first_half(2)
                third_half(1)
                second_half(2)
                first_half(3)
                third_half(2)
                second_half(3)
                third_half(3)

        @block.scalar
        def _(act):
            n = turns(act, k, part)
            act.sem_inc(sum_copied, 2)
            with act.Fori(0, n) as i:
                def exps(q):
                    act.wait_ge(score_ready, i * RING + q + 1)
                    nc.scalar.activation(ex[:, q % 2, :], score[:, q % 2, :], ACT.Exp).then_inc(ex_ready, 1)

                def rows(q):
                    act.wait_ge(summed, i * RING + q + 1)
                    act.wait_ge(scattered, i * RING + q + 1)
                    nc.scalar.activation(out[:, q, :, :], p_sum[q % 2][:, :, 0:W], ACT.Copy).then_inc(rows_ready, 1)
                    act.wait_ge(rows_ready, i * RING + q + 1)
                    act.sem_inc(sum_copied, 1)

                exps(0)
                exps(1)
                rows(0)
                exps(2)
                rows(1)
                exps(3)
                rows(2)
                rows(3)

        @block.tensor
        def _(pe):
            n = turns(pe, k, part)
            with pe.Fori(0, n) as i:
                def spread_idx(q):
                    pe.wait_ge(idx_ready, i * 2 + q // PER_STAGE + 1)
                    if q >= 2:
                        pe.wait_ge(eq_ready, i * RING + q - 1)
                    for j in range(S):
                        last = nc.tensor.matmul(p_idx[q % 2][:, j, :], bc(idx[:, q, j:j + 1], [P, P]), k.ident[:, :],
                                                start=True, stop=True)
                    last.then_inc(spread, 1)

                def sum_equal(q):
                    pe.wait_ge(eq_ready, i * RING + q + 1)
                    pe.wait_ge(vals_ready, i * RING + q + 1)
                    pe.wait_ge(sum_copied, i * RING + q + 1)
                    for j in range(S):
                        last = nc.tensor.matmul(p_sum[q % 2][:, j, 0:W], eq[:, q % 2, j, :], vals[:, q % 2, j, :],
                                                start=True, stop=True)
                    last.then_inc(summed, 1)

                spread_idx(0)
                spread_idx(1)
                sum_equal(0)
                spread_idx(2)
                sum_equal(1)
                spread_idx(3)
                sum_equal(2)
                sum_equal(3)



def cosine_close(nc, k, a):
    with ExitStack() as ctx:
        m = Mem(nc, ctx)
        x = m.sb("x_close", [NP_, NC, D])
        part = [m.sb(f"part{j}", [NP_, NC, D + 1]) for j in range(SLOTS)]
        den = m.sb("den", [NP_, NC])
        inv = m.sb("inv", [NP_, NC])
        x_in, stored, step, done = m.sem("x_in"), m.sem("stored"), m.sem("step"), m.sem("done")
        part_in = [m.sem(f"part_in{j}") for j in range(SLOTS)]
        block = ctx.enter_context(nc.Block())

        @block.sync
        def _(sp):
            for j in range(SLOTS):
                sp.dma_start(part[j][:, :, :], k.sums[j][0:N, :].rearrange("(p c) d -> p c d", p=NP_))\
                    .then_inc(part_in[j], 16)
            sp.dma_start(x[:, :, :], a["x"].rearrange("(p c) d -> p c d", p=NP_)).then_inc(x_in, 16)
            sp.wait_ge(done, 1)
            sp.dma_start(k.x1_tab[0:N, :].rearrange("(p c) d -> p c d", p=NP_), x[:, :, :]).then_inc(stored, 16)
            sp.wait_ge(stored, 16)

        @block.vector
        def _(dve):
            ch = Chain(dve, step)
            dve.wait_ge(part_in[0], 16)
            for j in range(1, SLOTS):
                dve.wait_ge(part_in[j], 16)
                ch.link(nc.vector.tensor_tensor(part[0][:, :, :], part[0][:, :, :], part[j][:, :, :], ALU.add))
            ch.link(nc.vector.tensor_scalar(den[:, :], part[0][:, :, D], 1e-30, None, ALU.max))
            ch.link(nc.vector.reciprocal(inv[:, :], den[:, :]))
            ch.link(nc.vector.tensor_tensor(part[1][:, :, 0:D], part[0][:, :, 0:D],
                                            bc(inv[:, :].unsqueeze(2), [NP_, NC, D]), ALU.mult))
            dve.wait_ge(x_in, 16)
            nc.vector.tensor_tensor(x[:, :, :], x[:, :, :], part[1][:, :, 0:D], ALU.add).then_inc(done, 1)


def load_weights(nc, k, a):
    with ExitStack() as ctx:
        m = Mem(nc, ctx)
        plain1, plain2 = m.sb("plain1", [P, D]), m.sb("plain2", [P, D])
        att = {n: m.sb("att_" + n, [P, D]) for n in ("a1_src", "a1_dst", "a2_src", "a2_dst")}
        prod, lin = m.sb("prod", [P, D]), m.sb("lin", [P, 1])
        wide = {n: m.sb("wide_" + n, [D, 2, 2, D]) for n in ("Wa_w", "lin_w")}
        p_w = [m.ps(f"p_w{j}", [P, D]) for j in range(4)]
        loaded, step, turned = m.sem("loaded"), m.sem("step"), m.sem("turned")
        block = ctx.enter_context(nc.Block())
        both = ((0, D), (D, P))

        @block.sync
        def _(sp):
            n = 0

            def load(dst, src):
                nonlocal n
                sp.dma_start(dst, src).then_inc(loaded, 16)
                n += 1

            for lo, hi in both:
                load(plain1[lo:hi, :], a["L1_gnn_W1"])
                load(plain2[lo:hi, :], a["L1_gnn_W2"])
                load(k.w_gcn[lo:hi, :], a["L2_gnn_W"])
                for t in range(TYPES):
                    load(k.w_src[lo:hi, AW + t * D:AW + (t + 1) * D], a["L3_gnn_r"][t, D:2 * D, :])
                    load(k.w_own[lo:hi, AW + t * D:AW + (t + 1) * D], a["L3_gnn_r"][t, 0:D, :])
            for name, tile in att.items():
                load(tile[:, :], a["L1_gnn_" + name].rearrange("h c -> (h c)").partition_broadcast(P))
            for name, tile in k.vec.items():
                load(tile[:, :], a[name].partition_broadcast(P))
            load(k.att_a[:, :], a["L3_gnn_a"][0, :].partition_broadcast(P))
            for name, tile in wide.items():
                for c in range(2):
                    load(tile[:, :, c, :], a["L3_gnn_" + name].rearrange("o (h i) -> o h i", h=2))
            k.weights_loaded = n * 16
            sp.wait_ge(loaded, k.weights_loaded)
            sp.sem_inc(turned, 1)

        @block.tensor
        def _(pe):
            pe.wait_ge(turned, 1)
            for j, name in enumerate(("Wa_w", "lin_w")):
                for h in range(2):
                    last = nc.tensor.transpose(p_w[2 * j + h][:, :], wide[name][:, h, :, :].rearrange("o c i -> o (c i)"),
                                               k.ident[0:D, 0:D])
            last.then_inc(turned, 1)

        @block.vector
        def _(dve):
            ch = Chain(dve, step)
            ch.link(nc.vector.memset(k.w_gat1[:, :], 0.0))
            ch.link(nc.vector.memset(k.w_gat2[:, :], 0.0))
            for row, heads, c in ((k.ones_row[1], H1, C1), (k.ones_row[2], 1, D)):
                ch.link(nc.vector.memset(row[:, :], 0.0))
                ch.link(nc.vector.memset(row[:, 0:heads * (c + 1)].rearrange("p (h c) -> p h c", h=heads)[:, :, c], 1.0))
            dve.wait_ge(turned, 1)
            for plain, w, heads, c, names in ((plain1, k.w_gat1, H1, C1, ("a1_src", "a1_dst")),
                                              (plain2, k.w_gat2, 1, D, ("a2_src", "a2_dst"))):
                ch.link(nc.vector.tensor_copy(w[:, 0:heads * (c + 1)].rearrange("p (h c) -> p h c", h=heads)[:, :, 0:c],
                                              plain[:, :].rearrange("p (h c) -> p h c", h=heads)))
                for n, name in enumerate(names):
                    at0 = heads * (c + 1) + n * heads
                    ch.link(nc.vector.tensor_tensor(prod[:, :], plain[:, :], att[name][:, :], ALU.mult))
                    ch.link(nc.vector.tensor_reduce(w[:, at0:at0 + heads],
                                                    prod[:, :].rearrange("p (h c) -> p h c", h=heads), AX, ALU.add))
            dve.wait_ge(turned, 2)
            for j, dst in enumerate((k.w_own[:, 0:D], k.w_src[:, 0:D], k.w_lin[:, 0, :], k.w_lin[:, 1, :])):
                ch.link(nc.vector.tensor_copy(dst, p_w[j][:, :]))
            bias_a = k.vec["L3_gnn_Wa_b"]
            for src, dst in ((k.w_own[:, 0:D], k.w_own[:, D:AW]), (k.w_src[:, 0:D], k.w_src[:, D:AW]),
                             (bias_a[:, :], k.own_bias[:, D:AW])):
                ch.link(nc.vector.tensor_tensor(prod[:, :], src, k.att_a[:, :], ALU.mult))
                ch.link(nc.vector.tensor_reduce(lin[:, :], prod[:, :], AX, ALU.add))
                ch.link(nc.vector.tensor_scalar(dst, lin[:, :], REL_SLOPE, None, ALU.mult))
            ch.add(nc.vector.tensor_copy(k.own_bias[:, 0:D], bias_a[:, :]))
            ch.add(nc.vector.memset(k.own_bias[:, AW:OROW], 0.0))
            ch.link(nc.vector.tensor_scalar(k.att_a99[:, :], k.att_a[:, :], 1.0 - REL_SLOPE, None, ALU.mult))


def open_layer(nc, k, x, h):
    with ExitStack() as ctx:
        m = Mem(nc, ctx)
        sq, st = m.sb("sq", [P, BLOCKS, D]), m.sb("st", [P, 4, BLOCKS])
        step, var_ready, std_ready = m.sem("step"), m.sem("var_ready"), m.sem("std_ready")
        block = ctx.enter_context(nc.Block())

        @block.vector
        def _(dve):
            relu_norm(nc, dve, Chain(dve, step), x[:, :, :], h[:, :, :], sq[:, :, :], st, [P, BLOCKS, D],
                      var_ready, std_ready, 1)

        @block.scalar
        def _(act):
            act.wait_ge(var_ready, 1)
            nc.scalar.activation(st[:, 2, :], st[:, 1, :], ACT.Sqrt).then_inc(std_ready, 1)


def project_and_spread(nc, k, h, weights, width, rows, finish, table, columns, dummy_col):
    with ExitStack() as ctx:
        m = Mem(nc, ctx)
        p_t = [m.ps(f"p_t{j}", [P, P]) for j in range(2)]
        p_o = [m.ps(f"p_o{j}", [P, 2, 512]) for j in range(2)]
        staged = m.sb("staged", [P, 2, 2, D])
        hT = m.sb("hT", [P, 2, P])
        dummy = m.sb("dummy", [P, columns])
        tr, copied, made, stored = m.sem("transposed"), m.sem("copied"), m.sem("made"), m.sem("stored")
        stage_ready, stage_free = m.sem("stage_ready"), m.sem("stage_free")
        set_, out, spread = m.sem("dummy_set"), m.sem("dummy_out"), m.sem("spread")
        block = ctx.enter_context(nc.Block())
        PAIRS = BLOCKS // 2
        TP = 7

        @block.tensor
        def _(pe):
            pe.sem_inc(stage_free, 2)
            with pe.Fori(0, PAIRS // TP) as t:
                for j in range(TP):
                    n, z = t * TP + j, j % 2
                    pe.wait_ge(stored, n + (1 if j else 2))
                    pe.wait_ge(stage_ready, n + 1)
                    nc.tensor.transpose(p_t[z][:, :], staged[:, z, :, :].rearrange("p b d -> p (b d)"),
                                        k.ident[:, :]).then_inc(tr, 1)
                    pe.wait_ge(copied, n + 1)
                    pe.sem_inc(stage_free, 1)
                    for y in range(2):
                        last = nc.tensor.matmul(p_o[z][:, y, 0:width], hT[y * D:(y + 1) * D, z, :],
                                                weights[y * D:(y + 1) * D, 0:width], start=True, stop=True)
                    last.then_inc(made, 1)

        @block.scalar
        def _(act):
            with act.Fori(0, PAIRS // TP) as t:
                for j in range(TP):
                    n = t * TP + j
                    act.wait_ge(stage_free, n + (1 if j else 2))
                    nc.scalar.activation(staged[:, j % 2, :, :], h[:, bass.ds(n * 2, 2), :], ACT.Copy)\
                        .then_inc(stage_ready, 1)
                    act.wait_ge(tr, n + 1)
                    nc.scalar.activation(hT[:, j % 2, :], p_t[j % 2][:, :], ACT.Copy).then_inc(copied, 1)

        @block.vector
        def _(dve):
            nc.vector.memset(dummy[:, :], 0.0).then_inc(set_, 1)
            dve.wait_ge(set_, 1)
            if dummy_col is not None:
                nc.vector.memset(dummy[:, dummy_col:columns], MINUS).then_inc(set_, 1)
            dve.sem_inc(stored, 2)
            with dve.Fori(0, PAIRS // TP) as t:
                for j in range(TP):
                    n = t * TP + j
                    dve.wait_ge(made, n + 1)
                    finish(rows[:, bass.ds(n * 2, 2), 0:width], p_o[j % 2][:, :, 0:width], bass.ds(n * 2, 2))\
                        .then_inc(stored, 1)
            dve.wait_ge(stored, PAIRS + 2)

        @block.sync
        def _(sp):
            sp.wait_ge(set_, 1 if dummy_col is None else 2)
            sp.dma_start(table[NPAD:ROWS, :], dummy[:, :]).then_inc(out, 16)
            sp.wait_ge(out, 16)

        @block.gpsimd
        def _(pool):
            for b in range(BLOCKS):
                pool.wait_ge(stored, b // 2 + 3)
                pool.indirect_dma_start(table, at(k.node_r[:, b:b + 1]), rows[:, b, 0:columns], None)\
                    .then_inc(spread, 16)
            pool.wait_ge(spread, 16 * BLOCKS)


def ring_buffers(m, part, width, stages=STAGES):
    S = part.slots
    r = type("Ring", (), {})()
    r.per_stage = RING // stages
    r.lists = [m.sb(f"list{s}", [P, r.per_stage, S], I32) for s in range(stages)]
    r.meta = m.sb("meta", [1, RING], I32)
    r.got = m.sb("got", [P, RING, S, width])
    r.list_in = [m.sem(f"list_in{s}") for s in range(stages)]
    r.list_used = [m.sem(f"list_used{s}") for s in range(stages)]
    r.meta_in, r.meta_used = m.sem("meta_in"), m.sem("meta_used")
    r.landed = [m.sem(f"landed{q}") for q in range(RING)]
    r.got_free = [m.sem(f"got_free{q}") for q in range(RING)]
    r.tick, r.turn_step = m.sem("tick"), m.sem("turn_step")
    return r


def turns(eng, k, part):
    return eng.value_load(k.ctl_i[0:1, part.ctl:part.ctl + 1], min_val=1, max_val=part.most)


def load_lists(nc, sp, k, part, r, i):
    for s in range(STAGES):
        sp.wait_ge(r.list_used[s], (i + 1) * PER_STAGE)
        sp.sem_inc(r.tick, 1)
        sp.dma_start(r.lists[s][:, :, :], k.chunk_tab[bass.ds(i * RING + (part.base + s * PER_STAGE), PER_STAGE), :,
                                                      0:part.slots].rearrange("a p c -> p a c"))\
            .then_inc(r.list_in[s], 16)
    sp.wait_ge(r.meta_used, i + 1)
    sp.sem_inc(r.tick, 1)
    sp.dma_start(r.meta[:, :], k.chunk_tab[bass.ds(i * RING + part.base, RING), 0, CROW - 1:CROW]
                 .rearrange("a c -> c a"), allow_slow_non_contiguous=True).then_inc(r.meta_in, 16)


def gather_all(nc, pool, k, part, r, table):
    n = turns(pool, k, part)
    with pool.Fori(0, n) as i:
        for q in range(RING):
            s, c = divmod(q, r.per_stage)
            if c == 0:
                pool.wait_ge(r.list_in[s], i * 16 + 16)
            pool.wait_ge(r.got_free[q], i + 1)
            pool.sem_inc(r.tick, 1)
            for j in range(part.slots):
                pool.indirect_dma_start(r.got[:, q, j, :], None, table, at(r.lists[s][:, c, j:j + 1]))\
                    .then_inc(r.landed[q], 16)


def ring_credits(dve, r, readers=1, free=RING):
    for q in range(free):
        dve.sem_inc(r.got_free[q], 1)
    for used in r.list_used:
        dve.sem_inc(used, r.per_stage)
    dve.sem_inc(r.meta_used, readers)


def turn_blocks(nc, eng, engines, r, i):
    eng.wait_ge(r.meta_in, i * 16 + 16)
    eng.sem_inc(r.tick, 1)
    _, b = nc.values_load_multi_w_load_instructions(r.meta[0:1, 0:RING], engines=engines, min_val=0,
                                                    max_val=BLOCKS - 1)
    eng.sem_inc(r.meta_used, 1)
    return b


def gat_edges(nc, k, part, heads, c, state, top, own_dst, table):
    HW = heads * (c + 1)
    W = HW + heads
    S = part.slots
    with ExitStack() as ctx:
        m = Mem(nc, ctx)
        r = ring_buffers(m, part, W)
        e = m.sb("e", [P, 2, S + 1, heads])
        p = m.sb("p", [P, 2, S + 1, heads])
        prod = m.sb("prod", [P, S, HW])
        chunk_sum = m.sb("chunk_sum", [P, HW])
        old = m.sb("old", [P, HW])
        e_ready, p_ready = m.sem("e_ready"), m.sem("p_ready")
        block = ctx.enter_context(nc.Block())

        @block.sync
        def _(sp):
            n = turns(sp, k, part)
            with sp.Fori(0, n) as i:
                load_lists(nc, sp, k, part, r, i)

        @block.gpsimd
        def _(pool):
            gather_all(nc, pool, k, part, r, table)

        @block.vector
        def _(dve):
            n = turns(dve, k, part)
            ring_credits(dve, r)
            with dve.Fori(0, n) as i:
                dve.sem_clear(r.turn_step)
                ts = Chain(dve, r.turn_step)
                b = turn_blocks(nc, dve, DVE, r, i)

                def add_dst(q):
                    z, blk = q % 2, bass.ds(b[q], 1)
                    dve.wait_ge(r.landed[q], i * (16 * S) + 16 * S)
                    dve.sem_inc(r.list_used[q // PER_STAGE], 1)
                    ts.add(nc.vector.tensor_copy(e[:, z, S, :], top[:, blk, :].rearrange("p b h -> p (b h)")))
                    return ts.add(nc.vector.tensor_tensor(e[:, z, 0:S, :], r.got[:, q, :, HW:W],
                                                          bc(own_dst[:, blk, :], [P, S, heads]), ALU.add))

                def leaky(q, after):
                    z = q % 2
                    ts.wait(after)
                    return ts.add(nc.vector.scalar_tensor_tensor(out=e[:, z, 0:S, :], in0=e[:, z, 0:S, :],
                                                                 scalar=SLOPE, in1=e[:, z, 0:S, :],
                                                                 op0=ALU.mult, op1=ALU.max))

                def maxima(q, after):
                    ts.wait(after)
                    return ts.add(nc.vector.tensor_reduce(top[:, bass.ds(b[q], 1), :].rearrange("p b h -> p (b h)"),
                                                          e[:, q % 2, :, :].rearrange("p s h -> p h s"), AX, ALU.max))

                def below_top(q, after):
                    z = q % 2
                    ts.wait(after)
                    nc.vector.tensor_tensor(e[:, z, :, :], e[:, z, :, :],
                                            bc(top[:, bass.ds(b[q], 1), :], [P, S + 1, heads]), ALU.subtract)\
                        .then_inc(e_ready, 1)

                def weigh(q):
                    z, blk = q % 2, bass.ds(b[q], 1)
                    dve.wait_ge(p_ready, i * RING + q + 1)
                    hc = "p s (h c) -> p s h c"
                    weighed = ts.add(nc.vector.tensor_tensor(prod[:, :, :].rearrange(hc, h=heads),
                                                             r.got[:, q, :, 0:HW].rearrange(hc, h=heads),
                                                             bc(p[:, z, 0:S, :].unsqueeze(3), [P, S, heads, c + 1]),
                                                             ALU.mult))
                    ts.add(nc.vector.tensor_tensor(old[:, :].rearrange("p (h c) -> p h c", h=heads),
                                                   state[:, blk, 0:HW].rearrange("p b (h c) -> p (b h) c", h=heads),
                                                   bc(p[:, z, S, :].unsqueeze(2), [P, heads, c + 1]), ALU.mult))
                    return weighed

                def add_slots(q, after):
                    ts.wait(after)
                    dve.sem_inc(r.got_free[q], 1)
                    return ts.add(nc.vector.tensor_reduce(chunk_sum[:, :], prod[:, :, :].rearrange("p s f -> p f s"),
                                                          AX, ALU.add))

                def accumulate(q, after):
                    ts.wait(after)
                    return ts.add(nc.vector.tensor_tensor(state[:, bass.ds(b[q], 1), 0:HW]
                                                          .rearrange("p b f -> p (b f)"), chunk_sum[:, :], old[:, :],
                                                          ALU.add))

                below_top(0, maxima(0, leaky(0, add_dst(0))))
                for q in range(1, RING):
                    n_a = add_dst(q)
                    n_b = weigh(q - 1)
                    n_a = leaky(q, n_a)
                    n_b = add_slots(q - 1, n_b)
                    n_a = maxima(q, n_a)
                    n_b = accumulate(q - 1, n_b)
                    below_top(q, n_a)
                    ts.wait(n_b)
                ts.wait(accumulate(RING - 1, add_slots(RING - 1, weigh(RING - 1))))
                dve.wait_ge(e_ready, i * RING + RING)

        @block.scalar
        def _(act):
            n = turns(act, k, part)
            with act.Fori(0, n) as i:
                for q in range(RING):
                    act.wait_ge(e_ready, i * RING + q + 1)
                    nc.scalar.activation(p[:, q % 2, :, :], e[:, q % 2, :, :], ACT.Exp).then_inc(p_ready, 1)


def gcn_edges(nc, k, part, state, table):
    S = part.slots
    with ExitStack() as ctx:
        m = Mem(nc, ctx)
        r = ring_buffers(m, part, D)
        chunk_sum = m.sb("chunk_sum", [P, D])
        block = ctx.enter_context(nc.Block())

        @block.sync
        def _(sp):
            n = turns(sp, k, part)
            with sp.Fori(0, n) as i:
                load_lists(nc, sp, k, part, r, i)

        @block.gpsimd
        def _(pool):
            gather_all(nc, pool, k, part, r, table)

        @block.vector
        def _(dve):
            n = turns(dve, k, part)
            ring_credits(dve, r)
            with dve.Fori(0, n) as i:
                dve.sem_clear(r.turn_step)
                ts = Chain(dve, r.turn_step)
                b = turn_blocks(nc, dve, DVE, r, i)
                for q in range(RING):
                    own = state[:, bass.ds(b[q], 1), :].rearrange("p b d -> p (b d)")
                    dve.wait_ge(r.landed[q], i * (16 * S) + 16 * S)
                    dve.sem_inc(r.list_used[q // PER_STAGE], 1)
                    ts.link(nc.vector.tensor_reduce(chunk_sum[:, :], r.got[:, q, :, :].rearrange("p s f -> p f s"), AX,
                                                    ALU.add))
                    dve.sem_inc(r.got_free[q], 1)
                    ts.link(nc.vector.tensor_tensor(own, own, chunk_sum[:, :], ALU.add))


def gat_open(nc, k, heads, c, state, own_dst, top):
    HW = heads * (c + 1)
    with ExitStack() as ctx:
        m = Mem(nc, ctx)
        step = m.sem("step")
        block = ctx.enter_context(nc.Block())

        @block.vector
        def _(dve):
            ch = Chain(dve, step)
            ch.add(nc.vector.tensor_copy(own_dst[:, :, :], state[:, :, HW + heads:HW + 2 * heads]))
            ch.link(nc.vector.tensor_tensor(top[:, :, :], state[:, :, HW:HW + heads],
                                            state[:, :, HW + heads:HW + 2 * heads], ALU.add))
            ch.link(nc.vector.scalar_tensor_tensor(out=top[:, :, :], in0=top[:, :, :], scalar=SLOPE,
                                                   in1=top[:, :, :], op0=ALU.mult, op1=ALU.max))


def gat_close(nc, k, heads, c, state, bias, gain, shift, y, x_add):
    HW = heads * (c + 1)
    H = BLOCKS // 2
    with ExitStack() as ctx:
        m = Mem(nc, ctx)
        sq, ex = m.sb("sq", [P, BLOCKS, D]), m.sb("ex", [P, BLOCKS, D])
        st = m.sb("st", [P, 4, BLOCKS])
        den = m.sb("den", [P, 2, BLOCKS, heads])
        step, var_ready, std_ready = m.sem("step"), m.sem("var_ready"), m.sem("std_ready")
        centred, squared, y_ready, ex_ready = m.sem("centred"), m.sem("squared"), m.sem("y_ready"), m.sem("ex_ready")
        block = ctx.enter_context(nc.Block())
        full = [P, H, D]
        half = lambda u: slice(u * H, (u + 1) * H)

        @block.vector
        def _(dve):
            ch = Chain(dve, step)
            tt, ts = nc.vector.tensor_tensor, nc.vector.tensor_scalar
            cols = state[:, :, 0:HW].rearrange("p b (h c) -> p b h c", h=heads)
            wide = lambda j, u: bc(st[:, j, half(u)].unsqueeze(2), full)
            vec = lambda t: bc(t[:, :].unsqueeze(1), full)
            ch.link(ts(den[:, 0, :, :], cols[:, :, :, c], SM_EPS, None, ALU.add))
            ch.link(nc.vector.reciprocal(den[:, 1, :, :], den[:, 0, :, :]))
            for u in range(2):
                Y = y[:, half(u), :]
                ch.link(tt(Y.rearrange("p b (h c) -> p b h c", h=heads), cols[:, half(u), :, 0:c],
                           bc(den[:, 1, half(u), :].unsqueeze(3), [P, H, heads, c]), ALU.mult))
                ch.link(tt(Y, Y, vec(bias), ALU.add))
                ch.link(nc.vector.tensor_reduce(st[:, 0, half(u)], Y, AX, ALU.add))
                ch.link(ts(st[:, 3, half(u)], st[:, 0, half(u)], 1.0 / D, None, ALU.mult))
                tt(Y, Y, wide(3, u), ALU.subtract).then_inc(centred, 1)
            for u in range(2):
                dve.wait_ge(squared, u + 1)
                ch.link(nc.vector.tensor_reduce(st[:, 0, half(u)], sq[:, half(u), :], AX, ALU.add))
                ts(st[:, 1, half(u)], st[:, 0, half(u)], 1.0 / D, LN_EPS, ALU.mult, ALU.add).then_inc(var_ready, 1)
            for u in range(2):
                Y = y[:, half(u), :]
                dve.wait_ge(std_ready, u + 1)
                ch.link(nc.vector.reciprocal(st[:, 3, half(u)], st[:, 2, half(u)]))
                ch.link(tt(Y, Y, wide(3, u), ALU.mult))
                ch.link(tt(Y, Y, vec(gain), ALU.mult))
                tt(Y, Y, vec(shift), ALU.add).then_inc(y_ready, 1)
            for u in range(2):
                flat = lambda t: t[:, half(u), :].rearrange("p b d -> p (b d)")
                dve.wait_ge(ex_ready, u + 1)
                ch.link(nc.vector.scalar_tensor_tensor(out=flat(y), in0=flat(ex), scalar=1.0, in1=flat(sq),
                                                       op0=ALU.min, op1=ALU.add))
                if x_add is None:
                    ch.link(ts(flat(y), flat(y), -1.0, None, ALU.add))
                else:
                    ch.link(nc.vector.scalar_tensor_tensor(out=flat(x_add), in0=flat(y), scalar=-1.0, in1=flat(x_add),
                                                           op0=ALU.add, op1=ALU.add))

        @block.scalar
        def _(act):
            for u in range(2):
                act.wait_ge(centred, u + 1)
                nc.scalar.activation(sq[:, half(u), :], y[:, half(u), :], ACT.Square).then_inc(squared, 1)
            for u in range(2):
                act.wait_ge(var_ready, u + 1)
                nc.scalar.activation(st[:, 2, half(u)], st[:, 1, half(u)], ACT.Sqrt).then_inc(std_ready, 1)
            for u in range(2):
                act.wait_ge(y_ready, u + 1)
                nc.scalar.activation(sq[:, half(u), :], y[:, half(u), :], ACT.Relu)
                nc.scalar.activation(ex[:, half(u), :], y[:, half(u), :], ACT.Exp).then_inc(ex_ready, 1)


def gcn_norm(nc, k, dis):
    with ExitStack() as ctx:
        m = Mem(nc, ctx)
        root = m.sb("root", [P, 2, BLOCKS])
        step, deg_ready, root_ready = m.sem("step"), m.sem("deg_ready"), m.sem("root_ready")
        block = ctx.enter_context(nc.Block())

        @block.vector
        def _(dve):
            nc.vector.tensor_scalar(root[:, 0, :], k.deg_r[:, :], 1.0, None, ALU.add).then_inc(deg_ready, 1)
            dve.wait_ge(root_ready, 1)
            Chain(dve, step).link(nc.vector.reciprocal(dis[:, :], root[:, 1, :]))

        @block.scalar
        def _(act):
            act.wait_ge(deg_ready, 1)
            nc.scalar.activation(root[:, 1, :], root[:, 0, :], ACT.Sqrt).then_inc(root_ready, 1)


def gcn_close(nc, k, state, dis, bias, x):
    with ExitStack() as ctx:
        m = Mem(nc, ctx)
        step = m.sem("step")
        block = ctx.enter_context(nc.Block())

        @block.vector
        def _(dve):
            ch = Chain(dve, step)
            S, full = state[:, :, :], [P, BLOCKS, D]
            ch.link(nc.vector.tensor_tensor(S, S, bc(dis[:, :].unsqueeze(2), full), ALU.mult))
            ch.link(nc.vector.tensor_tensor(S, S, bc(bias[:, :].unsqueeze(1), full), ALU.add))
            ch.link(nc.vector.scalar_tensor_tensor(out=x[:, :, :].rearrange("p b d -> p (b d)"),
                                                   in0=state[:, :, :].rearrange("p b d -> p (b d)"), scalar=0.0,
                                                   in1=x[:, :, :].rearrange("p b d -> p (b d)"),
                                                   op0=ALU.max, op1=ALU.add))


def rel_tables(nc, k, h):
    PAIRS = GROUP // 2
    with ExitStack() as ctx:
        m = Mem(nc, ctx)
        p_t = [m.ps(f"p_t{j}", [P, P]) for j in range(2)]
        p_s = [m.ps(f"p_s{j}", [P, OROW]) for j in range(2)]
        p_w = [m.ps(f"p_w{j}", [P, OROW]) for j in range(2)]
        staged = m.sb("staged", [P, 2, 2, D])
        stage_ready = m.sem("stage_ready")
        hT = m.sb("hT", [P, 2, P])
        rows = [m.sb(f"rows{j}", [P, TYPES, RROW]) for j in range(GROUP)]
        own = [m.sb(f"own{j}", [P, OROW]) for j in range(GROUP)]
        dummy = m.sb("dummy", [P, TYPES, RROW])
        tr, copied, made_s, made_w = m.sem("tr"), m.sem("copied"), m.sem("made_s"), m.sem("made_w")
        src_done, own_done = m.sem("src_done"), m.sem("own_done")
        half_done = m.sem("half_done")
        spread = [m.sem(f"spread{j}") for j in range(GROUP)]
        own_out = [m.sem(f"own_out{j}") for j in range(GROUP)]
        set_, dummy_out, tick = m.sem("set"), m.sem("dummy_out"), m.sem("tick")
        rows_free, own_free = m.sem("rows_free"), m.sem("own_free")
        block = ctx.enter_context(nc.Block())

        @block.tensor
        def _(pe):
            with pe.Fori(0, TURNS) as t:
                def turn_pair(pair):
                    pe.wait_ge(stage_ready, t * PAIRS + pair + 1)
                    nc.tensor.transpose(p_t[pair % 2][:, :], staged[:, pair % 2, :, :].rearrange("p b d -> p (b d)"),
                                        k.ident[:, :]).then_inc(tr, 1)

                turn_pair(0)
                for j in range(GROUP):
                    n, z, pair = t * GROUP + j, j % 2, j // 2
                    if z == 0:
                        pe.wait_ge(copied, t * PAIRS + pair + 1)
                    elif pair + 1 < PAIRS:
                        turn_pair(pair + 1)
                    lhsT = hT[z * D:(z + 1) * D, pair % 2, :]
                    pe.wait_ge(src_done, n + 1)
                    nc.tensor.matmul(p_s[z][:, :], lhsT, k.w_src[z * D:(z + 1) * D, :],
                                     start=True, stop=True).then_inc(made_s, 1)
                    pe.wait_ge(own_done, n + 1)
                    nc.tensor.matmul(p_w[z][:, :], lhsT, k.w_own[z * D:(z + 1) * D, :],
                                     start=True, stop=True).then_inc(made_w, 1)

        @block.scalar
        def _(act):
            act.sem_inc(src_done, 2)
            with act.Fori(0, TURNS) as t:
                def stage(pair):
                    nc.scalar.activation(staged[:, pair % 2, :, :], h[:, bass.ds(t * GROUP + 2 * pair, 2), :],
                                         ACT.Copy).then_inc(stage_ready, 1)

                def take_turned(pair):
                    act.wait_ge(tr, t * PAIRS + pair + 1)
                    nc.scalar.activation(hT[:, pair % 2, :], p_t[pair % 2][:, :], ACT.Copy).then_inc(copied, 1)

                stage(0)
                take_turned(0)
                for j in range(GROUP):
                    n, z, pair = t * GROUP + j, j % 2, j // 2
                    if pair + 1 < PAIRS:
                        if z == 0:
                            stage(pair + 1)
                        else:
                            take_turned(pair + 1)
                    act.wait_ge(made_s, n + 1)
                    act.wait_ge(rows_free, n + 1)
                    nc.scalar.activation(rows[j][:, :, 0:AW], bc(p_s[z][:, 0:AW].unsqueeze(1), [P, TYPES, AW]), ACT.Copy)
                    nc.scalar.activation(rows[j][:, :, AW:AW + D],
                                         p_s[z][:, AW:].rearrange("p (t d) -> p t d", t=TYPES), ACT.Copy)\
                        .then_inc(src_done, 1)

        @block.vector
        def _(dve):
            nc.vector.memset(dummy[:, :, :], 0.0).then_inc(set_, 1)
            dve.wait_ge(set_, 1)
            nc.vector.memset(dummy[:, :, D:AW], MINUS).then_inc(set_, 1)
            dve.sem_inc(own_done, 2)
            with dve.Fori(0, TURNS) as t:
                for j in range(GROUP):
                    n, z = t * GROUP + j, j % 2
                    dve.wait_ge(rows_free, n + 1)
                    nc.vector.tensor_scalar(rows[j][:, :, AW + D:RROW], bc(h[:, bass.ds(n, 1), :], [P, TYPES, D]), 0.5,
                                            None, ALU.mult).then_inc(half_done, 1)
                    dve.wait_ge(own_free, n + 1)
                    dve.wait_ge(made_w, n + 1)
                    nc.vector.tensor_tensor(own[j][:, :], p_w[z][:, :], k.own_bias[:, :], ALU.add)\
                        .then_inc(own_done, 1)

        @block.gpsimd
        def _(pool):
            pool.sem_inc(rows_free, GROUP)

            for b in range(BLOCKS):
                pool.wait_ge(src_done, b + 3)
                pool.wait_ge(half_done, b + 1)
                pool.indirect_dma_start(k.rel_tab[0:NPAD, :], at(k.node_r[:, b:b + 1]),
                                        rows[b % GROUP][:, :, :].rearrange("p t c -> p (t c)"), None)\
                    .then_inc(spread[b % GROUP], 16)
                if b >= 4:
                    c = b - 4
                    pool.wait_ge(spread[c % GROUP], 16 * (c // GROUP + 1))
                    pool.sem_inc(rows_free, 1)
            for j in range(GROUP):
                pool.wait_ge(spread[j], 16 * TURNS)

        @block.sync
        def _(sp):
            sp.wait_ge(set_, 2)
            sp.dma_start(k.rel_tab[NPAD:ROWS, :], dummy[:, :, :].rearrange("p t c -> p (t c)")).then_inc(dummy_out, 16)
            sp.sem_inc(own_free, GROUP)
            with sp.Fori(0, TURNS) as t:
                for j in range(GROUP):
                    sp.wait_ge(own_done, t * GROUP + j + 3)
                    sp.sem_inc(tick, 1)
                    sp.dma_start(k.own_tab[bass.ds(t * GROUP + j, 1)].rearrange("a p c -> p (a c)"), own[j][:, :])\
                        .then_inc(own_out[j], 16)
                    if j % 2:
                        for c in (j - 1, j):
                            sp.wait_ge(own_out[c], t * 16 + 16)
                            sp.sem_inc(own_free, 1)
            sp.wait_ge(dummy_out, 16)


def rel_edges(nc, k, part, state, top):
    AHEAD, LATE = 1, 2
    S = part.slots
    with ExitStack() as ctx:
        m = Mem(nc, ctx)
        r = ring_buffers(m, part, RROW, stages=RING)
        codes = m.sb("codes_of_turn", [P, RING, S], I32)
        own = m.sb("own", [P, RING, OROW])
        is_t = m.sb("is_t", [P, 3, RING, S], I32)
        feat, relu = m.sb("feat", [P, RING, S, D]), m.sb("relu", [P, RING, S, D])
        score = m.sb("score", [P, RING, S, AW])
        e = m.sb("e", [P, RING, S + 1])
        gate, th = m.sb("gate", [P, RING, S, D]), m.sb("th", [P, RING, S, D])
        value = m.sb("value", [P, RING, S, D])
        msg = m.sb("msg", [P, RING, S + 1, AW])
        p_gate = [m.ps(f"p_gate{z}", [P, S, D]) for z in range(2)]
        chunk_sum = m.sb("chunk_sum", [P, 2, AW])
        own_in = [m.sem(f"own_in{q}") for q in range(RING)]
        own_free = [m.sem(f"own_free{q}") for q in range(RING)]
        feat_ready, relu_ready, first_ready = m.sem("feat_ready"), m.sem("relu_ready"), m.sem("first_ready")
        e_ready, p_ready, value_ready = m.sem("e_ready"), m.sem("p_ready"), m.sem("value_ready")
        own_gate, gate_ready, th_ready = m.sem("own_gate"), m.sem("gate_ready"), m.sem("th_ready")
        codes_in, codes_used, start = m.sem("codes_in"), m.sem("codes_used"), m.sem("start")
        msg_ready, part_ready, added = m.sem("msg_ready"), m.sem("part_ready"), m.sem("added")
        block = ctx.enter_context(nc.Block())

        @block.sync
        def _(sp):
            n = turns(sp, k, part)
            with sp.Fori(0, n) as i:
                sp.wait_ge(r.meta_used, i * 2 + 2)
                sp.sem_inc(r.tick, 1)
                sp.dma_start(r.meta[:, :], k.chunk_tab[bass.ds(i * RING + part.base, RING), 0, CROW - 1:CROW]
                             .rearrange("a c -> c a"), allow_slow_non_contiguous=True).then_inc(r.meta_in, 16)
                b = turn_blocks(nc, sp, [mybir.EngineType.SP], r, i)
                sp.wait_ge(codes_used, i + 1)
                sp.sem_inc(r.tick, 1)
                sp.dma_start(codes[:, :, :], k.chunk_tab[bass.ds(i * RING + part.base, RING), :, SLOTS:SLOTS + S]
                             .rearrange("a p c -> p a c")).then_inc(codes_in, 16)

                def load_list(q):
                    sp.wait_ge(r.landed[q], i * (16 * S))
                    sp.sem_inc(r.tick, 1)
                    row = bass.ds(i * RING + (part.base + q), 1)
                    sp.dma_start(r.lists[q][:, :, :], k.chunk_tab[row, :, SLOTS:SLOTS + S]
                                 .rearrange("a p c -> p a c")).then_inc(r.list_in[q], 16)

                def load_own(q):
                    sp.wait_ge(own_free[q], i + 1)
                    sp.sem_inc(r.tick, 1)
                    sp.dma_start(own[:, q, :], k.own_tab[bass.ds(b[q], 1)].rearrange("a p c -> p (a c)"))\
                        .then_inc(own_in[q], 16)

                load_list(0)
                for q in range(1, RING):
                    load_list(q)
                    load_own(q - 1)
                load_own(RING - 1)

        @block.gpsimd
        def _(pool):
            gather_all(nc, pool, k, part, r, k.rel_tab.rearrange("n (t c) -> (n t) c", t=TYPES))

        @block.vector
        def _(dve):
            n = turns(dve, k, part)
            ring_credits(dve, r, readers=2, free=RING - 1)
            for q in range(RING - 1):
                dve.sem_inc(own_free[q], 1)
            dve.sem_inc(codes_used, 1)
            regs = [dve.alloc_register(m.name(f"block{q}")) for q in range(RING + 1)]
            for reg in regs:
                dve.reg_mov(reg, 0)
            b = [bass.RuntimeValue.of_register_unchecked(reg, min_val=0, max_val=BLOCKS - 1) for reg in regs]
            nc.vector.memset(th[:, RING - 1, :, :], 0.0).then_inc(start, 1)
            nc.vector.memset(value[:, RING - 1, :, :], 0.0).then_inc(start, 1)
            nc.vector.memset(msg[:, RING - 2:RING, :, :], 0.0).then_inc(start, 1)
            dve.wait_ge(start, 3)
            nc.vector.memset(msg[:, RING - 2:RING, S, D:AW], 1.0).then_inc(start, 1)
            dve.wait_ge(start, 4)
            dve.sem_inc(start, 1)
            dve.sem_inc(msg_ready, 1)
            nc.vector.memset(chunk_sum[:, RING % 2, :], 0.0).then_inc(part_ready, 1)
            def gated(q):
                nc.vector.scalar_tensor_tensor(out=msg[:, q, 0:S, 0:D], in0=th[:, q, :, :], scalar=1.0,
                                               in1=value[:, q, :, :], op0=ALU.add, op1=ALU.mult)\
                    .then_inc(msg_ready, 1)

            def add_up(q):
                nc.vector.tensor_reduce(chunk_sum[:, q % 2, :], msg[:, q, 0:S, :].rearrange("p s f -> p f s"), AX,
                                        ALU.add).then_inc(part_ready, 1)

            def add_part(q, blk):
                row = state[:, bass.ds(blk, 1), :].rearrange("p b f -> p (b f)")
                nc.vector.scalar_tensor_tensor(out=row, in0=row, scalar=msg[:, q, S, D:AW],
                                               in1=chunk_sum[:, q % 2, :], op0=ALU.mult, op1=ALU.add)\
                    .then_inc(added, 1)

            with dve.Fori(0, n) as i:
                dve.sem_clear(r.turn_step)
                ts = Chain(dve, r.turn_step)
                at_chunk = lambda q: i * RING + q + 1

                def types():
                    dve.wait_ge(codes_in, i * 16 + 16)
                    for t in range(2):
                        ts.add(nc.vector.tensor_single_scalar(is_t[:, t, :, :], codes[:, :, :], 1 + t,
                                                              ALU.bitwise_and))
                    ts.wait()
                    dve.sem_inc(codes_used, 1)
                    ts.link(nc.vector.tensor_tensor(is_t[:, 2, :, :], is_t[:, 0, :, :], is_t[:, 1, :, :], ALU.mult))

                def features(q):
                    z = q % 2
                    dve.wait_ge(r.landed[q], i * (16 * S) + 16 * S)
                    dve.wait_ge(own_in[q], i * 16 + 16)
                    nc.vector.tensor_tensor(feat[:, q, :, :], r.got[:, q, :, 0:D],
                                            bc(own[:, q, 0:D].unsqueeze(1), [P, S, D]), ALU.add)\
                        .then_inc(feat_ready, 1)

                def own_part(q, t):
                    ins = nc.vector.copy_predicated(gate[:, q, :, :],
                                                    bc(is_t[:, t, q, :].unsqueeze(2), [P, S, D]),
                                                    bc(own[:, q, AW + (t + 1) * D:AW + (t + 2) * D].unsqueeze(1),
                                                       [P, S, D]))
                    if t == TYPES - 2:
                        ins.then_inc(own_gate, 1)
                        return 0
                    return ts.add(ins)

                def scores(q):
                    blk = bass.ds(b[q], 1)
                    ts.add(nc.vector.tensor_copy(e[:, q, S:S + 1], top[:, blk]))
                    ts.add(nc.vector.tensor_tensor(score[:, q, :, D], r.got[:, q, :, D],
                                                   bc(own[:, q, D:AW], [P, S]), ALU.add))
                    dve.wait_ge(relu_ready, at_chunk(q))
                    return ts.add(nc.vector.tensor_tensor(score[:, q, :, 0:D], relu[:, q, :, :],
                                                          bc(k.att_a99[:, :].unsqueeze(1), [P, S, D]), ALU.mult))

                def score_sums(q, after):
                    ts.wait(after)
                    return ts.add(nc.vector.tensor_reduce(e[:, q, 0:S], score[:, q, :, :], AX, ALU.add))

                def maxima(q, after):
                    ts.wait(after)
                    return ts.add(nc.vector.tensor_reduce(top[:, bass.ds(b[q], 1)], e[:, q, :], AX, ALU.max))

                def below_top(q, after):
                    ts.wait(after)
                    nc.vector.tensor_tensor(e[:, q, :], e[:, q, :], bc(top[:, bass.ds(b[q], 1)], [P, S + 1]),
                                            ALU.subtract).then_inc(e_ready, 1)

                def messages(q, number):
                    dve.wait_ge(value_ready, i * RING + (number + 1 + AHEAD))
                    dve.wait_ge(th_ready, i * RING + (number + 1 + AHEAD))
                    dve.sem_inc(r.got_free[q], 1)
                    dve.sem_inc(own_free[q], 1)
                    gated(q)

                def parts(q, number):
                    dve.wait_ge(msg_ready, i * RING + (number + 1 + LATE))
                    dve.sem_inc(r.tick, 1)
                    add_up(q)

                def accumulate(q, number):
                    dve.wait_ge(part_ready, i * RING + (number + 1 + LATE))
                    if number > -2:
                        dve.wait_ge(added, i * RING + (number + LATE))
                    add_part(q, b[RING] if number == -1 else b[q])

                def own_start(q):
                    dve.wait_ge(first_ready, at_chunk(q))
                    dve.sem_inc(r.tick, 1)
                    return own_part(q, 0)

                types()
                features(0)
                accumulate(RING - 2, -2)
                dve.reg_mov(regs[RING], regs[RING - 1])
                dve.wait_ge(r.meta_in, i * 16 + 16)
                dve.sem_inc(r.tick, 1)
                dve.reg_load(regs[0:RING], r.meta[0:1, 0:RING])
                dve.sem_inc(r.meta_used, 1)
                n0 = own_start(0)
                messages(RING - 1, -1)
                ts.wait(n0)
                n1 = own_part(0, 1)
                ts.wait(n1)
                own_part(0, 2)
                parts(RING - 1, -1)
                for q in range(RING):
                    nxt = q + 1 < RING
                    if nxt:
                        features(q + 1)
                    n_s = scores(q)
                    if nxt:
                        n0 = own_start(q + 1)
                    n_e = score_sums(q, n_s)
                    if nxt:
                        ts.wait(n0)
                        n1 = own_part(q + 1, 1)
                    n_m = maxima(q, n_e)
                    if q:
                        accumulate((q - 2) % RING, q - 2)
                    below_top(q, n_m)
                    if q:
                        messages(q - 1, q - 1)
                    if nxt:
                        ts.wait(n1)
                        own_part(q + 1, 2)
                    if q:
                        parts(q - 1, q - 1)
                dve.sem_inc(r.tick, 1)
            dve.wait_ge(part_ready, n * RING + (LATE - 1))
            add_part(RING - 2, b[RING - 2])
            dve.wait_ge(value_ready, n * RING + AHEAD)
            dve.wait_ge(th_ready, n * RING + AHEAD)
            gated(RING - 1)
            dve.wait_ge(msg_ready, n * RING + LATE)
            add_up(RING - 1)
            dve.wait_ge(part_ready, n * RING + LATE)
            dve.wait_ge(added, n * RING + (LATE - 1))
            add_part(RING - 1, b[RING - 1])
            dve.wait_ge(added, n * RING + LATE)
            dve.sem_inc(r.tick, 1)

        @block.scalar
        def _(act):
            n = turns(act, k, part)
            act.wait_ge(start, 5)
            act.sem_inc(value_ready, AHEAD)
            act.sem_inc(th_ready, AHEAD)
            with act.Fori(0, n) as i:
                def first_types(q):
                    act.wait_ge(own_in[q], i * 16 + 16)
                    nc.scalar.activation(gate[:, q, :, :],
                                         bc(own[:, q, AW:AW + D].unsqueeze(1), [P, S, D]), ACT.Copy)\
                        .then_inc(first_ready, 1)

                def relus(q):
                    act.wait_ge(feat_ready, i * RING + q + 1)
                    nc.scalar.activation(relu[:, q, :, :], feat[:, q, :, :], ACT.Relu).then_inc(relu_ready, 1)

                def weights(q):
                    z = q % 2
                    act.wait_ge(e_ready, i * RING + q + 1)
                    nc.scalar.activation(msg[:, q, :, D], e[:, q, :], ACT.Exp).then_inc(p_ready, 1)
                    act.wait_ge(p_ready, i * RING + q + 1)
                    for j in range(S):
                        last = nc.scalar.activation(value[:, q, j, :], r.got[:, q, j, AW + D:RROW], ACT.Copy,
                                                    scale=msg[:, q, j, D:AW])
                    last.then_inc(value_ready, 1)

                def tanhs(q):
                    act.wait_ge(gate_ready, i * RING + q + 1)
                    nc.scalar.activation(th[:, q, :, :], p_gate[q % 2][:, :, :], ACT.Tanh, scale=0.5)\
                        .then_inc(th_ready, 1)

                first_types(0)
                relus(0)
                first_types(1)
                for q in range(RING):
                    if q + 1 < RING:
                        relus(q + 1)
                    if q + 2 < RING:
                        first_types(q + 2)
                    weights(q)
                    tanhs(q)

        @block.tensor
        def _(pe):
            n = turns(pe, k, part)

            with pe.Fori(0, n) as i:
                def gates(q):
                    z = q % 2
                    pe.wait_ge(own_gate, i * RING + q + 1)
                    pe.wait_ge(th_ready, i * RING + (q - 1 + AHEAD))
                    nc.tensor.matmul(p_gate[z][:, :, :], k.ident[:, :], r.got[:, q, :, AW:AW + D], start=True,
                                     stop=False)
                    nc.tensor.matmul(p_gate[z][:, :, :], k.ident[:, :], gate[:, q, :, :], start=False, stop=True)\
                        .then_inc(gate_ready, 1)

                for q in range(RING):
                    gates(q)


def rel_close(nc, k, h, state, x, out):
    with ExitStack() as ctx:
        m = Mem(nc, ctx)
        den, inv = m.sb("den", [P, BLOCKS]), m.sb("inv", [P, BLOCKS])
        hn = m.sb("hn", [P, BLOCKS, D])
        p_t = [m.ps(f"p_t{j}", [P, 2, P]) for j in range(2)]
        p_o = [m.ps(f"p_o{j}", [P, 2, 512]) for j in range(2)]
        staged = m.sb("staged", [P, 2, 2, 2, D])
        stage_ready, stage_free = m.sem("stage_ready"), m.sem("stage_free")
        hT = m.sb("hT", [P, 2, 2, P])
        lin = m.sb("lin", [P, 2, 2, D])
        step, hn_ready = m.sem("step"), m.sem("hn_ready")
        tr, copied, made, read, stored, spread = (m.sem("tr"), m.sem("copied"), m.sem("made"), m.sem("read"),
                                                  m.sem("stored"), m.sem("spread"))
        turn_step = m.sem("turn_step")
        block = ctx.enter_context(nc.Block())
        PAIRS, TP = BLOCKS // 2, 7

        @block.vector
        def _(dve):
            ch = Chain(dve, step)
            ch.link(nc.vector.tensor_scalar(den[:, :], state[:, :, D], 1e-30, None, ALU.max))
            ch.link(nc.vector.reciprocal(inv[:, :], den[:, :]))
            nc.vector.tensor_tensor(hn[:, :, :], state[:, :, 0:D], bc(inv[:, :].unsqueeze(2), [P, BLOCKS, D]),
                                    ALU.mult).then_inc(hn_ready, 1)
            dve.sem_inc(read, 2)
            with dve.Fori(0, PAIRS // TP) as t:
                dve.sem_clear(turn_step)
                ts = Chain(dve, turn_step)
                for j in range(TP):
                    n, z = t * TP + j, j % 2
                    L = lin[:, z, :, :].rearrange("p b d -> p (b d)")
                    xb = x[:, bass.ds(n * 2, 2), :].rearrange("p b d -> p (b d)")
                    dve.wait_ge(made, n + 1)
                    ts.link(nc.vector.tensor_tensor(lin[:, z, :, :], p_o[z][:, :, 0:D],
                                                    bc(k.vec["L3_gnn_lin_b"][:, :].unsqueeze(1), [P, 2, D]), ALU.add))
                    dve.sem_inc(read, 1)
                    ts.link(nc.vector.scalar_tensor_tensor(out=L, in0=L, scalar=0.01, in1=L, op0=ALU.mult,
                                                           op1=ALU.max))
                    nc.vector.tensor_tensor(xb, xb, L, ALU.add).then_inc(stored, 1)
                    dve.wait_ge(stored, n + 1)

        @block.tensor
        def _(pe):
            pe.wait_ge(hn_ready, 1)
            pe.sem_inc(stage_free, 2)
            with pe.Fori(0, PAIRS // TP) as t:
                for j in range(TP):
                    n, z = t * TP + j, j % 2
                    pe.wait_ge(read, n + (1 if j else 2))
                    pe.wait_ge(stage_ready, n * 2 + 2)
                    for w in range(2):
                        last = nc.tensor.transpose(p_t[z][:, w, :], staged[:, z, w, :, :]
                                                   .rearrange("p b d -> p (b d)"), k.ident[:, :])
                    last.then_inc(tr, 1)
                    pe.wait_ge(copied, n + 1)
                    pe.sem_inc(stage_free, 1)
                    for y in range(2):
                        for w in range(2):
                            last = nc.tensor.matmul(p_o[z][:, y, 0:D], hT[y * D:(y + 1) * D, z, w, :],
                                                    k.w_lin[y * D:(y + 1) * D, w, :], start=(w == 0), stop=(w == 1))
                    last.then_inc(made, 1)

        @block.scalar
        def _(act):
            act.wait_ge(hn_ready, 1)
            with act.Fori(0, PAIRS // TP) as t:
                def stage(j):
                    n = t * TP + j
                    act.wait_ge(stage_free, n + (1 if j else 2))
                    for w, buf in enumerate((h, hn)):
                        nc.scalar.activation(staged[:, j % 2, w, :, :], buf[:, bass.ds(n * 2, 2), :], ACT.Copy)\
                            .then_inc(stage_ready, 1)

                stage(0)
                for j in range(TP):
                    if j + 1 < TP:
                        stage(j + 1)
                    act.wait_ge(tr, t * TP + j + 1)
                    nc.scalar.activation(hT[:, j % 2, :, :], p_t[j % 2][:, :, :], ACT.Copy).then_inc(copied, 1)

        @block.gpsimd
        def _(pool):
            for b in range(BLOCKS):
                pool.wait_ge(stored, b // 2 + 1)
                pool.indirect_dma_start(out, at(k.node_r[:, b:b + 1]), x[:, b, :], None, bounds_check=N - 1,
                                        oob_is_err=False).then_inc(spread, 16)
            pool.wait_ge(spread, 16 * BLOCKS)


def gnn_program(nc, a, out):
    ctx = ExitStack()
    with ctx:
        k = type("Kept", (), {})()
        m = Mem(nc, ctx)
        k.ident, k.ones, k.before = m.sb("ident", [P, P]), m.sb("ones", [P, P]), m.sb("before", [P, P])
        k.zeros = m.sb("zeros", [P, 2 * D])
        k.iota_i, k.iota = m.sb("iota_i", [P, P], I32), m.sb("iota", [P, P])
        k.node_i = m.sb("node_i", [P, BLOCKS], I32)
        k.dummy_i, k.dummy, k.dummy4 = m.sb("dummy_i", [P, 1], I32), m.sb("dummy_row", [P, 1]), m.sb("dummy4", [P, 1])
        k.deg, k.deg_r = m.sb("deg", [P, BLOCKS]), m.sb("deg_r", [P, BLOCKS])
        k.node_r = m.sb("node_r", [P, BLOCKS], I32)
        k.ctl_i, k.row_i = m.sb("ctl_i", [1, 8], I32), m.sb("row_i", [1, 8, BLOCKS], I32)
        k.const_ready = m.sem("const_ready")

        def dram(name, shape, dt=F32):
            return nc.dram_tensor(name, shape, dt, kind="Internal").ap()

        k.codes = dram("codes", [E + WIDE], I32)
        k.runs = dram("runs", [E, WIDE], I32)
        k.info_tab = dram("info_tab", [NPAD, 4], I32)
        k.chunk_tab = dram("chunk_tab", [TABLE, P, CROW], I32)
        k.hn_tab, k.hh_tab = dram("hn_tab", [ROWS, D]), dram("hh_tab", [NPAD, 2 * D])
        k.sums = [dram(f"sums{j}", [ROWS, D + 1]) for j in range(SLOTS)]
        k.x1_tab = dram("x1_tab", [NPAD, D])
        k.gat1_tab = dram("gat1_tab", [ROWS, H1 * (C1 + 2)])
        k.gat2_tab = dram("gat2_tab", [ROWS, D + 2])
        k.gcn_tab = dram("gcn_tab", [ROWS, D])
        k.rel_tab = dram("rel_tab", [ROWS, TYPES * RROW])
        k.own_tab = dram("own_tab", [BLOCKS, P, OROW])
        k.w_gat1, k.w_gat2 = m.sb("w_gat1", [P, H1 * (C1 + 3)]), m.sb("w_gat2", [P, D + 3])
        k.w_gcn = m.sb("w_gcn", [P, D])
        k.ones_row = {1: m.sb("ones_row1", [P, H1 * (C1 + 3)]), 2: m.sb("ones_row2", [P, D + 3])}
        k.w_src, k.w_own = m.sb("w_src", [P, OROW]), m.sb("w_own", [P, OROW])
        k.w_lin = m.sb("w_lin", [P, 2, D])
        k.att_a, k.att_a99 = m.sb("att_a", [P, D]), m.sb("att_a99", [P, D])
        k.own_bias = m.sb("own_bias", [P, OROW])
        k.vec = {n: m.sb("v_" + n, [P, D]) for n in _VECS}
        constants(nc, k)
        count_edges(nc, k, a)
        rank_nodes(nc, k, a)
        with ExitStack() as ctx2:
            k.rows = Mem(nc, ctx2).sb("rows", [P, BLOCKS, WCH, CROW], I32)
            build_chunks(nc, k)
            load_weights(nc, k, a)
            first_layer(nc, k)
        cosine_close(nc, k, a)
        other_layers(nc, k, out)


def clear(nc, pairs):
    with ExitStack() as ctx:
        cleared = Mem(nc, ctx).sem("cleared")
        block = ctx.enter_context(nc.Block())

        @block.vector
        def _(dve):
            for buf, value in pairs:
                nc.vector.memset(buf, value).then_inc(cleared, 1)
            dve.wait_ge(cleared, len(pairs))


def first_layer(nc, k):
    with ExitStack() as ctx:
        m = Mem(nc, ctx)
        own_hn, own_v = m.sb("own_hn", [P, BLOCKS, D]), m.sb("own_v", [P, BLOCKS, D + 1])
        fetch_rows(nc, k, k.hh_tab, 2 * D, [(own_v, 0, D), (own_hn, D, D)], FIRST)
        clear(nc, [(own_v[:, :, D:D + 1], 1.0)])
        for part in PARTS:
            cosine_edges(nc, k, part, own_hn, own_v)


def other_layers(nc, k, out):
    with ExitStack() as ctx:
        m = Mem(nc, ctx)
        x, h = m.sb("x", [P, BLOCKS, D]), m.sb("h", [P, BLOCKS, D])
        fetch_and_open(nc, k, x, h)
        for step, heads, c, w, tab, res in ((1, H1, C1, k.w_gat1, k.gat1_tab, None), (2, 1, D, k.w_gat2, k.gat2_tab, x)):
            HW = heads * (c + 1)
            with ExitStack() as ctx2:
                m2 = Mem(nc, ctx2)
                state = m2.sb(f"state{step}", [P, BLOCKS, HW + 2 * heads])
                own_dst, top = m2.sb(f"own_dst{step}", [P, BLOCKS, heads]), m2.sb(f"top{step}", [P, BLOCKS, heads])
                ones, wide = k.ones_row[step], HW + 2 * heads
                project_and_spread(nc, k, h, w, wide, state,
                                   lambda o, x, b: nc.vector.tensor_tensor(o, x, bc(ones[:, :].unsqueeze(1),
                                                                                    [P, 2, wide]), ALU.add),
                                   tab, HW + heads, HW)
                gat_open(nc, k, heads, c, state, own_dst, top)
                for part in PARTS:
                    gat_edges(nc, k, part, heads, c, state, top, own_dst, tab)
                v = lambda n: k.vec["L1_gnn_" + n]
                gat_close(nc, k, heads, c, state, v(f"b{step}"), v(f"ln{step}_g"), v(f"ln{step}_b"), h, res)
        open_layer(nc, k, x, h)
        with ExitStack() as ctx2:
            m2 = Mem(nc, ctx2)
            state, dis = m2.sb("gcn_state", [P, BLOCKS, D]), m2.sb("dis", [P, BLOCKS])
            gcn_norm(nc, k, dis)
            project_and_spread(nc, k, h, k.w_gcn, D, state,
                               lambda o, x, b: nc.vector.tensor_tensor(o, x, bc(dis[:, b].unsqueeze(2), [P, 2, D]),
                                                                       ALU.mult),
                               k.gcn_tab, D, None)
            for part in PARTS:
                gcn_edges(nc, k, part, state, k.gcn_tab)
            gcn_close(nc, k, state, dis, k.vec["L2_gnn_b"], x)
        open_layer(nc, k, x, h)
        rel_tables(nc, k, h)
        with ExitStack() as ctx2:
            m2 = Mem(nc, ctx2)
            state, top = m2.sb("rel_state", [P, BLOCKS, AW]), m2.sb("rel_top", [P, BLOCKS])
            clear(nc, [(state[:, :, :], 0.0), (top[:, :], MINUS)])
            for part in PARTS:
                rel_edges(nc, k, part, state, top)
            rel_close(nc, k, h, state, x, out)


_VECS = ["L1_gnn_b1", "L1_gnn_b2", "L1_gnn_ln1_g", "L1_gnn_ln1_b", "L1_gnn_ln2_g", "L1_gnn_ln2_b", "L2_gnn_b",
         "L3_gnn_Wa_b", "L3_gnn_lin_b"]
_INS = ["x", "src", "dst", "edge_type_4", "L1_gnn_W1", "L1_gnn_a1_src", "L1_gnn_a1_dst", "L1_gnn_W2",
        "L1_gnn_a2_src", "L1_gnn_a2_dst", "L2_gnn_W", "L3_gnn_r", "L3_gnn_a", "L3_gnn_Wa_w", "L3_gnn_lin_w"] + _VECS


def kernel(**inputs):
    import numpy as _np
    import concourse.bacc as _bacc
    from concourse import mybir as _mybir
    from concourse.bass_utils import run_bass_kernel_spmd as _run

    nc = _bacc.Bacc("TRN2", target_bir_lowering=False, num_devices=1)
    arrays, args = {}, {}
    for name in _INS:
        arr = _np.ascontiguousarray(inputs[name])
        arrays[f"in_{name}_dram"] = arr
        args[name] = nc.dram_tensor(f"in_{name}_dram", arr.shape, _mybir.dt.from_np(arr.dtype),
                                    kind="ExternalInput").ap()
    out = nc.dram_tensor("out_dram", (N, D), F32, kind="ExternalOutput").ap()
    gnn_program(nc, args, out)
    r = _run(nc, [arrays], core_ids=[0])
    return r.results[0]["out_dram"]
```
